# Optimizing a Trainium2 kernel written in Bass

```python
import numpy as np
import jax
import jax.numpy as jnp

def _softmax(x, axis=-1):
    return jax.nn.softmax(x, axis=axis)

def _gelu(x):
    return jax.nn.gelu(x, approximate=True)

def _silu(x):
    return jax.nn.silu(x)

def _sigmoid(x):
    return jax.nn.sigmoid(x)

def _layernorm(x, axis=-1, eps=1e-05):
    m = jnp.mean(x, axis=axis, keepdims=True)
    v = jnp.var(x, axis=axis, keepdims=True)
    return (x - m) / jnp.sqrt(v + eps)

def _scatter_add(tgt, idx, src, axis=0):
    return tgt.at[idx].add(src)

def _segment_sum(src, seg, n):
    return jax.ops.segment_sum(src, seg, n)
kernel_name = 'mk_decoder_postln_d2_seqx_r8_e00ce7'

def setup_inputs(seed: int=0):
    np.random.seed(seed)
    _w = jnp.asarray

    def _rec_inputs():
        import jax
        import jax.numpy as jnp
        _rk = jax.random.key(seed)
        x = 7.22e-05 + 1 * jax.random.normal(jax.random.fold_in(_rk, 1), (1, 1024, 128), jnp.float32)
        _lenS = 1024 - jax.random.randint(jax.random.fold_in(_rk, 7), (1,), 0, max(1, 1024 // 4) + 1, jnp.int32)
        _lenS2 = 6404 - jax.random.randint(jax.random.fold_in(_rk, 8), (1,), 0, max(1, 6404 // 4) + 1, jnp.int32)
        _ctx_768P = jax.random.normal(jax.random.fold_in(_rk, 11), (1, 16, 96), jnp.float32)
        _ctx_768c = jax.random.dirichlet(jax.random.fold_in(_rk, 511), 0.3 * jnp.ones((16,), jnp.float32), (1, 6404))
        _ctx_768t = jnp.einsum('bsk,bkd->bsd', _ctx_768c, _ctx_768P)
        _ctx_768t = _ctx_768t * jax.lax.rsqrt(jnp.mean(jnp.square(_ctx_768t)) + 1e-12) * 0.953939
        ctx_768 = -0.000191848 + 0.999787 * (_ctx_768t + 0.3 * jax.random.normal(jax.random.fold_in(_rk, 611), (1, 6404, 96), jnp.float32))
        return (x, ctx_768)
    x, ctx_768 = _rec_inputs()

    def _L0_attn_setup():
        import jax, jax.numpy as jnp
        import numpy as np
        DIM = 128
        HEADS = 16
        DHEAD = DIM // HEADS
        EPS_NORM = 1e-06
        EPS_DEN = 1e-06

        def rmsnorm(x, w):
            xf = x.astype(jnp.float32)
            return (w * xf * jax.lax.rsqrt(jnp.mean(xf * xf, axis=-1, keepdims=True) + EPS_NORM)).astype(x.dtype)
        key = jax.random.key(seed)
        ks = jax.random.split(key, 6)
        b, n = (4, 512)
        x = jax.random.normal(ks[0], (b, n, DIM), dtype=jnp.float32)
        W_qkv = jax.random.normal(ks[1], (DIM, 3 * DIM), dtype=jnp.float32) * DIM ** (-0.5)
        qn_w = jnp.ones((DIM,), dtype=jnp.float32)
        kn_w = jnp.ones((DIM,), dtype=jnp.float32)
        W_out = jax.random.normal(ks[2], (DIM, DIM), dtype=jnp.float32) * DIM ** (-0.5)
        b_out = jnp.zeros((DIM,), dtype=jnp.float32)
        return {'x': x, 'W_qkv': W_qkv, 'qn_w': qn_w, 'kn_w': kn_w, 'W_out': W_out, 'b_out': b_out}
    _L0_attn_all = _L0_attn_setup()
    _L0_attn_in = {k: v for k, v in _L0_attn_all.items() if k in ('W_qkv', 'qn_w', 'kn_w', 'W_out', 'b_out')}
    del _L0_attn_all

    def _L0_xattn_setup():
        import jax, jax.numpy as jnp
        import numpy as np
        HEADS = 8
        DIM_HEAD = 64
        SCALE = DIM_HEAD ** (-0.5)
        key = jax.random.key(seed)
        ks = jax.random.split(key, 7)
        B, Nq, Nc = (4, 256, 256)
        Dq, Dc = (128, 96)
        inner = HEADS * DIM_HEAD
        x = jax.random.normal(ks[0], (B, Nq, Dq), dtype=jnp.float32)
        context = jax.random.normal(ks[1], (B, Nc, Dc), dtype=jnp.float32)
        Wq = jax.random.normal(ks[2], (Dq, inner), dtype=jnp.float32) * Dq ** (-0.5)
        Wk = jax.random.normal(ks[3], (Dc, inner), dtype=jnp.float32) * Dc ** (-0.5)
        Wv = jax.random.normal(ks[4], (Dc, inner), dtype=jnp.float32) * Dc ** (-0.5)
        Wo = jax.random.normal(ks[5], (inner, Dq), dtype=jnp.float32) * inner ** (-0.5)
        bo = jax.random.normal(ks[6], (Dq,), dtype=jnp.float32) * 0.01
        return {'x': x, 'context': context, 'Wq': Wq, 'Wk': Wk, 'Wv': Wv, 'Wo': Wo, 'bo': bo}
    _L0_xattn_all = _L0_xattn_setup()
    _L0_xattn_in = {k: v for k, v in _L0_xattn_all.items() if k in ('Wq', 'Wk', 'Wv', 'Wo', 'bo')}
    del _L0_xattn_all

    def _L0_ffn_setup():
        import jax, jax.numpy as jnp
        import numpy as np
        H = 128
        I = 88
        E = 64
        TOP_K = 8
        NG = 8
        TOPK_GROUP = 4
        N_SHARED = 2
        ROUTED_SCALE = 2.5
        S_I = I * N_SHARED

        def _route(x, gate_w, gate_bias):
            T = x.shape[0]
            logits = x @ gate_w.T
            scores = jax.nn.sigmoid(logits)
            scores_for_choice = scores + gate_bias[None, :]
            grp = scores_for_choice.reshape(T, NG, E // NG)
            group_scores = jnp.sum(jax.lax.top_k(grp, 2)[0], axis=-1)
            _, gidx = jax.lax.top_k(group_scores, TOPK_GROUP)
            gmask = jnp.zeros((T, NG), dtype=scores.dtype).at[jnp.arange(T)[:, None], gidx].set(1.0)
            emask = jnp.repeat(gmask, E // NG, axis=1)
            masked = jnp.where(emask > 0, scores_for_choice, 0.0)
            _, topk_idx = jax.lax.top_k(masked, TOP_K)
            topk_w = jnp.take_along_axis(scores, topk_idx, axis=1)
            topk_w = topk_w / (jnp.sum(topk_w, axis=-1, keepdims=True) + 1e-20)
            topk_w = topk_w * ROUTED_SCALE
            rw = jnp.zeros((T, E), dtype=scores.dtype).at[jnp.arange(T)[:, None], topk_idx].add(topk_w)
            return rw

        def _mlp(x, gw, uw, dw):
            return jax.nn.silu(x @ gw.T) * (x @ uw.T) @ dw.T
        key = jax.random.key(seed)
        ks = jax.random.split(key, 10)
        sc = 0.02
        return {'hidden_states': jax.random.normal(ks[0], (1, 128, H), dtype=jnp.float32), 'gate_w': sc * jax.random.normal(ks[1], (E, H), dtype=jnp.float32), 'gate_bias': sc * jax.random.normal(ks[2], (E,), dtype=jnp.float32), 'Wg': sc * jax.random.normal(ks[3], (E, I, H), dtype=jnp.float32), 'Wu': sc * jax.random.normal(ks[4], (E, I, H), dtype=jnp.float32), 'Wd': sc * jax.random.normal(ks[5], (E, H, I), dtype=jnp.float32), 'Sg': sc * jax.random.normal(ks[6], (S_I, H), dtype=jnp.float32), 'Su': sc * jax.random.normal(ks[7], (S_I, H), dtype=jnp.float32), 'Sd': sc * jax.random.normal(ks[8], (H, S_I), dtype=jnp.float32)}
    _L0_ffn_all = _L0_ffn_setup()
    _L0_ffn_in = {k: v for k, v in _L0_ffn_all.items() if k in ('gate_w', 'gate_bias', 'Wg', 'Wu', 'Wd', 'Sg', 'Su', 'Sd')}
    del _L0_ffn_all

    def _L1_attn_setup():
        import jax, jax.numpy as jnp
        import numpy as np
        B, S, D = (4, 256, 128)

        def givens_rotate(r, x):
            g = r.reshape(-1, 2)
            g = g / jnp.linalg.norm(g, axis=-1, keepdims=True)
            xp = x.reshape(x.shape[:-1] + (x.shape[-1] // 2, 2))
            c, s = (g[:, 0], g[:, 1])
            y0 = c * xp[..., 0] - s * xp[..., 1]
            y1 = c * xp[..., 1] + s * xp[..., 0]
            return jnp.stack([y0, y1], axis=-1).reshape(x.shape)
        key = jax.random.key(seed)
        k1, k2 = jax.random.split(key, 2)
        Q = jax.random.normal(k1, (B, S, D), dtype=jnp.float32)
        rot_w = jax.random.uniform(k2, (3, D), dtype=jnp.float32, minval=-1.0, maxval=1.0)
        scale = jnp.array([np.sqrt(D)], dtype=jnp.float32)
        bias = jnp.zeros((), dtype=jnp.float32)
        return {'Q': Q, 'rot_w': rot_w, 'scale': scale, 'bias': bias}
    _L1_attn_all = _L1_attn_setup()
    _L1_attn_in = {k: v for k, v in _L1_attn_all.items() if k in ('rot_w', 'scale', 'bias')}
    del _L1_attn_all

    def _L1_xattn_setup():
        import jax, jax.numpy as jnp
        import numpy as np
        import math
        E = 128
        EV = 128
        FFN = 512
        DINO = 96
        B, S, P = (64, 64, 32)

        def bitnet_linear(x, W, b):
            w_scale = jnp.maximum(jnp.mean(jnp.abs(W)), 1e-05)
            qW = jnp.sign(W) * (jnp.abs(W) > 0.5 * w_scale).astype(W.dtype)
            i_scale = jnp.maximum(jnp.max(jnp.abs(x)), 1e-08) / 127.0
            qx = jnp.clip(jnp.round(x / i_scale), -128.0, 127.0)
            out = jnp.einsum('...i,oi->...o', qx, qW) * (w_scale * i_scale)
            return out + b
        key = jax.random.key(seed)
        ks = iter(jax.random.split(key, 32))

        def lin_w(fin, fout):
            return jax.random.normal(next(ks), (fout, fin), jnp.float32) * math.sqrt(2.0 / fin)
        return {'text_embeddings': jax.random.normal(next(ks), (B, S, E), jnp.float32), 'dinov2_features': jax.random.normal(next(ks), (B, P, DINO), jnp.float32), 'W_d2v': lin_w(DINO, EV), 'b_d2v': jnp.zeros((EV,), jnp.float32), 'W_img': lin_w(EV, E), 'b_img': jnp.zeros((E,), jnp.float32), 'W_txt': lin_w(E, E), 'b_txt': jnp.zeros((E,), jnp.float32), 'W_att0': lin_w(E, E // 2), 'b_att0': jnp.zeros((E // 2,), jnp.float32), 'W_att1': lin_w(E, E // 2), 'b_att1': jnp.zeros((E // 2,), jnp.float32), 'W_f1': lin_w(2 * E, FFN), 'b_f1': jnp.zeros((FFN,), jnp.float32), 'W_f2': lin_w(FFN, E), 'b_f2': jnp.zeros((E,), jnp.float32)}
    _L1_xattn_all = _L1_xattn_setup()
    _L1_xattn_in = {k: v for k, v in _L1_xattn_all.items() if k in ('W_d2v', 'b_d2v', 'W_img', 'b_img', 'W_txt', 'b_txt', 'W_att0', 'b_att0', 'W_att1', 'b_att1', 'W_f1', 'b_f1', 'W_f2', 'b_f2')}
    del _L1_xattn_all

    def _L1_ffn_setup():
        import jax, jax.numpy as jnp
        import numpy as np
        B, L, H = (8, 256, 128)
        E, K, R = (8, 2, 64)

        def _gates(cls_tok, Wr):
            logits = cls_tok @ Wr.T
            top_vals, top_idx = jax.lax.top_k(logits, K)
            neg_inf = jnp.full_like(logits, -jnp.inf)
            rows = jnp.arange(logits.shape[0])[:, None]
            masked = neg_inf.at[rows, top_idx].set(top_vals)
            return jax.nn.softmax(masked, axis=-1)
        key = jax.random.key(seed)
        k1, k2, k3, k4 = jax.random.split(key, 4)
        x = jax.random.normal(k1, (B, L, H), dtype=jnp.float32)
        Wr = jax.random.normal(k2, (E, H), dtype=jnp.float32) * (1.0 / np.sqrt(H))
        A = jax.random.normal(k3, (E, R, H), dtype=jnp.float32) * (1.0 / np.sqrt(H))
        Bw = jax.random.normal(k4, (E, H, R), dtype=jnp.float32) * (1.0 / np.sqrt(R))
        return {'x': x, 'Wr': Wr, 'A': A, 'Bw': Bw}
    _L1_ffn_all = _L1_ffn_setup()
    _L1_ffn_in = {k: v for k, v in _L1_ffn_all.items() if k in ('Wr', 'A', 'Bw')}
    del _L1_ffn_all
    return {'x': x, 'ctx_768': ctx_768, 'L0_attn_W_qkv': _L0_attn_in['W_qkv'], 'L0_attn_qn_w': _L0_attn_in['qn_w'], 'L0_attn_kn_w': _L0_attn_in['kn_w'], 'L0_attn_W_out': _L0_attn_in['W_out'], 'L0_attn_b_out': _L0_attn_in['b_out'], 'L0_xattn_Wq': _L0_xattn_in['Wq'], 'L0_xattn_Wk': _L0_xattn_in['Wk'], 'L0_xattn_Wv': _L0_xattn_in['Wv'], 'L0_xattn_Wo': _L0_xattn_in['Wo'], 'L0_xattn_bo': _L0_xattn_in['bo'], 'L0_ffn_gate_w': _L0_ffn_in['gate_w'], 'L0_ffn_gate_bias': _L0_ffn_in['gate_bias'], 'L0_ffn_Wg': _L0_ffn_in['Wg'], 'L0_ffn_Wu': _L0_ffn_in['Wu'], 'L0_ffn_Wd': _L0_ffn_in['Wd'], 'L0_ffn_Sg': _L0_ffn_in['Sg'], 'L0_ffn_Su': _L0_ffn_in['Su'], 'L0_ffn_Sd': _L0_ffn_in['Sd'], 'L1_attn_rot_w': _L1_attn_in['rot_w'], 'L1_attn_scale': _L1_attn_in['scale'], 'L1_attn_bias': _L1_attn_in['bias'], 'L1_xattn_W_d2v': _L1_xattn_in['W_d2v'], 'L1_xattn_b_d2v': _L1_xattn_in['b_d2v'], 'L1_xattn_W_img': _L1_xattn_in['W_img'], 'L1_xattn_b_img': _L1_xattn_in['b_img'], 'L1_xattn_W_txt': _L1_xattn_in['W_txt'], 'L1_xattn_b_txt': _L1_xattn_in['b_txt'], 'L1_xattn_W_att0': _L1_xattn_in['W_att0'], 'L1_xattn_b_att0': _L1_xattn_in['b_att0'], 'L1_xattn_W_att1': _L1_xattn_in['W_att1'], 'L1_xattn_b_att1': _L1_xattn_in['b_att1'], 'L1_xattn_W_f1': _L1_xattn_in['W_f1'], 'L1_xattn_b_f1': _L1_xattn_in['b_f1'], 'L1_xattn_W_f2': _L1_xattn_in['W_f2'], 'L1_xattn_b_f2': _L1_xattn_in['b_f2'], 'L1_ffn_Wr': _L1_ffn_in['Wr'], 'L1_ffn_A': _L1_ffn_in['A'], 'L1_ffn_Bw': _L1_ffn_in['Bw']}

def reference(x, ctx_768, L0_attn_W_qkv, L0_attn_qn_w, L0_attn_kn_w, L0_attn_W_out, L0_attn_b_out, L0_xattn_Wq, L0_xattn_Wk, L0_xattn_Wv, L0_xattn_Wo, L0_xattn_bo, L0_ffn_gate_w, L0_ffn_gate_bias, L0_ffn_Wg, L0_ffn_Wu, L0_ffn_Wd, L0_ffn_Sg, L0_ffn_Su, L0_ffn_Sd, L1_attn_rot_w, L1_attn_scale, L1_attn_bias, L1_xattn_W_d2v, L1_xattn_b_d2v, L1_xattn_W_img, L1_xattn_b_img, L1_xattn_W_txt, L1_xattn_b_txt, L1_xattn_W_att0, L1_xattn_b_att0, L1_xattn_W_att1, L1_xattn_b_att1, L1_xattn_W_f1, L1_xattn_b_f1, L1_xattn_W_f2, L1_xattn_b_f2, L1_ffn_Wr, L1_ffn_A, L1_ffn_Bw):
    import jax
    import jax.numpy as jnp

    def _L0_attn_ref(x, W_qkv, qn_w, kn_w, W_out, b_out):
        import jax, jax.numpy as jnp
        import numpy as np
        DIM = 128
        HEADS = 16
        DHEAD = DIM // HEADS
        EPS_NORM = 1e-06
        EPS_DEN = 1e-06

        def rmsnorm(x, w):
            xf = x.astype(jnp.float32)
            return (w * xf * jax.lax.rsqrt(jnp.mean(xf * xf, axis=-1, keepdims=True) + EPS_NORM)).astype(x.dtype)
        b, n, _ = x.shape
        qkv = x @ W_qkv
        q, k, v = jnp.split(qkv, 3, axis=-1)
        q = rmsnorm(q, qn_w)
        k = rmsnorm(k, kn_w)

        def split_heads(t):
            return t.reshape(b, n, HEADS, DHEAD).transpose(0, 2, 1, 3)
        q, k, v = map(split_heads, (q, k, v))
        q = jax.nn.relu(q).astype(jnp.float32)
        k = jax.nn.relu(k).astype(jnp.float32)
        v = v.astype(jnp.float32)
        kv = jnp.einsum('bhnd,bhne->bhde', k, v)
        out = jnp.einsum('bhnd,bhde->bhne', q, kv)
        k_sum = k.sum(axis=2)
        normalizer = jnp.einsum('bhnd,bhd->bhn', q, k_sum) + EPS_DEN
        out = out / normalizer[..., None]
        out = out.transpose(0, 2, 1, 3).reshape(b, n, DIM)
        return out @ W_out + b_out

    def _L0_xattn_ref(x, context, Wq, Wk, Wv, Wo, bo):
        import jax, jax.numpy as jnp
        import numpy as np
        HEADS = 8
        DIM_HEAD = 64
        SCALE = DIM_HEAD ** (-0.5)
        B, Nq, _ = x.shape
        q = (x @ Wq).reshape(B, Nq, HEADS, DIM_HEAD)
        k = (context @ Wk).reshape(B, context.shape[1], HEADS, DIM_HEAD)
        v = (context @ Wv).reshape(B, context.shape[1], HEADS, DIM_HEAD)
        sim = jnp.einsum('bihd,bjhd->bhij', q, k) * SCALE
        attn = jax.nn.softmax(sim, axis=-1)
        out = jnp.einsum('bhij,bjhd->bihd', attn, v)
        out = out.reshape(B, Nq, HEADS * DIM_HEAD)
        return out @ Wo + bo

    def _L0_ffn_ref(hidden_states, gate_w, gate_bias, Wg, Wu, Wd, Sg, Su, Sd):
        import jax, jax.numpy as jnp
        import numpy as np
        H = 128
        I = 88
        E = 64
        TOP_K = 8
        NG = 8
        TOPK_GROUP = 4
        N_SHARED = 2
        ROUTED_SCALE = 2.5
        S_I = I * N_SHARED

        def _route(x, gate_w, gate_bias):
            T = x.shape[0]
            logits = x @ gate_w.T
            scores = jax.nn.sigmoid(logits)
            scores_for_choice = scores + gate_bias[None, :]
            grp = scores_for_choice.reshape(T, NG, E // NG)
            group_scores = jnp.sum(jax.lax.top_k(grp, 2)[0], axis=-1)
            _, gidx = jax.lax.top_k(group_scores, TOPK_GROUP)
            gmask = jnp.zeros((T, NG), dtype=scores.dtype).at[jnp.arange(T)[:, None], gidx].set(1.0)
            emask = jnp.repeat(gmask, E // NG, axis=1)
            masked = jnp.where(emask > 0, scores_for_choice, 0.0)
            _, topk_idx = jax.lax.top_k(masked, TOP_K)
            topk_w = jnp.take_along_axis(scores, topk_idx, axis=1)
            topk_w = topk_w / (jnp.sum(topk_w, axis=-1, keepdims=True) + 1e-20)
            topk_w = topk_w * ROUTED_SCALE
            rw = jnp.zeros((T, E), dtype=scores.dtype).at[jnp.arange(T)[:, None], topk_idx].add(topk_w)
            return rw

        def _mlp(x, gw, uw, dw):
            return jax.nn.silu(x @ gw.T) * (x @ uw.T) @ dw.T
        B, S, _ = hidden_states.shape
        x = hidden_states.reshape(B * S, H)
        rw = _route(x, gate_w, gate_bias)
        expert_out = jax.vmap(lambda gw_, uw_, dw_: _mlp(x, gw_, uw_, dw_))(Wg, Wu, Wd)
        routed = jnp.einsum('eth,te->th', expert_out, rw)
        shared = _mlp(x, Sg, Su, Sd)
        out = (routed + shared).reshape(B, S, H)
        return out

    def _L1_attn_ref(Q, rot_w, scale, bias):
        import jax, jax.numpy as jnp
        import numpy as np
        B, S, D = (4, 256, 128)

        def givens_rotate(r, x):
            g = r.reshape(-1, 2)
            g = g / jnp.linalg.norm(g, axis=-1, keepdims=True)
            xp = x.reshape(x.shape[:-1] + (x.shape[-1] // 2, 2))
            c, s = (g[:, 0], g[:, 1])
            y0 = c * xp[..., 0] - s * xp[..., 1]
            y1 = c * xp[..., 1] + s * xp[..., 0]
            return jnp.stack([y0, y1], axis=-1).reshape(x.shape)
        q = givens_rotate(rot_w[0], Q)
        k = givens_rotate(rot_w[1], Q)
        v = givens_rotate(rot_w[2], Q)
        zeros = jnp.zeros(Q.shape[:-1] + (1,), Q.dtype)
        q = jnp.concatenate([zeros, q], axis=-1)[:, None]
        k = jnp.concatenate([zeros, k], axis=-1)[:, None]
        v = jnp.concatenate([zeros, v], axis=-1)[:, None]
        sgn = jnp.concatenate([-jnp.ones((1,), Q.dtype), jnp.ones((q.shape[-1] - 1,), Q.dtype)])
        cin = jnp.einsum('bhqd,bhkd->bhqk', q * sgn, k)
        attn = jax.nn.softmax((2.0 + 2.0 * cin) / scale + bias, axis=-1)
        ave = jnp.einsum('bhqk,bhkd->bhqd', attn, v)
        inner = jnp.sum(ave * ave * sgn, axis=-1, keepdims=True)
        denom = jnp.sqrt(jnp.clip(jnp.abs(inner), 1e-08, None))
        out = (ave / denom)[:, 0]
        return out[..., 1:]

    def _L1_xattn_ref(text_embeddings, dinov2_features, W_d2v, b_d2v, W_img, b_img, W_txt, b_txt, W_att0, b_att0, W_att1, b_att1, W_f1, b_f1, W_f2, b_f2):
        import jax, jax.numpy as jnp
        import numpy as np
        import math
        E = 128
        EV = 128
        FFN = 512
        DINO = 96
        B, S, P = (64, 64, 32)

        def bitnet_linear(x, W, b):
            w_scale = jnp.maximum(jnp.mean(jnp.abs(W)), 1e-05)
            qW = jnp.sign(W) * (jnp.abs(W) > 0.5 * w_scale).astype(W.dtype)
            i_scale = jnp.maximum(jnp.max(jnp.abs(x)), 1e-08) / 127.0
            qx = jnp.clip(jnp.round(x / i_scale), -128.0, 127.0)
            out = jnp.einsum('...i,oi->...o', qx, qW) * (w_scale * i_scale)
            return out + b
        b, s, e = text_embeddings.shape
        vis = bitnet_linear(dinov2_features, W_d2v, b_d2v)
        image_embeds = bitnet_linear(vis, W_img, b_img)
        fused = bitnet_linear(text_embeddings, W_txt, b_txt)
        inv_sqrt_e = 1.0 / math.sqrt(e)
        for Wa, ba in ((W_att0, b_att0), (W_att1, b_att1)):
            kv = bitnet_linear(image_embeds, Wa, ba)
            k = jnp.concatenate([kv, kv], axis=-1)
            scores = jnp.einsum('bse,bpe->bsp', fused, k) * inv_sqrt_e
            attn = jax.nn.softmax(scores, axis=-1)
            fused = fused + 0.1 * jnp.einsum('bsp,bpe->bse', attn, k)
        avg_img = jnp.mean(image_embeds, axis=1, keepdims=True)
        concatenated = jnp.concatenate([fused, jnp.broadcast_to(avg_img, (b, s, e))], axis=-1)
        h = jax.nn.relu(bitnet_linear(concatenated, W_f1, b_f1))
        return bitnet_linear(h, W_f2, b_f2)

    def _L1_ffn_ref(x, Wr, A, Bw):
        import jax, jax.numpy as jnp
        import numpy as np
        B, L, H = (8, 256, 128)
        E, K, R = (8, 2, 64)

        def _gates(cls_tok, Wr):
            logits = cls_tok @ Wr.T
            top_vals, top_idx = jax.lax.top_k(logits, K)
            neg_inf = jnp.full_like(logits, -jnp.inf)
            rows = jnp.arange(logits.shape[0])[:, None]
            masked = neg_inf.at[rows, top_idx].set(top_vals)
            return jax.nn.softmax(masked, axis=-1)
        gates = _gates(x[:, 0, :], Wr)
        mid = jnp.einsum('blh,erh->belr', x, A)
        expert_out = jnp.einsum('belr,ehr->belh', mid, Bw)
        weighted = jnp.einsum('be,belh->blh', gates, expert_out)
        return x + weighted
    x = _layernorm(x + _L0_attn_ref(x, L0_attn_W_qkv, L0_attn_qn_w, L0_attn_kn_w, L0_attn_W_out, L0_attn_b_out), axis=-1)
    x = _layernorm(x + _L0_xattn_ref(x, ctx_768, L0_xattn_Wq, L0_xattn_Wk, L0_xattn_Wv, L0_xattn_Wo, L0_xattn_bo), axis=-1)
    x = _layernorm(x + _L0_ffn_ref(x, L0_ffn_gate_w, L0_ffn_gate_bias, L0_ffn_Wg, L0_ffn_Wu, L0_ffn_Wd, L0_ffn_Sg, L0_ffn_Su, L0_ffn_Sd), axis=-1)
    x = _layernorm(x + _L1_attn_ref(x, L1_attn_rot_w, L1_attn_scale, L1_attn_bias), axis=-1)
    x = _layernorm(x + _L1_xattn_ref(x, ctx_768, L1_xattn_W_d2v, L1_xattn_b_d2v, L1_xattn_W_img, L1_xattn_b_img, L1_xattn_W_txt, L1_xattn_b_txt, L1_xattn_W_att0, L1_xattn_b_att0, L1_xattn_W_att1, L1_xattn_b_att1, L1_xattn_W_f1, L1_xattn_b_f1, L1_xattn_W_f2, L1_xattn_b_f2), axis=-1)
    x = _layernorm(x + _L1_ffn_ref(x, L1_ffn_Wr, L1_ffn_A, L1_ffn_Bw), axis=-1)
    return x

_drawn_inputs = setup_inputs


def setup_inputs(seed=0):
    import zlib

    import numpy as np

    out = dict(_drawn_inputs(seed))
    spreads = {'L0_attn_qn_w': (1.0, 0.6),
     'L0_attn_kn_w': (1.0, 0.6),
     'L0_attn_b_out': (0.0, 0.1),
     'L1_xattn_b_d2v': (0.0, 0.1),
     'L1_xattn_b_img': (0.0, 0.1),
     'L1_xattn_b_txt': (0.0, 0.1),
     'L1_xattn_b_att0': (0.0, 0.8),
     'L1_xattn_b_att1': (0.0, 2.0),
     'L1_xattn_b_f1': (0.0, 0.1),
     'L1_xattn_b_f2': (0.0, 0.1)}
    factors = {'L0_xattn_bo': 5.204,
     'L0_ffn_gate_w': 7.313,
     'L0_ffn_gate_bias': 8.0,
     'L0_ffn_Wg': 7.12,
     'L0_ffn_Wu': 6.95,
     'L0_ffn_Wd': 6.984,
     'L0_ffn_Sg': 5.846,
     'L0_ffn_Su': 5.895,
     'L0_ffn_Sd': 5.797}
    for name, (base, spread) in spreads.items():
        noise = np.random.default_rng([zlib.crc32(name.encode()), seed]).standard_normal(out[name].shape)
        drawn = base * np.exp(spread * noise) if base else spread * noise
        out[name] = jnp.asarray(drawn.astype(out[name].dtype))
    for name, factor in factors.items():
        out[name] = (out[name] * factor).astype(out[name].dtype)
    return out
```

```python
from contextlib import ExitStack

import concourse.bass as bass
from concourse import mybir

P = 128
T = 1024
NT = T // P
D = 128
HALF = 512
NC = 6404
DC = 96
KT = -(-NC // P)
TAIL = NC - (KT - 1) * P
HD = 64
HEADS0 = 8
PAIRS = HEADS0 // 2
L0H = 16
L0D = D // L0H
E = 64
EI = 88
NG = 8
GE = E // NG
BLK = E * EI // P
RE = 8
RR = 64
FFN = 512
LN_EPS = 1e-5
RMS_EPS = 1e-6
DEN_EPS = 1e-6
ROUTED_SCALE = 2.5
MAGIC = 12582912.0
NEG = -3.0e38
KW = 1024
KCH = [(c, min(KW, NC - c)) for c in range(0, NC, KW)]
NKC = len(KCH)
VG = [list(range(g, min(g + 4, KT))) for g in range(0, KT, 4)]
NVG = len(VG)
MW = 2048
MCH = [(c, min(MW, NC - c)) for c in range(0, NC, MW)]
NM = len(MCH)

F32 = mybir.dt.float32
F16 = mybir.dt.float16
BF16 = mybir.dt.bfloat16
ALU = mybir.AluOpType
ACT = mybir.ActivationFunctionType
X = mybir.AxisListType.X
RED = bass.bass_isa.ReduceOp

SMALL = {}
_at = 0
for _n, _w in [("qk_w", 2 * D), ("b_out", D), ("bo", D), ("gate_w", E), ("gate_b", E), ("rot", 6), ("sb", 2),
               ("b_d2v", 1), ("b_img", 1), ("b_txt", 1), ("b_att0", 1), ("b_att1", 1), ("b_f1", FFN // P),
               ("b_f2", D), ("b_att0_row", HD), ("b_att1_row", HD), ("w_r", RE), ("w_out", D), ("w_qkv", 3 * D)]:
    SMALL[_n] = (_at, _at + _w)
    _at += _w
NSMALL = _at
BIT = {"d2v": (0, 128, DC, DC * 128), "img": (128, 128, 128, 128 * 128), "txt": (256, 128, 128, 128 * 128),
       "att0": (384, 64, 128, 64 * 128), "att1": (448, 64, 128, 64 * 128),
       "f1": (512, 2 * FFN, 128, 2 * D * FFN), "f2": (1536, 4 * D, 128, D * FFN)}
BIT_N = list(BIT)
NBIT = 2048


def rows_of(j):
    return P if j < KT - 1 else TAIL


def build_decoder(nc, x_tm, x_fm, ctx_fm, small, pair_w, moe_w, sh_gu, sh_d, bit_w, lr_a, lr_b, out, last=6):
    with ExitStack() as ctx:
        def sb(name, shape, dt=F32):
            return ctx.enter_context(nc.sbuf_tensor(name, shape, dt))

        def sem(name):
            return ctx.enter_context(nc.semaphore(name))

        PS = ctx.enter_context(nc.psum_tensor("PS", [P, 8, HALF], F32))

        CTX = sb("CTX", [DC, NC])
        KA = [sb(f"KA{h}", [P, NC], F16) for h in range(2)]
        KB = [sb(f"KB{h}", [P, NC], F16) for h in range(2)]
        V = sb("V", [P, KT, P])
        PR = sb("PR", [P, 3, T])
        ACC = sb("ACC", [P, 2, T])
        X_ = sb("X", [P, NT, D])
        R = sb("R", [P, NT, D])
        XT = sb("XT", [P, T])
        QS = sb("QS", [P, T])
        ON = sb("ON", [P, T])
        QA = [sb(f"QA{h}", [P, T], F16) for h in range(2)]
        QB = [sb(f"QB{h}", [P, T], F16) for h in range(2)]
        SM = sb("SM", [P, NSMALL])
        ident = sb("ident", [P, P])
        ones = sb("ones", [P, P])
        PWQ = sb("PWQ", [P, 3, P])
        PWO = sb("PWO", [P, D])
        LNS = sb("LNS", [P, NT, 6])
        LNM = sb("LNM", [P, NT, 2])
        LNV = sb("LNV", [P, NT])
        LND = sb("LND", [P, NT])
        LNR = sb("LNR", [P, NT])
        MXP = sb("MXP", [P, 2 * NT, NM])
        NEGM = sb("NEGM", [P, 2 * NT])

        def sm(name):
            a, b = SMALL[name]
            return SM[:, a:b]

        BIG = V[:, :, :].rearrange("p a b -> p (a b)")
        KF = [KA[h][:, :].bitcast(F32) for h in range(2)]
        KG = [KB[h][:, :].bitcast(F32) for h in range(2)]

        sems = {}

        def S(name):
            if name not in sems:
                sems[name] = sem(name)
            return sems[name]



        def bank(a, b=None, part=slice(0, P)):
            b = a + 1 if b is None else b
            return PS[part, a:b, :].rearrange("p a b -> p (a b)")

        def MW_(s):
            return BIG[:, s * 384:(s + 1) * 384].rearrange("p (a b) -> p a b", a=3)
        ROUT = 1536
        SEL = KA[0][:, 0:E * EI]
        MH = [KG[0][:, 0:T], KG[0][:, T:2 * T]]
        MS = [KG[1][:, 0:T], KG[1][:, T:2 * T]]
        MU = KA[1][:, 0:2 * T].bitcast(F32)
        RWT = KA[1][:, 2 * T:3 * T]
        RWF = KA[1][:, 3 * T:5 * T].bitcast(F32)
        VA = BIG[:, 0:NT * (D + 1)].rearrange("p (t d) -> p t d", t=NT)
        QK0 = KF[0][:, 0:NT * 2 * D].rearrange("p (t a d) -> p t a d", t=NT, a=2)
        SCR = KF[1][:, 0:2 * NT * D].rearrange("p (n d) -> p n d", d=D)
        SS = LNS[:, :, 0:2]
        MASK = KG[0][:, 0:D]
        KVB = KG[0][:, D:3 * D]
        KVS = KG[0][:, 3 * D:4 * D + 1]
        DEN = KG[1][:, 0:T]
        RMS = KG[1][:, T:T + 2 * NT]
        RMD = KG[1][:, T + 32:T + 32 + 2 * NT]
        RMR = KG[1][:, T + 64:T + 64 + 2 * NT]
        QS2 = KG[1][:, T + 128:2 * T + 128]
        XB = PR[:, 0, :]
        DEN2 = sb("DEN2", [P, HALF])[:, :]
        RW_TM = [None]
        SWAP = BIG[:, 0:D]
        ROT = BIG[:, D:4 * D].rearrange("p (a d) -> p a d", a=3)
        G3 = BIG[:, 512:518].rearrange("p (a b) -> p a b", b=2)
        GQ = BIG[:, 520:526].rearrange("p (a b) -> p a b", b=2)
        GN = BIG[:, 528:531]
        GD = BIG[:, 532:535]
        GR = BIG[:, 536:539]
        HS = BIG[:, 540:544]
        HM = BIG[:, 544:544 + NT]
        HL = BIG[:, 552:552 + NT]
        HLR = BIG[:, 560:560 + NT]
        HI = BIG[:, 568:568 + NT]
        HID = BIG[:, 576:576 + NT]
        HIR = BIG[:, 584:584 + NT]
        HC = BIG[:, 592:592 + NT]
        HNM = BIG[:, 600:600 + NT]
        HQ = KF[0][:, 0:T]
        HK = KF[0][:, T:2 * T]
        HV = KF[1][:, 0:T].rearrange("p (j d) -> p j d", j=NT)
        HP = [PR[:, 0, :], PR[:, 1, :]]
        HPT = [KG[0][:, 0:T].rearrange("p (j d) -> p j d", j=NT),
               KG[0][:, T:2 * T].rearrange("p (j d) -> p j d", j=NT)]
        HO = KG[1][:, 0:T].rearrange("p (j d) -> p j d", j=NT)
        HSQ = KG[1][:, T:2 * T].rearrange("p (j d) -> p j d", j=NT)
        BW = sb("BW", [P, NBIT])
        BQ = sb("BQ", [P, NBIT], BF16)
        BQD = sb("BQD", [P, 2, P], BF16)
        BR = sb("BR", [P, 8])
        BT = sb("BT", [P, 8])
        BS = sb("BS", [P, 8])
        BH = sb("BH", [P, 8])
        BN = sb("BN", [P, 8])
        NQ = 8
        AX = sb("AX", [P, NQ])
        AM = sb("AM", [P, NQ])
        AS = sb("AS", [P, NQ])
        AI = sb("AI", [P, NQ])
        WS = sb("WS", [P, NQ + 2])
        AVG = sb("AVG", [P, 4])
        DUP = sb("DUP", [P, P])[:, :]
        LA = PR[:, 0, 0:4 * P]
        LB = PR[:, 0, 4 * P:8 * P].rearrange("p (a d) -> p a d", a=4)


        CQ = KA[1][0:DC, :].bitcast(BF16)
        VQ = KA[1][:, :].bitcast(BF16)
        IQ = KB[1][:, :].bitcast(BF16)
        KVF = BIG
        V2 = sb("V2", [P, KT, HD])
        HB = [BIG[:, b * T:(b + 1) * T] for b in range(4)]
        HBQ = [KA[1][:, b * T:(b + 1) * T].bitcast(BF16) for b in range(4)]
        FQ = KB[1][:, 0:T].bitcast(BF16)
        AQ = KB[1][:, T:T + HALF].bitcast(BF16)
        XQ = KA[0][:, 0:T].bitcast(BF16)
        XF = PR[:, 0, :]
        OO = PR[:, 1, :]
        GC = sb("GC", [P, 4])
        GNM = sb("GNM", [1, 1])[:, :]
        GE_ = sb("GE", [1, RE])[:, :]
        GL0 = sb("GL", [1, RE])[:, :]
        GX = sb("GX", [1, 4 * P])[:, :]
        GT = sb("GT", [1, 64])
        MID = [BIG[:, b * T:(b + 1) * T] for b in range(4)]

        block = ctx.enter_context(nc.Block())

        @block.sync
        def _(q):
            q.dma_start(SM[:, :], small).then_inc(S("ld_small"), 16)
            q.dma_start(XT[:, :], x_fm).then_inc(S("ld_x"), 16)
            q.dma_start(X_[:, :, :], x_tm.rearrange("(t p) d -> p t d", p=P)).then_inc(S("ld_x"), 16)
            q.dma_start(CTX[:, :], ctx_fm).then_inc(S("ld_ctx"), 16)
            if last >= 2:
                def copy_k_hi(p):
                    q.wait_ge(S("k_hi"), p * NKC + NKC)
                    q.dma_start(KB[0][0:HD, :], KA[0][0:HD, :]).then_inc(S("kb"), 16)
                    q.dma_start(KB[1][HD:P, :], KA[1][HD:P, :]).then_inc(S("kb"), 16)

                q.dma_start(PWQ[:, :, :], pair_w[0, :, 0:3, :]).then_inc(S("ld_pwq"), 16)
                q.dma_start(PWO[:, :], pair_w[0, :, 3, :]).then_inc(S("ld_pwo"), 16)
                copy_k_hi(0)
                with q.Fori(1, PAIRS) as p:
                    q.wait_ge(S("v_ps"), p * NVG)
                    q.dma_start(PWQ[:, :, :], pair_w[bass.ds(p, 1), :, 0:3, :].rearrange("o p a b -> (o p) a b")
                                ).then_inc(S("ld_pwq"), 16)
                    q.wait_ge(S("wo_ps"), p)
                    q.dma_start(PWO[:, :], pair_w[bass.ds(p, 1), :, 3, :].rearrange("o p b -> (o p) b")
                                ).then_inc(S("ld_pwo"), 16)
                    copy_k_hi(p)
            if last >= 3:
                q.wait_ge(S("x_fm"), 2)
                q.wait_ge(S("moe_zero"), 1)
                for h in range(2):
                    q.dma_start(MW_(2 + h)[:, 0:2, 0:EI], sh_gu[h]).then_inc(S(f"ld_w{2 + h}"), 16)
                    q.dma_start(MW_(2 + h)[0:EI, 2, :], sh_d[h]).then_inc(S(f"ld_w{2 + h}"), 16)
                for j in range(4):
                    if j >= 2:
                        q.wait_ge(S("moe_down"), j - 1)
                    q.dma_start(MW_(j)[:, :, :], moe_w[j]).then_inc(S(f"ld_w{j}"), 16)
                with q.Fori(1, BLK // 4) as i:
                    for j in range(4):
                        q.wait_ge(S("moe_down"), 4 * i + (j - 1))
                        q.dma_start(MW_(j)[:, :, :],
                                    moe_w[bass.ds(4 * i + j, 1)].rearrange("o p a b -> (o p) a b")
                                    ).then_inc(S(f"ld_w{j}"), 16)
            if last >= 5:
                q.wait_ge(S("bit_zero"), 1)
                q.dma_start(BW[:, 128:NBIT], bit_w[:, 128:NBIT]).then_inc(S("ld_bit"), 16)
                q.dma_start(BW[0:DC, 0:128], bit_w[0:DC, 0:128]).then_inc(S("ld_bit"), 16)
            if last >= 6:
                q.wait_ge(S("ln_x"), 5)
                q.dma_start(LA, lr_a).then_inc(S("ld_lr"), 16)
                q.dma_start(LB, lr_b.rearrange("(a p) d -> p a d", p=P)).then_inc(S("ld_lr"), 16)
            q.wait_ge(S("ln_x"), last)
            q.dma_start(out.rearrange("o (t p) d -> p (o t) d", p=P), X_[:, :, :]).then_inc(S("stored"), 16)
            q.wait_ge(S("stored"), 16)

        @block.gpsimd
        def _(e):
            n = [0]

            def link(ins):
                n[0] += 1
                ins.then_inc(S("pool_step"), 1)
                e.wait_ge(S("pool_step"), n[0])

            def diag(ap, base, fill=1.0, pattern=None, mult=1):
                link(e.affine_select(out=ap, in_=ap, compare_op=ALU.not_equal, fill=fill, base=base,
                                     pattern=pattern or [[-1, P]], channel_multiplier=mult))

            link(e.memset(ident[:, :], 0.0))
            diag(ident[:, :], 0)
            link(e.memset(ones[:, :], 1.0))
            link(e.memset(MASK, 1.0))
            m3 = MASK.rearrange("p (a b) -> p a b", b=L0D)
            link(e.affine_select(out=m3, in_=m3, compare_op=ALU.is_ge, fill=0.0, base=0,
                                 pattern=[[-L0D, L0H], [0, L0D]], channel_multiplier=1))
            link(e.affine_select(out=m3, in_=m3, compare_op=ALU.is_ge, fill=0.0, base=L0D - 1,
                                 pattern=[[L0D, L0H], [0, L0D]], channel_multiplier=-1))
            link(e.memset(VA[:, :, D:D + 1], 1.0))
            e.sem_inc(S("consts"), 1)

            if last >= 2:
                e.wait_ge(S("x_fm"), 1)
                for h in range(2):
                    lo = slice(HD, P) if h == 0 else slice(0, HD)
                    link(e.memset(KB[h][lo, :], 0.0))
                    link(e.memset(KB[h][lo.start:lo.start + 1, :], 1.0))
                    link(e.memset(QB[h][lo, :], 0.0))
                e.sem_inc(S("shift_rows"), 1)
            if last >= 3:
                e.wait_ge(S("ln_x"), 2)
                sv = SEL.rearrange("p (e i) -> p e i", i=EI)
                link(e.memset(SEL, 0.0))
                for base in (0, -E):
                    diag(sv, base, pattern=[[-1, E], [0, EI]])
                link(e.memset(BIG[:, 2 * 384:4 * 384], 0.0))
                e.sem_inc(S("moe_zero"), 1)
            if last >= 4:
                e.wait_ge(S("ln_x"), 3)
                link(e.memset(SWAP, 0.0))
                w3 = SWAP.rearrange("p (a b) -> p a b", b=2)
                diag(w3[:, :, 1], 0, 1.0, [[-2, D // 2]])
                diag(w3[:, :, 0], -1, -1.0, [[-2, D // 2]])
                e.sem_inc(S("swap"), 1)
            if last >= 5:
                e.wait_ge(S("ln_x"), 4)
                link(e.memset(DUP, 0.0))
                for base in (0, HD, -HD):
                    diag(DUP, base)
                link(e.memset(AX[:, :], 0.0))
                link(e.memset(BW[:, 0:128], 0.0))
                link(e.memset(KB[0][HD:P, :], 0.0))
                link(e.memset(KB[0][HD:HD + 1, :], 1.0))
                link(e.memset(QB[0][HD:P, :], 0.0))
                e.sem_inc(S("bit_zero"), 1)
                e.wait_ge(S("bit_rows"), 1)
                e.partition_all_reduce(BT[:, 0:7], BR[:, 0:7], P, RED.add).then_inc(S("bit_sum"), 1)
                for i in range(6):
                    e.wait_ge(S("ax"), i + 1)
                    e.partition_all_reduce(AM[:, i:i + 1], AX[:, i:i + 1], P, RED.max).then_inc(S("am"), 1)

        @block.scalar
        def _(e):
            n = [0]

            def link(ins):
                n[0] += 1
                ins.then_inc(S("act_step"), 1)
                e.wait_ge(S("act_step"), n[0])

            def ln(k):
                e.wait_ge(S("ln_var"), k)
                e.activation(LND[:, :], LNV[:, :], ACT.Sqrt).then_inc(S("ln_sd"), 1)

            def to_fm(k, a):
                e.wait_ge(S("xt_ps"), k)
                e.activation(XT[:, :], bank(a, a + 2), ACT.Copy).then_inc(S("x_fm"), 1)

            for t in range(NT):
                e.wait_ge(S("qkv"), t + 1)
                for a in range(2):
                    e.activation(SCR[:, 2 * t + a, :], PS[:, t, a * D:(a + 1) * D], ACT.Square,
                                 accum_out=SS[:, t, a:a + 1])
                e.wait_ge(S("consts"), 1)
                e.activation(VA[:, t, 0:D], PS[:, t, 2 * D:3 * D], ACT.Copy).then_inc(S("v0"), 1)
            e.wait_ge(S("rms"), 1)
            e.activation(RMD, RMS, ACT.Sqrt).then_inc(S("rms_sd"), 1)
            e.wait_ge(S("q0_t"), 1)
            e.activation(QS[:, :], bank(1, 3), ACT.Copy).then_inc(S("q0_fm"), 1)
            ln(1)
            to_fm(1, 0)

            def exps(base, count, j_of):
                for g in range(count):
                    r = rows_of(j_of(g))
                    e.wait_ge(S("scores"), base + g + 1)
                    if g >= 3:
                        e.wait_ge(S("pv"), base + g - 2)
                        e.wait_ge(S("acc"), base + g - 2)
                    e.activation(PR[0:r, g % 3, :], bank(2 * (g % 2), 2 * (g % 2) + 2, slice(0, r)), ACT.Exp,
                                 scale=exp_scale[0]).then_inc(S("exp"), 1)

            exp_scale = [1.0]
            if last >= 2:
                with e.Fori(0, PAIRS) as p:
                    e.wait_ge(S("q_ps"), p + 1)
                    e.activation(QS[:, :], bank(0, 2), ACT.Copy, scale=HD ** -0.5).then_inc(S("q_ev"), 1)
                    for c, (a, w) in enumerate(KCH):
                        b = 2 * ((c + 1) % 2)
                        e.wait_ge(S("k_ps"), p * NKC + c + 1)
                        e.activation(KA[0][0:HD, a:a + w], bank(b, b + 2, slice(0, HD))[:, 0:w], ACT.Copy)
                        e.activation(KA[1][HD:P, a:a + w], bank(b, b + 2, slice(HD, P))[:, 0:w],
                                     ACT.Copy).then_inc(S("k_hi"), 1)
                        for g in (2 * c, 2 * c + 1):
                            if g < NVG:
                                e.wait_ge(S("v_ps"), p * NVG + g + 1)
                                full = [j for j in VG[g] if rows_of(j) == P]
                                ins = e.activation(V[:, full[0]:full[-1] + 1, :],
                                                   PS[:, 4 + g % 4, 0:P * len(full)].rearrange(
                                                       "p (a b) -> p a b", b=P), ACT.Copy)
                                if len(full) < len(VG[g]):
                                    ins = e.activation(V[0:TAIL, KT - 1, :],
                                                       PS[0:TAIL, 4 + g % 4, P * len(full):P * len(full) + P],
                                                       ACT.Copy)
                                ins.then_inc(S("v_ev"), 1)
                    e.wait_ge(S("shift_ps"), p + 1)
                    e.wait_ge(S("shift_rows"), 1)
                    e.activation(QB[0][HD:HD + 1, :], bank(0, 2, slice(HD, HD + 1)), ACT.Copy)
                    e.activation(QB[1][0:1, :], bank(2, 4, slice(0, 1)), ACT.Copy).then_inc(S("shift"), 1)
                    exps(p * 2 * KT, 2 * KT, lambda g: g % KT)
                ln(2)
                to_fm(2, 0)
            if last >= 3:
                e.wait_ge(S("logits"), 1)
                e.activation(BIG[:, ROUT:ROUT + NT * E], bank(2), ACT.Sigmoid).then_inc(S("sig"), 1)
                e.wait_ge(S("rw_t"), 1)
                e.activation(RWF[0:E, :], bank(2, 4, slice(0, E)), ACT.Copy).then_inc(S("rw_fm"), 1)

                def silu(n, slot):
                    e.wait_ge(S("moe_gate"), n + 1)
                    if not isinstance(n, int) or n >= 2:
                        e.wait_ge(S("moe_h1"), n - 1)
                    e.activation(MS[slot], bank(0, 2), ACT.Silu).then_inc(S("moe_silu"), 1)

                silu(0, 0)
                silu(1, 1)
                with e.Fori(0, BLK // 4) as i:
                    for j in range(4):
                        silu(4 * i + (2 + j), j % 2)
                e.wait_ge(S("moe_down"), BLK + 2)
                e.activation(QS[:, :], bank(6, 8), ACT.Copy).then_inc(S("moe_fm"), 1)
                ln(3)
                to_fm(3, 0)
            if last >= 4:
                e.wait_ge(S("rot_n"), 1)
                e.activation(GD, GN, ACT.Sqrt).then_inc(S("rot_sd"), 1)
                e.wait_ge(S("hq"), 1)
                e.activation(HQ, bank(0, 2), ACT.Copy, scale=HS[:, 0:1])
                e.activation(HK, bank(2, 4), ACT.Copy)
                e.activation(HV.rearrange("p j d -> p (j d)"), bank(4, 6), ACT.Copy).then_inc(S("hqkv"), 1)
                for t in range(NT):
                    b = 2 * (t % 2)
                    e.wait_ge(S("h_max"), t + 1)
                    if t >= 2:
                        e.wait_ge(S("h_pt"), t - 1)
                    e.activation(HP[t % 2], bank(b, b + 2), ACT.Exp, bias=HNM[:, t:t + 1],
                                 accum_out=HL[:, t:t + 1]).then_inc(S("h_exp"), 1)
                    e.wait_ge(S("h_pt"), t + 1)
                    if t >= 2:
                        e.wait_ge(S("h_av"), t - 1)
                    e.activation(HPT[t % 2].rearrange("p j d -> p (j d)"), bank(4, 6),
                                 ACT.Copy).then_inc(S("h_ptc"), 1)
                for t in range(NT):
                    e.wait_ge(S("h_o"), 1)
                    ins = e.activation(HSQ[:, t, :], HO[:, t, :], ACT.Square, accum_out=HI[:, t:t + 1])
                ins.then_inc(S("h_inner"), 1)
                e.wait_ge(S("h_clip"), 1)
                e.activation(HID, HC, ACT.Sqrt).then_inc(S("h_sd"), 1)
                ln(4)
            if last >= 5:
                def scaled(out, a, w, q, bias, name, rows=slice(0, P), func=ACT.Identity):
                    e.activation(out, a, func, scale=WS[rows, q:q + 1], bias=bias).then_inc(S(name), 1)

                for lay, (q, bn) in enumerate((("0", "b_d2v"), ("1", "b_img"))):
                    e.wait_ge(S("ws"), lay + 1)
                    for m, (a, w) in enumerate(MCH):
                        e.wait_ge(S("bp"), lay * NM + m + 1)
                        b = 4 * (m % 2)
                        scaled(BIG[:, a:a + w], bank(b, b + 4)[:, 0:w], w, lay, sm(bn), "bev")
                e.wait_ge(S("f_int"), 1)
                e.wait_ge(S("ws"), 4)
                scaled(XT[:, :], bank(0, 2), T, 3, sm("b_txt"), "fused")
                for r in range(2):
                    e.wait_ge(S("kv_free"), r + 1)
                    for m, (a, w) in enumerate(MCH):
                        e.wait_ge(S("bp"), (2 + r) * NM + m + 1)
                        b = 4 * (m % 2)
                        scaled(KVF[:, a:a + w], bank(b, b + 4)[:, 0:w], w, 2 if r == 0 else 6,
                               sm(f"b_att{r}"), "bev")
                    e.wait_ge(S("vt_ps"), r + 1)
                    e.activation(V2[:, 0:KT - 1, :], bank(0, 7)[:, 0:(KT - 1) * HD].rearrange(
                        "p (a b) -> p a b", b=HD), ACT.Copy, scale=WS[:, (2 if r == 0 else 6):(3 if r == 0 else 7)])
                    e.activation(V2[0:TAIL, KT - 1, :], bank(0, 7, slice(0, TAIL))[:, (KT - 1) * HD:KT * HD],
                                 ACT.Copy, scale=WS[0:TAIL, (2 if r == 0 else 6):(3 if r == 0 else 7)]
                                 ).then_inc(S("vt_ev"), 1)
                    e.wait_ge(S("f2_ps"), r + 1)
                    e.activation(QS[:, :], bank(0, 2), ACT.Copy, scale=D ** -0.5).then_inc(S("f2"), 1)
                    e.wait_ge(S("shift_ps"), PAIRS + r + 1)
                    e.activation(QB[0][HD:HD + 1, :], bank(0, 2, slice(HD, HD + 1)),
                                 ACT.Copy).then_inc(S("shift"), 1)
                    exps(PAIRS * 2 * KT + r * KT, KT, lambda g: g)
                for b in range(4):
                    e.wait_ge(S("h1_ps"), b + 1)
                    e.wait_ge(S("ws"), 5)
                    scaled(HB[b], bank(2 * b, 2 * b + 2), T, 4, SM[:, SMALL["b_f1"][0] + b:SMALL["b_f1"][0] + b + 1],
                           "hb", func=ACT.Relu)
                e.wait_ge(S("f2o_ps"), 1)
                e.activation(QS[:, :], bank(0, 2), ACT.Copy, scale=WS[:, 5:6]).then_inc(S("f2o"), 1)
                ln(5)
                to_fm(4, 0)
            if last >= 6:
                e.wait_ge(S("g_max"), 1)
                e.activation(GE_, GL0, ACT.Exp, bias=GNM).then_inc(S("g_exp"), 1)
                for b in range(4):
                    e.wait_ge(S("mid_ps"), b + 1)
                    e.wait_ge(S("g_col"), 1)
                    e.activation(MID[b], bank(2 * (b % 2), 2 * (b % 2) + 2), ACT.Copy,
                                 scale=GC[:, b:b + 1]).then_inc(S("mid"), 1)
                ln(6)

        @block.vector
        def _(e):
            n = [0]

            def link(ins):
                n[0] += 1
                ins.then_inc(S("dve_step"), 1)
                e.wait_ge(S("dve_step"), n[0])

            def ln(k):
                for t in range(NT):
                    ins = e.bn_stats(LNS[:, t, :], R[:, t, :])
                link(ins)
                for t in range(NT):
                    ins = e.bn_aggr(LNM[:, t, :], LNS[:, t, :])
                link(ins)
                e.tensor_scalar(LNV[:, :], LNM[:, :, 1], LN_EPS, None, ALU.add).then_inc(S("ln_var"), 1)
                e.wait_ge(S("ln_sd"), k)
                link(e.reciprocal(LNR[:, :], LND[:, :]))
                for t in range(NT):
                    ins = e.tensor_scalar(X_[:, t, :], R[:, t, :], LNM[:, t, 0:1], LNR[:, t:t + 1],
                                          ALU.subtract, ALU.mult)
                ins.then_inc(S("ln_x"), 1)
                e.wait_ge(S("ln_x"), k)

            def over_tiles(row, tiles=NT):
                return row.unsqueeze(1).to_broadcast([P, tiles, row.shape[-1]])

            x2 = X_[:, :, :].rearrange("p t d -> p (t d)")
            r2 = R[:, :, :].rearrange("p t d -> p (t d)")

            e.wait_ge(S("ld_small"), 16)
            e.wait_ge(S("ld_x"), 32)
            link(e.tensor_tensor(XB.rearrange("p (t d) -> p t d", t=NT), X_[:, :, :], over_tiles(sm("b_out")),
                                 ALU.add))
            e.wait_ge(S("v0"), NT)
            e.tensor_scalar(RMS.rearrange("p (t a) -> p t a", a=2), SS, 1.0 / D, RMS_EPS, ALU.mult,
                            ALU.add).then_inc(S("rms"), 1)
            e.wait_ge(S("rms_sd"), 1)
            link(e.reciprocal(RMR, RMD))
            w = sm("qk_w")
            for t in range(NT):
                for a in range(2):
                    ins = e.scalar_tensor_tensor(QK0[:, t, a, :], PS[:, t, a * D:(a + 1) * D],
                                                 RMR[:, 2 * t + a:2 * t + a + 1], w[:, a * D:(a + 1) * D],
                                                 ALU.mult, ALU.mult)
            link(ins)
            qk_all = QK0.rearrange("p t a d -> p (t a d)")
            e.tensor_scalar(qk_all, qk_all, 0.0, None, ALU.max).then_inc(S("qk0"), 1)
            e.wait_ge(S("kv0"), 1)
            e.wait_ge(S("consts"), 1)
            link(e.tensor_copy(KVS, bank(0)[:, 0:D + 1]))
            link(e.tensor_tensor(KVB[:, 0:D], KVS[:, 0:D], MASK, ALU.mult))
            e.tensor_scalar(KVB[:, D:2 * D], MASK, KVS[:, D:D + 1], None, ALU.mult).then_inc(S("kvb"), 1)
            e.wait_ge(S("o0"), 1)
            link(e.tensor_scalar(DEN, bank(5, 7), DEN_EPS, None, ALU.add))
            link(e.reciprocal(QS2, DEN))
            e.tensor_tensor(ON[:, :], bank(3, 5), QS2, ALU.mult).then_inc(S("on0"), 1)
            e.wait_ge(S("wo0"), 1)
            link(e.tensor_tensor(r2, bank(1, 3), XB, ALU.add))
            ln(1)

            def split_lo(out, full, hi):
                return e.tensor_tensor(out, full, hi, ALU.subtract)

            def maxima(base, heads):
                m = 0
                for hq in range(heads * NT):
                    for c, (a, w) in enumerate(MCH):
                        b = 4 * (m % 2)
                        e.wait_ge(S("max_ps"), base + m + 1)
                        e.tensor_reduce(MXP[:, hq, c:c + 1], bank(b, b + 4)[:, 0:w], X,
                                        ALU.max).then_inc(S("max_red"), 1)
                        m += 1
                e.wait_ge(S("max_red"), base + m)
                e.tensor_reduce(NEGM[:, 0:heads * NT], MXP[:, 0:heads * NT, :], X, ALU.max,
                                negate=True).then_inc(S("negm"), 1)

            def sums(base, first, u):
                for j in range(KT):
                    g = first + j
                    r = rows_of(j)
                    e.wait_ge(S("exp"), base + g + 1)
                    if j == 0:
                        ins = e.tensor_copy(ACC[:, u, :], PR[:, g % 3, :])
                    else:
                        e.wait_ge(S("acc"), base + g)
                        ins = e.tensor_tensor(ACC[0:r, u, :], ACC[0:r, u, :], PR[0:r, g % 3, :], ALU.add)
                    ins.then_inc(S("acc"), 1)
                    if first and j == 1:
                        yield

            def normalize(base, u, obank, dbank):
                e.wait_ge(S("den_ps"), base + u + 1)
                e.reciprocal(DEN2, bank(dbank)).then_inc(S("den_r"), 1)
                e.wait_ge(S("den_r"), base + u + 1)
                e.tensor_tensor(ON[:, u * HALF:(u + 1) * HALF], bank(obank), DEN2, ALU.mult).then_inc(S("on"), 1)

            if last >= 2:
                link(e.tensor_tensor(R[:, :, :], X_[:, :, :], over_tiles(sm("bo")), ALU.add))
                e.wait_ge(S("shift_rows"), 1)
                with e.Fori(0, PAIRS) as p:
                    e.wait_ge(S("q_ev"), p + 1)
                    e.tensor_copy(QA[0][0:HD, :], QS[0:HD, :])
                    e.tensor_copy(QA[0][HD:P, :], QS[0:HD, :])
                    e.tensor_copy(QA[1][0:HD, :], QS[HD:P, :])
                    e.tensor_copy(QA[1][HD:P, :], QS[HD:P, :]).then_inc(S("q_hi"), 1)
                    e.wait_ge(S("q_hi"), p + 1)
                    split_lo(QB[0][0:HD, :], QS[0:HD, :], QA[0][0:HD, :])
                    split_lo(QB[1][HD:P, :], QS[HD:P, :], QA[1][HD:P, :]).then_inc(S("q_split"), 1)
                    for c, (a, w) in enumerate(KCH):
                        b = 2 * ((c + 1) % 2)
                        e.wait_ge(S("k_hi"), p * NKC + c + 1)
                        split_lo(KA[0][HD:P, a:a + w], bank(b, b + 2, slice(0, HD))[:, 0:w], KA[0][0:HD, a:a + w])
                        split_lo(KA[1][0:HD, a:a + w], bank(b, b + 2, slice(HD, P))[:, 0:w],
                                 KA[1][HD:P, a:a + w]).then_inc(S("k_lo"), 1)
                    maxima(p * 2 * NT * NM, 2)
                    for _s in sums(p * 2 * KT, 0, 0):
                        pass
                    for _s in sums(p * 2 * KT, KT, 1):
                        normalize(2 * p, 0, 4, 6)
                    normalize(2 * p, 1, 5, 7)
                    e.wait_ge(S("wo_ps"), p + 1)
                    e.tensor_tensor(r2, r2, bank(0, 2), ALU.add).then_inc(S("r_add"), 1)
                    e.wait_ge(S("r_add"), p + 1)
                ln(2)
            if last >= 3:
                at = [ROUT]

                def scratch(width):
                    a = at[0]
                    at[0] += width
                    return BIG[:, a:a + width]

                sig = scratch(NT * E)
                sfc = scratch(NT * E)
                e.wait_ge(S("sig"), 1)
                gb = sm("gate_b").unsqueeze(1).to_broadcast([P, NT, E])
                link(e.tensor_tensor(sfc.rearrange("p (t e) -> p t e", e=E), sig.rearrange("p (t e) -> p t e", e=E),
                                     gb, ALU.add))
                hi, lo = scratch(NT * E // 2), scratch(NT * E // 2)
                v = sfc.rearrange("p (n b) -> p n b", b=2)
                link(e.tensor_tensor(hi, v[:, :, 0], v[:, :, 1], ALU.max))
                link(e.tensor_tensor(lo, v[:, :, 0], v[:, :, 1], ALU.min))
                wdt = NT * E // 2
                while wdt > NT * NG:
                    wdt //= 2
                    nh, nl, t1 = scratch(wdt), scratch(wdt), scratch(wdt)
                    h2, l2 = (z.rearrange("p (n b) -> p n b", b=2) for z in (hi, lo))
                    link(e.tensor_tensor(nh, h2[:, :, 0], h2[:, :, 1], ALU.max))
                    link(e.tensor_tensor(t1, h2[:, :, 0], h2[:, :, 1], ALU.min))
                    link(e.tensor_tensor(nl, l2[:, :, 0], l2[:, :, 1], ALU.max))
                    link(e.tensor_tensor(nl, nl, t1, ALU.max))
                    hi, lo = nh, nl
                gs = scratch(NT * NG)
                link(e.tensor_tensor(gs, hi, lo, ALU.add))
                rank = scratch(NT * NG)
                cmp = scratch(NT * NG)
                g3 = gs.rearrange("p (t g) -> p t g", g=NG)
                k3 = rank.rearrange("p (t g) -> p t g", g=NG)
                c3 = cmp.rearrange("p (t g) -> p t g", g=NG)
                link(e.memset(rank, 0.0))
                for o in range(NG):
                    other = g3[:, :, o:o + 1].to_broadcast([P, NT, NG])
                    if o < NG - 1:
                        link(e.tensor_tensor(c3[:, :, o + 1:NG], other[:, :, o + 1:NG], g3[:, :, o + 1:NG], ALU.is_ge))
                    if o > 0:
                        link(e.tensor_tensor(c3[:, :, 0:o], other[:, :, 0:o], g3[:, :, 0:o], ALU.is_gt))
                    link(e.memset(c3[:, :, o:o + 1], 0.0))
                    link(e.tensor_tensor(rank, rank, cmp, ALU.add))
                link(e.tensor_scalar(cmp, rank, float(NG // 2), None, ALU.is_lt))
                msk = scratch(NT * E)
                link(e.tensor_tensor(msk.rearrange("p (n e) -> p n e", e=GE), sfc.rearrange("p (n e) -> p n e", e=GE),
                                     cmp.unsqueeze(2).to_broadcast([P, NT * NG, GE]), ALU.mult))
                top = scratch(NT * 8)
                rep = scratch(NT * E)
                for t in range(NT):
                    ins = e.max(top[:, 8 * t:8 * t + 8], msk[:, t * E:(t + 1) * E])
                link(ins)
                for t in range(NT):
                    ins = e.match_replace(rep[:, t * E:(t + 1) * E], top[:, 8 * t:8 * t + 8],
                                          msk[:, t * E:(t + 1) * E], NEG)
                link(ins)
                tw = scratch(NT * E)
                link(e.scalar_tensor_tensor(tw, rep, NEG, sig, ALU.is_equal, ALU.mult))
                ts, tr = scratch(NT), scratch(NT)
                link(e.tensor_reduce(ts, tw.rearrange("p (t e) -> p t e", e=E), X, ALU.add))
                link(e.tensor_scalar(ts, ts, 1e-20, None, ALU.add))
                link(e.reciprocal(tr, ts))
                link(e.tensor_scalar(tr, tr, ROUTED_SCALE, None, ALU.mult))
                e.tensor_tensor(rep.rearrange("p (t e) -> p t e", e=E), tw.rearrange("p (t e) -> p t e", e=E),
                                tr.unsqueeze(2).to_broadcast([P, NT, E]), ALU.mult).then_inc(S("rw"), 1)
                RW_TM[0] = rep
                e.wait_ge(S("rw_fm"), 1)
                link(e.tensor_copy(RWT[0:E, :], RWF[0:E, :]))
                split_lo(RWT[E:P, :], RWF[0:E, :], RWT[0:E, :]).then_inc(S("rw_split"), 1)

                def hidden(n, slot, routed):
                    e.wait_ge(S("moe_silu"), n + 1)
                    e.wait_ge(S("moe_up"), n + 1)
                    if not isinstance(n, int) or n >= 1:
                        e.wait_ge(S("moe_h"), n)
                    e.tensor_tensor(MU, bank(2, 4), MS[slot], ALU.mult).then_inc(S("moe_h1"), 1)
                    e.wait_ge(S("moe_h1"), n + 1)
                    if not isinstance(n, int) or n >= 2:
                        e.wait_ge(S("moe_down"), n - 1)
                    if routed:
                        e.wait_ge(S("moe_rw"), n - 1)
                        ins = e.tensor_tensor(MH[slot], bank(4, 6), MU, ALU.mult)
                    else:
                        ins = e.tensor_copy(MH[slot], MU)
                    ins.then_inc(S("moe_h"), 1)

                hidden(0, 0, False)
                hidden(1, 1, False)
                with e.Fori(0, BLK // 4) as i:
                    for j in range(4):
                        hidden(4 * i + (2 + j), j % 2, True)
                e.wait_ge(S("moe_tm"), 1)
                link(e.tensor_tensor(r2, bank(0, 2), x2, ALU.add))
                ln(3)
            if last >= 4:
                e.wait_ge(S("swap"), 1)
                g = sm("rot").rearrange("p (a b) -> p a b", b=2)
                link(e.tensor_tensor(GQ, g, g, ALU.mult))
                e.tensor_reduce(GN, GQ, X, ALU.add).then_inc(S("rot_n"), 1)
                e.wait_ge(S("rot_sd"), 1)
                link(e.reciprocal(GR, GD))
                link(e.tensor_tensor(G3, g, GR.unsqueeze(2).to_broadcast([P, 3, 2]), ALU.mult))
                for a in range(3):
                    link(e.tensor_scalar(ROT[:, a, :], ident[:, :], G3[:, a, 0:1], None, ALU.mult))
                    link(e.scalar_tensor_tensor(ROT[:, a, :], SWAP, G3[:, a, 1:2], ROT[:, a, :], ALU.mult, ALU.add))
                sbv = sm("sb")
                link(e.reciprocal(HS[:, 1:2], sbv[:, 0:1]))
                link(e.tensor_scalar(HS[:, 0:1], HS[:, 1:2], 2.0, None, ALU.mult))
                e.tensor_tensor(HS[:, 2:3], HS[:, 0:1], sbv[:, 1:2], ALU.add).then_inc(S("rot"), 1)
                e.wait_ge(S("rot"), 1)
                for t in range(NT):
                    b = 2 * (t % 2)
                    e.wait_ge(S("h_s"), t + 1)
                    link(e.tensor_reduce(HM[:, t:t + 1], bank(b, b + 2), X, ALU.max))
                    link(e.tensor_scalar(HM[:, t:t + 1], HM[:, t:t + 1], HS[:, 2:3], -1.0, ALU.add, ALU.mult))
                    e.tensor_scalar(HNM[:, t:t + 1], HM[:, t:t + 1], HS[:, 2:3], None,
                                    ALU.add).then_inc(S("h_max"), 1)
                e.wait_ge(S("h_av"), NT)
                e.wait_ge(S("h_exp"), NT)
                link(e.reciprocal(HLR, HL))
                e.tensor_tensor(HO, bank(6, 8).rearrange("p (t d) -> p t d", d=D),
                                HLR.unsqueeze(2).to_broadcast([P, NT, D]), ALU.mult).then_inc(S("h_o"), 1)
                e.wait_ge(S("h_inner"), 1)
                e.tensor_scalar(HC, HI, 1e-8, None, ALU.max).then_inc(S("h_clip"), 1)
                e.wait_ge(S("h_sd"), 1)
                link(e.reciprocal(HIR, HID))
                link(e.tensor_tensor(HO, HO, HIR.unsqueeze(2).to_broadcast([P, NT, D]), ALU.mult))
                link(e.tensor_tensor(R[:, :, :], HO, X_[:, :, :], ALU.add))
                ln(4)
            if last >= 5:
                e.wait_ge(S("ld_bit"), 32)
                for i, nme in enumerate(BIT_N):
                    c, w_, _, _ = BIT[nme]
                    ins = e.tensor_reduce(BR[:, i:i + 1], BW[:, c:c + w_], X, ALU.add, apply_absolute_value=True)
                ins.then_inc(S("bit_rows"), 1)
                e.wait_ge(S("bit_zero"), 1)
                e.tensor_reduce(AX[0:DC, 0:1], CTX[:, :], X, ALU.max, apply_absolute_value=True
                                ).then_inc(S("ax"), 1)
                e.wait_ge(S("bit_sum"), 1)
                for i, nme in enumerate(BIT_N):
                    ins = e.tensor_scalar(BS[:, i:i + 1], BT[:, i:i + 1], 1.0 / BIT[nme][3], 1e-5, ALU.mult, ALU.max)
                link(ins)
                link(e.tensor_scalar(BH[:, 0:7], BS[:, 0:7], 0.5, None, ALU.mult))
                link(e.tensor_scalar(BN[:, 0:7], BS[:, 0:7], -0.5, None, ALU.mult))
                for i, nme in enumerate(BIT_N):
                    c, w_, _, _ = BIT[nme]
                    link(e.tensor_scalar(BQ[:, c:c + w_], BW[:, c:c + w_], BN[:, i:i + 1], None, ALU.is_lt))
                    link(e.scalar_tensor_tensor(BQ[:, c:c + w_], BW[:, c:c + w_], BH[:, i:i + 1], BQ[:, c:c + w_],
                                                ALU.is_gt, ALU.subtract))
                for r in range(2):
                    for a in range(2):
                        ins = e.tensor_copy(BQD[:, r, a * HD:(a + 1) * HD], BQ[:, 384 + 64 * r:448 + 64 * r])
                ins.then_inc(S("bit_q"), 1)

                def scale_of(i, weights):
                    e.wait_ge(S("am"), i + 1)
                    link(e.tensor_scalar(AS[:, i:i + 1], AM[:, i:i + 1], 1e-8, 1.0 / 127.0, ALU.max, ALU.mult))
                    link(e.reciprocal(AI[:, i:i + 1], AS[:, i:i + 1]))
                    for col, nme in weights:
                        k = BIT_N.index(nme)
                        ins = e.tensor_tensor(WS[:, col:col + 1], AS[:, i:i + 1], BS[:, k:k + 1], ALU.mult)
                    ins.then_inc(S("ws"), 1)

                def quantize(dst, src, tmp, i, rows=slice(0, P)):
                    link(e.tensor_scalar(tmp, src, AI[rows, i:i + 1], 127.0, ALU.mult, ALU.min))
                    link(e.tensor_scalar(tmp, tmp, -128.0, MAGIC, ALU.max, ALU.add))
                    return e.tensor_scalar(dst, tmp, MAGIC, None, ALU.subtract)

                scale_of(0, [(0, "d2v")])
                quantize(CQ, CTX[:, :], CTX[:, :], 0, slice(0, DC)).then_inc(S("quant"), 1)
                e.wait_ge(S("bev"), NM)
                e.tensor_reduce(AX[:, 1:2], BIG[:, 0:NC], X, ALU.max, apply_absolute_value=True
                                ).then_inc(S("ax"), 1)
                scale_of(1, [(1, "img")])
                e.wait_ge(S("bp"), NM)
                quantize(VQ, BIG[:, 0:NC], BIG[:, 0:NC], 1).then_inc(S("quant"), 1)
                e.wait_ge(S("bev"), 2 * NM)
                e.tensor_reduce(AX[:, 2:3], BIG[:, 0:NC], X, ALU.max, apply_absolute_value=True
                                ).then_inc(S("ax"), 1)
                link(e.tensor_reduce(AVG[:, 0:1], BIG[:, 0:NC], X, ALU.add))
                link(e.tensor_scalar(AVG[:, 1:2], AVG[:, 0:1], 1.0 / NC, None, ALU.mult))
                scale_of(2, [(2, "att0"), (6, "att1")])
                quantize(IQ, BIG[:, 0:NC], BIG[:, 0:NC], 2).then_inc(S("quant"), 1)
                e.wait_ge(S("quant"), 3)
                e.tensor_reduce(AX[:, 3:4], x2, X, ALU.max, apply_absolute_value=True).then_inc(S("ax"), 1)
                scale_of(3, [(3, "txt")])
                e.wait_ge(S("x4_t"), 1)
                quantize(XQ, bank(0, 2), XF, 3).then_inc(S("quant"), 1)

                for r in range(2):
                    wcol = 2 if r == 0 else 6
                    if r == 0:
                        e.sem_inc(S("kv_free"), 1)
                    e.wait_ge(S("bev"), (3 + r) * NM)
                    link(e.tensor_copy(KA[0][:, :], BIG[:, 0:NC]))
                    link(e.tensor_copy(KB[0][0:HD, :], KA[0][0:HD, :]))
                    link(split_lo(KA[0][HD:P, :], BIG[HD:P, 0:NC], KA[0][HD:P, :]))
                    e.sem_inc(S("kv_split"), 1)
                    e.wait_ge(S("vt_ev"), r + 1)
                    brow = sm(f"b_att{r}_row")
                    link(e.tensor_tensor(V2[:, 0:KT - 1, :], V2[:, 0:KT - 1, :],
                                         brow.unsqueeze(1).to_broadcast([P, KT - 1, HD]), ALU.add))
                    e.tensor_tensor(V2[0:TAIL, KT - 1, :], V2[0:TAIL, KT - 1, :], brow[0:TAIL, :],
                                    ALU.add).then_inc(S("v2"), 1)
                    e.wait_ge(S("f2"), r + 1)
                    link(e.tensor_copy(QA[0][:, :], QS[:, :]))
                    split_lo(QB[0][0:HD, :], QS[0:HD, :], QA[0][0:HD, :]).then_inc(S("q_split"), 1)
                    maxima(PAIRS * 2 * NT * NM + r * NT * NM, 1)
                    for _s in sums(PAIRS * 2 * KT + r * KT, 0, 0):
                        pass
                    normalize(2 * PAIRS + r, 0, 4, 6)
                    e.wait_ge(S("on"), 2 * PAIRS + r + 1)
                    for qh in range(2):
                        for fh in range(2):
                            ins = e.tensor_copy(OO[fh * HD:(fh + 1) * HD, qh * HALF:(qh + 1) * HALF],
                                                ON[qh * HD:(qh + 1) * HD, 0:HALF])
                    link(ins)
                    ins = e.scalar_tensor_tensor(XT[:, :], OO, 0.1, XT[:, :], ALU.mult, ALU.add)
                    if r == 0:
                        ins.then_inc(S("kv_free"), 1)
                        e.wait_ge(S("kv_free"), 2)
                    else:
                        link(ins)
                    e.sem_inc(S("fused_upd"), 1)
                link(e.tensor_reduce(AVG[:, 2:3], XT[:, :], X, ALU.max, apply_absolute_value=True))
                link(e.tensor_reduce(AVG[:, 3:4], AVG[:, 1:2], X, ALU.max, apply_absolute_value=True))
                e.tensor_tensor(AX[:, 4:5], AVG[:, 2:3], AVG[:, 3:4], ALU.max).then_inc(S("ax"), 1)
                scale_of(4, [(4, "f1")])
                link(quantize(FQ, XT[:, :], XF, 4))
                link(quantize(AVG[:, 2:3], AVG[:, 1:2], AVG[:, 0:1], 4))
                e.tensor_copy(AQ, AVG[:, 2:3].to_broadcast([P, HALF])).then_inc(S("quant"), 1)
                e.wait_ge(S("hb"), 4)
                e.tensor_reduce(AX[:, 5:6], BIG[:, 0:4 * T], X, ALU.max).then_inc(S("ax"), 1)
                scale_of(5, [(5, "f2")])
                quantize(KA[1][:, 0:4 * T].bitcast(BF16), BIG[:, 0:4 * T], BIG[:, 0:4 * T], 5).then_inc(S("quant"), 1)
                e.wait_ge(S("f2o"), 1)
                link(e.tensor_tensor(R[:, :, :], QS[:, :].rearrange("p (t d) -> p t d", d=D),
                                     over_tiles(sm("b_f2")), ALU.add))
                link(e.tensor_tensor(r2, r2, x2, ALU.add))
                ln(5)
            if last >= 6:
                e.wait_ge(S("gl_ps"), 1)
                link(e.tensor_copy(GL0, PS[0:1, 2, 0:RE]))
                rank, cmp = GT[:, 0:RE], GT[:, RE:2 * RE]
                link(e.memset(rank, 0.0))
                for o in range(RE):
                    other = GL0[:, o:o + 1]
                    if o < RE - 1:
                        link(e.tensor_scalar(cmp[:, o + 1:RE], GL0[:, o + 1:RE], other, None, ALU.is_le))
                    if o > 0:
                        link(e.tensor_scalar(cmp[:, 0:o], GL0[:, 0:o], other, None, ALU.is_lt))
                    link(e.memset(cmp[:, o:o + 1], 0.0))
                    link(e.tensor_tensor(rank, rank, cmp, ALU.add))
                link(e.tensor_scalar(cmp, rank, 2.0, None, ALU.is_lt))
                e.tensor_reduce(GNM, GL0, X, ALU.max, negate=True).then_inc(S("g_max"), 1)
                e.wait_ge(S("g_exp"), 1)
                gm, gsum, grec, gate = GT[:, 16:24], GT[:, 24:25], GT[:, 25:26], GT[:, 32:40]
                link(e.tensor_tensor(gm, GE_, cmp, ALU.mult))
                link(e.tensor_reduce(gsum, gm, X, ALU.add))
                link(e.reciprocal(grec, gsum))
                link(e.tensor_scalar(gate, gm, grec, None, ALU.mult))
                e.tensor_copy(GX.rearrange("p (e r) -> p e r", r=RR),
                              gate.unsqueeze(2).to_broadcast([1, RE, RR])).then_inc(S("g_row"), 1)
                e.wait_ge(S("gc_ps"), 1)
                e.tensor_copy(GC[:, :], PS[:, 7, 0:4]).then_inc(S("g_col"), 1)
                e.wait_ge(S("lr_ps"), 1)
                link(e.scalar_tensor_tensor(r2, x2, 2.0, bank(5, 7), ALU.mult, ALU.add))
                ln(6)

        @block.tensor
        def _(e):
            def transposes(src, a, k, gate=None):
                for t in range(NT):
                    ins = e.transpose(PS[:, a + t // 4, (t % 4) * P:(t % 4 + 1) * P], src[:, t, :], ident[:, :])
                return ins

            def to_fm(k, a, lns):
                e.wait_ge(S("ln_x"), lns)
                transposes(X_, a, k).then_inc(S("xt_ps"), 1)

            e.wait_ge(S("ld_small"), 16)
            e.wait_ge(S("ld_x"), 32)
            for t in range(NT):
                e.matmul(PS[:, t, 0:3 * D], XT[:, t * P:(t + 1) * P], sm("w_qkv"), start=True,
                         stop=True).then_inc(S("qkv"), 1)
            e.wait_ge(S("qk0"), 1)
            e.wait_ge(S("v0"), NT)
            e.wait_ge(S("consts"), 1)
            for t in range(NT):
                ins = e.matmul(PS[:, 0, 0:D + 1], QK0[:, t, 1, :], VA[:, t, :], start=(t == 0), stop=(t == NT - 1))
            ins.then_inc(S("kv0"), 1)
            for t in range(NT):
                ins = e.transpose(PS[:, 1 + t // 4, (t % 4) * P:(t % 4 + 1) * P], QK0[:, t, 0, :], ident[:, :])
            ins.then_inc(S("q0_t"), 1)
            e.wait_ge(S("kvb"), 1)
            e.wait_ge(S("q0_fm"), 1)
            for a in range(2):
                for h in range(2):
                    ins = e.matmul(bank(3 + 2 * a + h), KVB[:, a * D:(a + 1) * D], QS[:, h * HALF:(h + 1) * HALF],
                                   start=True, stop=True)
            ins.then_inc(S("o0"), 1)
            e.wait_ge(S("on0"), 1)
            for t in range(NT):
                ins = e.matmul(PS[:, 1 + t // 4, (t % 4) * P:(t % 4 + 1) * P], ON[:, t * P:(t + 1) * P], sm("w_out"),
                               start=True, stop=True)
            ins.then_inc(S("wo0"), 1)
            to_fm(1, 0, 1)

            def max_scores(base, heads):
                m = 0
                for h in range(heads):
                    for t in range(NT):
                        for a, w in MCH:
                            if m >= 2:
                                e.wait_ge(S("max_red"), base + m - 1)
                            for i in range(-(-w // HALF)):
                                c = min(HALF, w - i * HALF)
                                ins = e.matmul(PS[:, 4 * (m % 2) + i, 0:c], QA[h][:, t * P:(t + 1) * P],
                                               KA[h][:, a + i * HALF:a + i * HALF + c], start=True, stop=True)
                            ins.then_inc(S("max_ps"), 1)
                            m += 1

            def shift_row(h, r, b):
                for t in range(NT):
                    ins = e.matmul(PS[r:r + 1, b + t // 4, (t % 4) * P:(t % 4 + 1) * P],
                                   NEGM[:, h * NT + t:h * NT + t + 1], ident[:, :], start=True, stop=True)
                return ins

            def attend(base, units, operands, den_base):
                def scores(g):
                    u, j = divmod(g, KT)
                    r = rows_of(j)
                    if g >= 2:
                        e.wait_ge(S("exp"), base + g - 1)
                    for side in range(2):
                        ka, kb, qa, qb, _ = operands(u, side)
                        o = PS[0:r, 2 * (g % 2) + side, :]
                        e.matmul(o, ka[:, j * P:j * P + r], qa, start=True, stop=False)
                        ins = e.matmul(o, kb[:, j * P:j * P + r], qb, start=False, stop=True)
                    ins.then_inc(S("scores"), 1)

                def values(g):
                    u, j = divmod(g, KT)
                    r = rows_of(j)
                    e.wait_ge(S("exp"), base + g + 1)
                    for side in range(2):
                        v = operands(u, side)[4]
                        ins = e.matmul(PS[side * HD:(side + 1) * HD, 4 + u, :], v(r, j),
                                       PR[0:r, g % 3, side * HALF:(side + 1) * HALF], start=(j == 0),
                                       stop=(j == KT - 1), skip_group_check=True)
                    ins.then_inc(S("pv"), 1)
                    if j == KT - 1:
                        e.wait_ge(S("acc"), base + g + 1)
                        for side in range(2):
                            ins = e.matmul(PS[side * HD:(side + 1) * HD, 6 + u, :], ones[:, 0:HD],
                                           ACC[:, u, side * HALF:(side + 1) * HALF], start=True, stop=True)
                        ins.then_inc(S("den_ps"), 1)

                for g in range(units * KT):
                    scores(g)
                    if g:
                        values(g - 1)
                values(units * KT - 1)

            if last >= 2:
                e.wait_ge(S("x_fm"), 1)
                e.wait_ge(S("ld_ctx"), 16)
                with e.Fori(0, PAIRS) as p:
                    e.wait_ge(S("ld_pwq"), p * 16 + 16)
                    for h in range(2):
                        ins = e.matmul(bank(h), PWQ[:, 0, :], XT[:, h * HALF:(h + 1) * HALF], start=True, stop=True)
                    ins.then_inc(S("q_ps"), 1)
                    for c, (a, w) in enumerate(KCH):
                        b = 2 * ((c + 1) % 2)
                        if c == 1:
                            e.wait_ge(S("q_ev"), p + 1)
                        if c >= 2:
                            e.wait_ge(S("k_lo"), p * NKC + c - 1)
                        for i in range(-(-w // HALF)):
                            cw = min(HALF, w - i * HALF)
                            ins = e.matmul(PS[:, b + i, 0:cw], PWQ[0:DC, 1, :],
                                           CTX[:, a + i * HALF:a + i * HALF + cw], start=True, stop=True)
                        ins.then_inc(S("k_ps"), 1)
                        for g in (2 * c, 2 * c + 1):
                            if g >= NVG:
                                continue
                            if g >= 4:
                                e.wait_ge(S("v_ev"), p * NVG + g - 3)
                            for i, j in enumerate(VG[g]):
                                r = rows_of(j)
                                ins = e.matmul(PS[0:r, 4 + g % 4, i * P:(i + 1) * P], CTX[:, j * P:j * P + r],
                                               PWQ[0:DC, 2, :], start=True, stop=True)
                            ins.then_inc(S("v_ps"), 1)
                    e.wait_ge(S("k_lo"), p * NKC + NKC)
                    e.wait_ge(S("v_ev"), p * NVG + NVG)
                    e.wait_ge(S("q_split"), p + 1)
                    max_scores(p * 2 * NT * NM, 2)
                    e.wait_ge(S("negm"), p + 1)
                    shift_row(0, HD, 0)
                    shift_row(1, 0, 2).then_inc(S("shift_ps"), 1)
                    e.wait_ge(S("shift"), p + 1)
                    e.wait_ge(S("kb"), 32 * p + 32)
                    e.wait_ge(S("shift_rows"), 1)

                    def operands(u, side):
                        q = slice(u * HALF, (u + 1) * HALF)
                        return (KA[side], KB[side], QA[side][:, q], QB[side][:, q],
                                lambda r, j: V[0:r, j, side * HD:(side + 1) * HD])
                    attend(p * 2 * KT, 2, operands, 2 * p)
                    e.wait_ge(S("on"), 2 * p + 2)
                    e.wait_ge(S("ld_pwo"), p * 16 + 16)
                    for t in range(NT):
                        ins = e.matmul(PS[:, t // 4, (t % 4) * P:(t % 4 + 1) * P], ON[:, t * P:(t + 1) * P],
                                       PWO[:, :], start=True, stop=True)
                    ins.then_inc(S("wo_ps"), 1)
                    e.wait_ge(S("r_add"), p + 1)
                to_fm(2, 0, 2)
            if last >= 3:
                e.wait_ge(S("x_fm"), 2)
                for t in range(NT):
                    ins = e.matmul(PS[:, 2, t * E:(t + 1) * E], XT[:, t * P:(t + 1) * P], sm("gate_w"),
                                   start=True, stop=True)
                ins.then_inc(S("logits"), 1)
                e.wait_ge(S("rw"), 1)
                for t in range(NT):
                    ins = e.transpose(PS[0:E, 2 + t // 4, (t % 4) * P:(t % 4 + 1) * P],
                                      RW_TM[0][:, t * E:(t + 1) * E], ident[:, :])
                ins.then_inc(S("rw_t"), 1)
                e.wait_ge(S("rw_split"), 1)
                e.wait_ge(S("moe_zero"), 1)

                def product(b, w_, n, name, ready):
                    for h in range(2):
                        ins = e.matmul(bank(b + h), w_, XT[:, h * HALF:(h + 1) * HALF], start=True, stop=True)
                    ins.then_inc(S(name), 1)

                def expert(n, slot, ld, block_at):
                    e.wait_ge(S(f"ld_w{slot}"), ld)
                    if not isinstance(n, int) or n >= 1:
                        e.wait_ge(S("moe_silu"), n)
                    product(0, MW_(slot)[:, 0, :], n, "moe_gate", None)
                    if not isinstance(n, int) or n >= 1:
                        e.wait_ge(S("moe_h1"), n)
                    product(2, MW_(slot)[:, 1, :], n, "moe_up", None)
                    if block_at is not None:
                        e.wait_ge(S("moe_h"), n)
                        for h in range(2):
                            ins = e.matmul(bank(4 + h), SEL[:, bass.ds(block_at, P)],
                                           RWT[:, h * HALF:(h + 1) * HALF], start=True, stop=True)
                        ins.then_inc(S("moe_rw"), 1)

                def down(n, slot, hslot, first=False, stop=False):
                    e.wait_ge(S("moe_h"), n + 1)
                    for h in range(2):
                        ins = e.matmul(bank(6 + h), MW_(slot)[:, 2, :], MH[hslot][:, h * HALF:(h + 1) * HALF],
                                       start=first, stop=stop, skip_group_check=True)
                    ins.then_inc(S("moe_down"), 1)

                expert(0, 2, 32, None)
                expert(1, 3, 32, None)
                down(0, 2, 0, first=True)
                with e.Fori(0, BLK // 4) as i:
                    for j in range(4):
                        expert(4 * i + (2 + j), j, 16 * i + (48 if j >= 2 else 16), 4 * P * i + j * P)
                        down(4 * i + (1 + j), (j - 1) % 4, (j + 1) % 2)
                down(BLK + 1, 3, 1, stop=True)
                e.wait_ge(S("moe_fm"), 1)
                for t in range(NT):
                    ins = e.transpose(PS[:, t // 4, (t % 4) * P:(t % 4 + 1) * P], QS[:, t * P:(t + 1) * P], ident[:, :])
                ins.then_inc(S("moe_tm"), 1)
                to_fm(3, 0, 3)
            if last >= 4:
                e.wait_ge(S("x_fm"), 3)
                e.wait_ge(S("rot"), 1)
                for a in range(2):
                    for h in range(2):
                        e.matmul(bank(2 * a + h), ROT[:, a, :], XT[:, h * HALF:(h + 1) * HALF], start=True, stop=True)
                for t in range(NT):
                    ins = e.matmul(PS[:, 4 + t // 4, (t % 4) * P:(t % 4 + 1) * P], XT[:, t * P:(t + 1) * P],
                                   ROT[:, 2, :], start=True, stop=True)
                ins.then_inc(S("hq"), 1)
                e.wait_ge(S("hqkv"), 1)

                def h_scores(t):
                    b = 2 * (t % 2)
                    if t >= 2:
                        e.wait_ge(S("h_exp"), t - 1)
                    for h in range(2):
                        ins = e.matmul(bank(b + h), HQ[:, t * P:(t + 1) * P], HK[:, h * HALF:(h + 1) * HALF],
                                       start=True, stop=True)
                    ins.then_inc(S("h_s"), 1)

                h_scores(0)
                for t in range(NT):
                    if t + 1 < NT:
                        h_scores(t + 1)
                    e.wait_ge(S("h_exp"), t + 1)
                    if t:
                        e.wait_ge(S("h_ptc"), t)
                    for j in range(NT):
                        ins = e.transpose(PS[:, 4 + j // 4, (j % 4) * P:(j % 4 + 1) * P], HP[t % 2][:, j * P:(j + 1) * P],
                                          ident[:, :])
                    ins.then_inc(S("h_pt"), 1)
                    e.wait_ge(S("h_ptc"), t + 1)
                    for j in range(NT):
                        ins = e.matmul(PS[:, 6 + t // 4, (t % 4) * P:(t % 4 + 1) * P], HPT[t % 2][:, j, :], HV[:, j, :],
                                       start=(j == 0), stop=(j == NT - 1))
                    ins.then_inc(S("h_av"), 1)
            if last >= 5:
                def ctx_layer(k, rhs, w_, rows, waits):
                    for s_, v_ in waits:
                        e.wait_ge(S(s_), v_)
                    for m, (a, w) in enumerate(MCH):
                        if m >= 2:
                            e.wait_ge(S("bev"), k * NM + m - 1)
                        for i in range(-(-w // HALF)):
                            c = min(HALF, w - i * HALF)
                            ins = e.matmul(PS[:, 4 * (m % 2) + i, 0:c], w_,
                                           rhs[:, a + i * HALF:a + i * HALF + c], start=True, stop=True)
                        ins.then_inc(S("bp"), 1)

                e.wait_ge(S("ln_x"), 4)
                ctx_layer(0, CQ, BQ[0:DC, 0:128], DC, [("bit_q", 1), ("quant", 1)])
                ctx_layer(1, VQ, BQ[:, 128:256], P, [("quant", 2), ("bev", NM)])
                e.wait_ge(S("bev"), 2 * NM)
                transposes(X_, 0, 0).then_inc(S("x4_t"), 1)
                e.wait_ge(S("quant"), 4)
                for h in range(2):
                    ins = e.matmul(bank(h), BQ[:, 256:384], XQ[:, h * HALF:(h + 1) * HALF], start=True, stop=True)
                ins.then_inc(S("f_int"), 1)
                e.wait_ge(S("fused"), 1)
                for r in range(2):
                    ctx_layer(2 + r, IQ, BQD[:, r, :], P, [("kv_free", r + 1)])
                    e.wait_ge(S("bev"), (3 + r) * NM)
                    for j in range(KT):
                        rr = rows_of(j)
                        ins = e.matmul(PS[0:rr, j // 8, (j % 8) * HD:(j % 8 + 1) * HD], IQ[:, j * P:j * P + rr],
                                       BQ[:, 384 + 64 * r:448 + 64 * r], start=True, stop=True)
                    ins.then_inc(S("vt_ps"), 1)
                    e.wait_ge(S("vt_ev"), r + 1)
                    if r:
                        e.wait_ge(S("fused_upd"), 1)
                    for h in range(2):
                        ins = e.matmul(bank(h), DUP, XT[:, h * HALF:(h + 1) * HALF], start=True, stop=True)
                    ins.then_inc(S("f2_ps"), 1)
                    e.wait_ge(S("kv_split"), r + 1)
                    e.wait_ge(S("q_split"), PAIRS + r + 1)
                    max_scores(PAIRS * 2 * NT * NM + r * NT * NM, 1)
                    e.wait_ge(S("negm"), PAIRS + r + 1)
                    shift_row(0, HD, 0).then_inc(S("shift_ps"), 1)
                    e.wait_ge(S("shift"), PAIRS + r + 1)
                    e.wait_ge(S("v2"), r + 1)

                    def operands(u, side):
                        q = slice(side * HALF, (side + 1) * HALF)
                        return KA[0], KB[0], QA[0][:, q], QB[0][:, q], lambda r_, j: V2[0:r_, j, :]
                    attend(PAIRS * 2 * KT + r * KT, 1, operands, 0)
                e.wait_ge(S("quant"), 5)
                e.wait_ge(S("on"), 2 * PAIRS + 2)
                for b in range(4):
                    for h in range(2):
                        e.matmul(bank(2 * b + h), BQ[:, 512 + b * P:512 + (b + 1) * P],
                                 FQ[:, h * HALF:(h + 1) * HALF], start=True, stop=False)
                        ins = e.matmul(bank(2 * b + h), BQ[:, 512 + FFN + b * P:512 + FFN + (b + 1) * P], AQ,
                                       start=False, stop=True)
                    ins.then_inc(S("h1_ps"), 1)
                e.wait_ge(S("quant"), 6)
                for t in range(NT):
                    for b in range(4):
                        ins = e.matmul(PS[:, t // 4, (t % 4) * P:(t % 4 + 1) * P], HBQ[b][:, t * P:(t + 1) * P],
                                       BQ[:, 1536 + b * P:1536 + (b + 1) * P], start=(b == 0), stop=(b == 3))
                ins.then_inc(S("f2o_ps"), 1)
                to_fm(4, 0, 5)
            if last >= 6:
                e.wait_ge(S("x_fm"), 4)
                e.wait_ge(S("ld_lr"), 32)
                e.matmul(PS[0:1, 2, 0:RE], XT[:, 0:1], sm("w_r"), start=True, stop=True).then_inc(S("gl_ps"), 1)
                e.wait_ge(S("g_row"), 1)
                for b in range(4):
                    ins = e.matmul(PS[:, 7, b:b + 1], GX[:, b * P:(b + 1) * P], ones[0:1, 0:1], start=True, stop=True)
                ins.then_inc(S("gc_ps"), 1)
                for b in range(4):
                    if b >= 2:
                        e.wait_ge(S("mid"), b - 1)
                    for h in range(2):
                        ins = e.matmul(bank(2 * (b % 2) + h), LA[:, b * P:(b + 1) * P], XT[:, h * HALF:(h + 1) * HALF],
                                       start=True, stop=True)
                    ins.then_inc(S("mid_ps"), 1)
                e.wait_ge(S("mid"), 4)
                for t in range(NT):
                    for b in range(4):
                        ins = e.matmul(PS[:, 5 + t // 4, (t % 4) * P:(t % 4 + 1) * P], MID[b][:, t * P:(t + 1) * P],
                                       LB[:, b, :], start=(b == 0), stop=(b == 3))
                ins.then_inc(S("lr_ps"), 1)


def kernel(**inputs):
    import numpy as np
    import concourse.bacc as bacc
    from concourse.bass_utils import run_bass_kernel_spmd

    v = {k: np.asarray(a) for k, a in inputs.items()}

    def rows(a):
        a = a.reshape(1, -1)
        return np.broadcast_to(a, (P, a.shape[1]))

    def col(a):
        return a.reshape(-1, P).T

    x = v["x"][0]
    ctx = v["ctx_768"][0]
    parts = {
        "qk_w": rows(np.concatenate([v["L0_attn_qn_w"], v["L0_attn_kn_w"]])),
        "b_out": rows(v["L0_attn_b_out"]), "bo": rows(v["L0_xattn_bo"]),
        "gate_w": v["L0_ffn_gate_w"].T, "gate_b": rows(v["L0_ffn_gate_bias"]),
        "rot": np.repeat(v["L1_attn_rot_w"].reshape(3, D // 2, 2).transpose(1, 0, 2).reshape(D // 2, 6), 2, axis=0),
        "sb": rows(np.concatenate([v["L1_attn_scale"].reshape(1), v["L1_attn_bias"].reshape(1)])),
        "b_d2v": col(v["L1_xattn_b_d2v"]), "b_img": col(v["L1_xattn_b_img"]), "b_txt": col(v["L1_xattn_b_txt"]),
        "b_att0": col(np.tile(v["L1_xattn_b_att0"], 2)), "b_att1": col(np.tile(v["L1_xattn_b_att1"], 2)),
        "b_f1": col(v["L1_xattn_b_f1"]), "b_f2": rows(v["L1_xattn_b_f2"]),
        "b_att0_row": rows(v["L1_xattn_b_att0"]), "b_att1_row": rows(v["L1_xattn_b_att1"]),
        "w_r": v["L1_ffn_Wr"].T, "w_out": v["L0_attn_W_out"], "w_qkv": v["L0_attn_W_qkv"],
    }
    small = np.concatenate([parts[n] for n in SMALL], axis=1)
    pair_w = np.zeros((PAIRS, P, 4, P), np.float32)
    for i, n in enumerate(("Wq", "Wk", "Wv")):
        w = v["L0_xattn_" + n]
        pair_w[:, :w.shape[0], i, :] = w.reshape(w.shape[0], PAIRS, P).transpose(1, 0, 2)
    pair_w[:, :, 3, :] = v["L0_xattn_Wo"].reshape(PAIRS, P, D)
    moe_w = np.stack([v["L0_ffn_Wg"].reshape(BLK, P, D).transpose(0, 2, 1),
                      v["L0_ffn_Wu"].reshape(BLK, P, D).transpose(0, 2, 1),
                      v["L0_ffn_Wd"].transpose(0, 2, 1).reshape(BLK, P, D)], axis=2)
    sh_gu = np.stack([v["L0_ffn_Sg"].reshape(2, EI, D).transpose(0, 2, 1),
                      v["L0_ffn_Su"].reshape(2, EI, D).transpose(0, 2, 1)], axis=2)
    sh_d = v["L0_ffn_Sd"].T.reshape(2, EI, D)
    bit_w = np.zeros((P, NBIT), np.float32)
    for n in ("d2v", "img", "txt", "att0", "att1"):
        w = v["L1_xattn_W_" + n].T
        bit_w[:w.shape[0], BIT[n][0]:BIT[n][0] + w.shape[1]] = w
    for n in ("f1", "f2"):
        w = v["L1_xattn_W_" + n].T
        bit_w[:, BIT[n][0]:BIT[n][0] + BIT[n][1]] = w.reshape(-1, P, w.shape[1]).transpose(1, 0, 2).reshape(P, -1)
    named = {
        "x_tm": x, "x_fm": x.T, "ctx_fm": ctx.T, "small": small, "pair_w": pair_w, "moe_w": moe_w, "sh_gu": sh_gu,
        "sh_d": sh_d, "bit_w": bit_w, "lr_a": v["L1_ffn_A"].reshape(RE * RR, D).T,
        "lr_b": v["L1_ffn_Bw"].transpose(0, 2, 1).reshape(RE * RR, D),
    }
    nc = bacc.Bacc("TRN2", target_bir_lowering=False, num_devices=1)
    arrays, args = {}, {}
    for n, a in named.items():
        a = np.ascontiguousarray(a)
        arrays[f"in_{n}_dram"] = a
        args[n] = nc.dram_tensor(f"in_{n}_dram", a.shape, mybir.dt.from_np(a.dtype), kind="ExternalInput").ap()
    args["out"] = nc.dram_tensor("out_0_dram", (1, T, D), F32, kind="ExternalOutput").ap()
    build_decoder(nc, **args)
    r = run_bass_kernel_spmd(nc, [arrays], core_ids=[0])
    return r.results[0]["out_0_dram"]
```

```python
from contextlib import ExitStack

import concourse.bass as bass
from concourse import mybir

P = 128
T = 1024
NT = T // P
D = 128
HALF = 512
NC = 6404
DC = 96
KT = -(-NC // P)
TAIL = NC - (KT - 1) * P
HD = 64
HEADS0 = 8
PAIRS = HEADS0 // 2
L0H = 16
L0D = D // L0H
E = 64
EI = 88
NG = 8
GE = E // NG
BLK = E * EI // P
RE = 8
RR = 64
FFN = 512
LN_EPS = 1e-5
RMS_EPS = 1e-6
DEN_EPS = 1e-6
ROUTED_SCALE = 2.5
MAGIC = 12582912.0
NEG = -3.0e38
KW = 1024
KCH = [(c, min(KW, NC - c)) for c in range(0, NC, KW)]
NKC = len(KCH)
VG = [list(range(g, min(g + 4, KT))) for g in range(0, KT, 4)]
NVG = len(VG)
MW = 2048
MCH = [(c, min(MW, NC - c)) for c in range(0, NC, MW)]
NM = len(MCH)
FULLS = NC // KW
KIND = "AAAAAA"
assert len(KIND) == FULLS and KIND[0] == "A"
NA = KIND.count("A")
PARTS = []
for _h in range(2):
    for _t in range(NT):
        PARTS += [("full", _h, _t, _k) for _k in range(FULLS)]
        if _t % 2:
            PARTS.append(("rest", _h, _t - 1, 0))
NX = len(PARTS)
ALONE = "AAAVAA"
NAA = ALONE.count("A")
PARTS1 = PARTS[:NX // 2]
ENGINE1 = [ALONE[k] if kind == "full" else "V" for kind, _, _, k in PARTS1]


def parts_on(engine, m):
    full, some = divmod(m, NX // 2)
    return full * ENGINE1.count(engine) + ENGINE1[:some].count(engine)


EXTRAS = [("q",)] + [("k", c) for c in range(NKC)] + [("part", m) for m in range(NX)]


def extras_of(g):
    n = len(EXTRAS)
    return EXTRAS[g * n // (2 * KT):(g + 1) * n // (2 * KT)]

F32 = mybir.dt.float32
F16 = mybir.dt.float16
BF16 = mybir.dt.bfloat16
ALU = mybir.AluOpType
ACT = mybir.ActivationFunctionType
X = mybir.AxisListType.X
RED = bass.bass_isa.ReduceOp

SMALL = {}
_at = 0
for _n, _w in [("qk_w", 2 * D), ("b_out", D), ("bo", D), ("gate_w", E), ("gate_b", E), ("rot", 6), ("sb", 2),
               ("b_d2v", 1), ("b_img", 1), ("b_txt", 1), ("b_att0", 1), ("b_att1", 1), ("b_f1", FFN // P),
               ("b_f2", D), ("b_att0_row", HD), ("b_att1_row", HD), ("w_r", RE), ("w_out", D), ("w_qkv", 3 * D)]:
    SMALL[_n] = (_at, _at + _w)
    _at += _w
NSMALL = _at
BIT = {"d2v": (0, 128, DC, DC * 128), "img": (128, 128, 128, 128 * 128), "txt": (256, 128, 128, 128 * 128),
       "att0": (384, 64, 128, 64 * 128), "att1": (448, 64, 128, 64 * 128),
       "f1": (512, 2 * FFN, 128, 2 * D * FFN), "f2": (1536, 4 * D, 128, D * FFN)}
BIT_N = list(BIT)
NBIT = 2048


def rows_of(j):
    return P if j < KT - 1 else TAIL


def build_decoder(nc, x_tm, x_fm, ctx_fm, small, pair_w, moe_w, sh_gu, sh_d, bit_w, lr_a, lr_b, out, last=6):
    with ExitStack() as ctx:
        def sb(name, shape, dt=F32):
            return ctx.enter_context(nc.sbuf_tensor(name, shape, dt))

        def sem(name):
            return ctx.enter_context(nc.semaphore(name))

        PS = ctx.enter_context(nc.psum_tensor("PS", [P, 8, HALF], F32))

        CTX = sb("CTX", [DC, NC])
        KA = [sb(f"KA{h}", [P, NC], F16) for h in range(2)]
        KB = [sb(f"KB{h}", [P, NC], F16) for h in range(2)]
        KNB = sb("KNB", [P, 2 * NC], F16)
        KN = [KNB[:, h * NC:(h + 1) * NC] for h in range(2)]
        V = sb("V", [P, KT, P])
        PR = sb("PR", [P, 3, T])
        ACC = sb("ACC", [P, 2, T])
        X_ = sb("X", [P, NT, D])
        R = sb("R", [P, NT, D])
        XT = sb("XT", [P, T])
        QS = sb("QS", [P, T])
        ON = sb("ON", [P, T])
        QA = [sb(f"QA{h}", [P, T], F16) for h in range(2)]
        QB = [sb(f"QB{h}", [P, T], F16) for h in range(2)]
        QN = [sb(f"QN{h}", [P, T], F16) for h in range(2)]
        ME = sb("ME", [P, 2, KW], F16)
        MF = sb("MF", [P, 2, KW], F16)
        SM = sb("SM", [P, NSMALL])
        ident = sb("ident", [P, P])
        ones = sb("ones", [P, P])
        PWQ = sb("PWQ", [P, 2, P])
        PWV = sb("PWV", [P, P])
        PWO = sb("PWO", [P, D])
        LNS = sb("LNS", [P, NT, 6])
        LNM = sb("LNM", [P, NT, 2])
        LNV = sb("LNV", [P, NT])
        LND = sb("LND", [P, NT])
        LNR = sb("LNR", [P, NT])
        MXP = sb("MXP", [P, 2 * NT, NM])
        NEGM = sb("NEGM", [P, 2 * NT])

        def sm(name):
            a, b = SMALL[name]
            return SM[:, a:b]

        BIG = V[:, :, :].rearrange("p a b -> p (a b)")
        KF = [KA[h][:, :].bitcast(F32) for h in range(2)]
        KG = [KB[h][:, :].bitcast(F32) for h in range(2)]

        sems = {}

        def S(name):
            if name not in sems:
                sems[name] = sem(name)
            return sems[name]



        def bank(a, b=None, part=slice(0, P)):
            b = a + 1 if b is None else b
            return PS[part, a:b, :].rearrange("p a b -> p (a b)")

        def MW_(s):
            return BIG[:, s * 384:(s + 1) * 384].rearrange("p (a b) -> p a b", a=3)
        ROUT = 1536
        SEL = KA[0][:, 0:E * EI]
        MH = [KG[0][:, 0:T], KG[0][:, T:2 * T]]
        MS = [KG[1][:, 0:T], KG[1][:, T:2 * T]]
        MU = KA[1][:, 0:2 * T].bitcast(F32)
        RWT = KA[1][:, 2 * T:3 * T]
        RWF = KA[1][:, 3 * T:5 * T].bitcast(F32)
        VA = BIG[:, 0:NT * (D + 1)].rearrange("p (t d) -> p t d", t=NT)
        QK0 = KF[0][:, 0:NT * 2 * D].rearrange("p (t a d) -> p t a d", t=NT, a=2)
        SCR = KF[1][:, 0:2 * NT * D].rearrange("p (n d) -> p n d", d=D)
        SS = LNS[:, :, 0:2]
        MASK = KG[0][:, 0:D]
        KVB = KG[0][:, D:3 * D]
        KVS = KG[0][:, 3 * D:4 * D + 1]
        DEN = KG[1][:, 0:T]
        RMS = KG[1][:, T:T + 2 * NT]
        RMD = KG[1][:, T + 32:T + 32 + 2 * NT]
        RMR = KG[1][:, T + 64:T + 64 + 2 * NT]
        QS2 = KG[1][:, T + 128:2 * T + 128]
        XB = PR[:, 0, :]
        DEN2 = sb("DEN2", [P, HALF])[:, :]
        RW_TM = [None]
        SWAP = BIG[:, 0:D]
        ROT = BIG[:, D:4 * D].rearrange("p (a d) -> p a d", a=3)
        G3 = BIG[:, 512:518].rearrange("p (a b) -> p a b", b=2)
        GQ = BIG[:, 520:526].rearrange("p (a b) -> p a b", b=2)
        GN = BIG[:, 528:531]
        GD = BIG[:, 532:535]
        GR = BIG[:, 536:539]
        HS = BIG[:, 540:544]
        HM = BIG[:, 544:544 + NT]
        HL = BIG[:, 552:552 + NT]
        HLR = BIG[:, 560:560 + NT]
        HI = BIG[:, 568:568 + NT]
        HID = BIG[:, 576:576 + NT]
        HIR = BIG[:, 584:584 + NT]
        HC = BIG[:, 592:592 + NT]
        HNM = BIG[:, 600:600 + NT]
        HQ = KF[0][:, 0:T]
        HK = KF[0][:, T:2 * T]
        HV = KF[1][:, 0:T].rearrange("p (j d) -> p j d", j=NT)
        HP = [PR[:, 0, :], PR[:, 1, :]]
        HPT = [KG[0][:, 0:T].rearrange("p (j d) -> p j d", j=NT),
               KG[0][:, T:2 * T].rearrange("p (j d) -> p j d", j=NT)]
        HO = KG[1][:, 0:T].rearrange("p (j d) -> p j d", j=NT)
        HSQ = KG[1][:, T:2 * T].rearrange("p (j d) -> p j d", j=NT)
        BW = ACC[:, :, :].rearrange("p a b -> p (a b)")
        BQ = sb("BQ", [P, NBIT], BF16)
        BQD = sb("BQD", [P, 2, P], BF16)
        BR = sb("BR", [P, 8])
        BT = sb("BT", [P, 8])
        BS = sb("BS", [P, 8])
        BH = sb("BH", [P, 8])
        BN = sb("BN", [P, 8])
        NQ = 8
        AX = sb("AX", [P, NQ])
        AM = sb("AM", [P, NQ])
        AS = sb("AS", [P, NQ])
        AI = sb("AI", [P, NQ])
        WS = sb("WS", [P, NQ + 2])
        AVG = sb("AVG", [P, 4])
        DUP = sb("DUP", [P, P])[:, :]
        LA = PR[:, 0, 0:4 * P]
        LB = PR[:, 0, 4 * P:8 * P].rearrange("p (a d) -> p a d", a=4)


        CQ = KA[1][0:DC, :].bitcast(BF16)
        VQ = KA[1][:, :].bitcast(BF16)
        IQ = KB[1][:, :].bitcast(BF16)
        KVF = BIG
        V2 = KNB[:, 0:2 * KT * HD].bitcast(F32).rearrange("p (a b) -> p a b", b=HD)
        HB = [BIG[:, b * T:(b + 1) * T] for b in range(4)]
        HBQ = [KA[1][:, b * T:(b + 1) * T].bitcast(BF16) for b in range(4)]
        FQ = KB[1][:, 0:T].bitcast(BF16)
        AQ = KB[1][:, T:T + HALF].bitcast(BF16)
        XQ = KA[0][:, 0:T].bitcast(BF16)
        XF = PR[:, 0, :]
        OO = PR[:, 1, :]
        GC = sb("GC", [P, 4])
        GNM = sb("GNM", [1, 1])[:, :]
        GE_ = sb("GE", [1, RE])[:, :]
        GL0 = sb("GL", [1, RE])[:, :]
        GX = sb("GX", [1, 4 * P])[:, :]
        GT = sb("GT", [1, 64])
        MID = [BIG[:, b * T:(b + 1) * T] for b in range(4)]

        block = ctx.enter_context(nc.Block())

        @block.sync
        def _(q):
            q.dma_start(SM[:, :], small).then_inc(S("ld_small"), 16)
            q.dma_start(XT[:, :], x_fm).then_inc(S("ld_x"), 16)
            q.dma_start(X_[:, :, :], x_tm.rearrange("(t p) d -> p t d", p=P)).then_inc(S("ld_x"), 16)
            q.dma_start(CTX[:, :], ctx_fm).then_inc(S("ld_ctx"), 16)
            if last >= 2:
                def load_qk(p, w):
                    q.dma_start(PWQ[:, :, :], w[:, 0:2, :]).then_inc(S("ld_pwq"), 16)

                def copy_keys(p):
                    q.wait_ge(S("k_lo"), p * NKC + NKC)
                    for h in range(2):
                        hi = slice(0, HD) if h == 0 else slice(HD, P)
                        q.dma_start(KA[h][:, :], KN[h]).then_inc(S("keys"), 16)
                        q.dma_start(KB[h][hi, :], KN[h][hi, :]).then_inc(S("keys"), 16)

                load_qk(0, pair_w[0])
                q.dma_start(PWV[:, :], pair_w[0, :, 2, :]).then_inc(S("ld_pwv"), 16)
                q.dma_start(PWO[:, :], pair_w[0, :, 3, :]).then_inc(S("ld_pwo"), 16)
                copy_keys(0)
                with q.Fori(0, PAIRS - 1) as p:
                    w = pair_w[bass.ds(p + 1, 1)].rearrange("o p a b -> (o p) a b")
                    q.wait_ge(S("k_ps"), p * NKC + NKC)
                    load_qk(p + 1, w)
                    q.wait_ge(S("v_ps"), p * NVG + NVG)
                    q.dma_start(PWV[:, :], w[:, 2, :]).then_inc(S("ld_pwv"), 16)
                    q.wait_ge(S("pv"), p * 2 * KT + 2 * KT)
                    copy_keys(p + 1)
                    q.wait_ge(S("wo_ps"), p + 1)
                    q.dma_start(PWO[:, :], w[:, 3, :]).then_inc(S("ld_pwo"), 16)
            if last >= 3:
                q.wait_ge(S("x_fm"), 2)
                q.wait_ge(S("moe_zero"), 1)
                for h in range(2):
                    q.dma_start(MW_(2 + h)[:, 0:2, 0:EI], sh_gu[h]).then_inc(S(f"ld_w{2 + h}"), 16)
                    q.dma_start(MW_(2 + h)[0:EI, 2, :], sh_d[h]).then_inc(S(f"ld_w{2 + h}"), 16)
                for j in range(4):
                    if j >= 2:
                        q.wait_ge(S("moe_down"), j - 1)
                    q.dma_start(MW_(j)[:, :, :], moe_w[j]).then_inc(S(f"ld_w{j}"), 16)
                with q.Fori(1, BLK // 4) as i:
                    for j in range(4):
                        q.wait_ge(S("moe_down"), 4 * i + (j - 1))
                        q.dma_start(MW_(j)[:, :, :],
                                    moe_w[bass.ds(4 * i + j, 1)].rearrange("o p a b -> (o p) a b")
                                    ).then_inc(S(f"ld_w{j}"), 16)
            if last >= 5:
                q.wait_ge(S("bit_zero"), 1)
                q.dma_start(BW[:, 128:NBIT], bit_w[:, 128:NBIT]).then_inc(S("ld_bit"), 16)
                q.dma_start(BW[0:DC, 0:128], bit_w[0:DC, 0:128]).then_inc(S("ld_bit"), 16)
            if last >= 6:
                q.wait_ge(S("ln_x"), 5)
                q.dma_start(LA, lr_a).then_inc(S("ld_lr"), 16)
                q.dma_start(LB, lr_b.rearrange("(a p) d -> p a d", p=P)).then_inc(S("ld_lr"), 16)
            q.wait_ge(S("ln_x"), last)
            q.dma_start(out.rearrange("o (t p) d -> p (o t) d", p=P), X_[:, :, :]).then_inc(S("stored"), 16)
            q.wait_ge(S("stored"), 16)

        @block.gpsimd
        def _(e):
            n = [0]

            def link(ins):
                n[0] += 1
                ins.then_inc(S("pool_step"), 1)
                e.wait_ge(S("pool_step"), n[0])

            def diag(ap, base, fill=1.0, pattern=None, mult=1):
                link(e.affine_select(out=ap, in_=ap, compare_op=ALU.not_equal, fill=fill, base=base,
                                     pattern=pattern or [[-1, P]], channel_multiplier=mult))

            link(e.memset(ident[:, :], 0.0))
            diag(ident[:, :], 0)
            link(e.memset(ones[:, :], 1.0))
            link(e.memset(MASK, 1.0))
            m3 = MASK.rearrange("p (a b) -> p a b", b=L0D)
            link(e.affine_select(out=m3, in_=m3, compare_op=ALU.is_ge, fill=0.0, base=0,
                                 pattern=[[-L0D, L0H], [0, L0D]], channel_multiplier=1))
            link(e.affine_select(out=m3, in_=m3, compare_op=ALU.is_ge, fill=0.0, base=L0D - 1,
                                 pattern=[[L0D, L0H], [0, L0D]], channel_multiplier=-1))
            link(e.memset(VA[:, :, D:D + 1], 1.0))
            e.sem_inc(S("consts"), 1)

            if last >= 2:
                e.wait_ge(S("x_fm"), 1)
                for h in range(2):
                    lo = slice(HD, P) if h == 0 else slice(0, HD)
                    link(e.memset(KB[h][lo, :], 0.0))
                    link(e.memset(KB[h][lo.start:lo.start + 1, :], 1.0))
                    link(e.memset(QB[h][lo, :], 0.0))
                e.sem_inc(S("shift_rows"), 1)
            if last >= 3:
                e.wait_ge(S("ln_x"), 2)
                sv = SEL.rearrange("p (e i) -> p e i", i=EI)
                link(e.memset(SEL, 0.0))
                for base in (0, -E):
                    diag(sv, base, pattern=[[-1, E], [0, EI]])
                link(e.memset(BIG[:, 2 * 384:4 * 384], 0.0))
                e.sem_inc(S("moe_zero"), 1)
            if last >= 4:
                e.wait_ge(S("ln_x"), 3)
                link(e.memset(SWAP, 0.0))
                w3 = SWAP.rearrange("p (a b) -> p a b", b=2)
                diag(w3[:, :, 1], 0, 1.0, [[-2, D // 2]])
                diag(w3[:, :, 0], -1, -1.0, [[-2, D // 2]])
                e.sem_inc(S("swap"), 1)
            if last >= 5:
                e.wait_ge(S("ln_x"), 4)
                link(e.memset(DUP, 0.0))
                for base in (0, HD, -HD):
                    diag(DUP, base)
                link(e.memset(AX[:, :], 0.0))
                link(e.memset(BW[:, 0:128], 0.0))
                link(e.memset(KB[0][HD:P, :], 0.0))
                link(e.memset(KB[0][HD:HD + 1, :], 1.0))
                link(e.memset(QB[0][HD:P, :], 0.0))
                e.sem_inc(S("bit_zero"), 1)
                e.wait_ge(S("bit_rows"), 1)
                e.partition_all_reduce(BT[:, 0:7], BR[:, 0:7], P, RED.add).then_inc(S("bit_sum"), 1)
                for i in range(6):
                    e.wait_ge(S("ax"), i + 1)
                    e.partition_all_reduce(AM[:, i:i + 1], AX[:, i:i + 1], P, RED.max).then_inc(S("am"), 1)

        @block.scalar
        def _(e):
            n = [0]

            def link(ins):
                n[0] += 1
                ins.then_inc(S("act_step"), 1)
                e.wait_ge(S("act_step"), n[0])

            def ln(k):
                e.wait_ge(S("ln_var"), k)
                e.activation(LND[:, :], LNV[:, :], ACT.Sqrt).then_inc(S("ln_sd"), 1)

            def to_fm(k, a):
                e.wait_ge(S("xt_ps"), k)
                e.activation(XT[:, :], bank(a, a + 2), ACT.Copy).then_inc(S("x_fm"), 1)

            for t in range(NT):
                e.wait_ge(S("qkv"), t + 1)
                for a in range(2):
                    e.activation(SCR[:, 2 * t + a, :], PS[:, t, a * D:(a + 1) * D], ACT.Square,
                                 accum_out=SS[:, t, a:a + 1])
                e.wait_ge(S("consts"), 1)
                e.activation(VA[:, t, 0:D], PS[:, t, 2 * D:3 * D], ACT.Copy).then_inc(S("v0"), 1)
            e.wait_ge(S("rms"), 1)
            e.activation(RMD, RMS, ACT.Sqrt).then_inc(S("rms_sd"), 1)
            e.wait_ge(S("q0_t"), 1)
            e.activation(QS[:, :], bank(1, 3), ACT.Copy).then_inc(S("q0_fm"), 1)
            ln(1)
            to_fm(1, 0)

            def copy_out(base, obase, u):
                e.wait_ge(S("pv"), base + KT * (u + 1))
                e.activation(ON[:, u * HALF:(u + 1) * HALF], bank(4), ACT.Copy).then_inc(S("o_ev"), 1)

            def exps(base, units, obase, extra=None):
                for g in range(units * KT):
                    r = rows_of(g % KT)
                    e.wait_ge(S("scores"), base + g + 1)
                    if g >= 3:
                        e.wait_ge(S("pv"), base + g - 2)
                        e.wait_ge(S("acc"), base + g - 2)
                    e.activation(PR[0:r, g % 3, :], bank(2 * (g % 2), 2 * (g % 2) + 2, slice(0, r)),
                                 ACT.Exp).then_inc(S("exp"), 1)
                    if g == KT:
                        copy_out(base, obase, 0)
                    for x in extras_of(g) if extra else ():
                        extra(x)
                copy_out(base, obase, units - 1)

            def q_out(p, b):
                e.wait_ge(S("q_ps"), p + 1)
                e.activation(QS[:, :], bank(b, b + 2), ACT.Copy, scale=HD ** -0.5).then_inc(S("q_ev"), 1)

            def k_out(p, c, b):
                a, w = KCH[c]
                e.wait_ge(S("k_ps"), p * NKC + c + 1)
                e.activation(KN[0][0:HD, a:a + w], bank(b, b + 2, slice(0, HD))[:, 0:w], ACT.Copy)
                e.activation(KN[1][HD:P, a:a + w], bank(b, b + 2, slice(HD, P))[:, 0:w],
                             ACT.Copy).then_inc(S("k_hi"), 1)

            def max_copies(first, heads):
                for h in range(heads):
                    for x, (kind, _, t, k) in enumerate(PARTS1):
                        if kind == "rest" or ALONE[k] != "A":
                            continue
                        m, i = (first + h) * len(PARTS1) + x, (first + h) * NT + t
                        n = ALONE[:k].count("A")
                        e.wait_ge(S("alone_ps"), m + 1)
                        if n == 0:
                            if i >= 2:
                                e.wait_ge(S("alone_tile"), i - 1)
                            dst = ME[:, i % 2, :]
                        else:
                            f = i * (NAA - 1) + n - 1
                            if f >= 2:
                                e.wait_ge(S("alone_merged"), f - 1)
                            dst = MF[:, f % 2, :]
                        e.activation(dst, bank(2 * (m % 4), 2 * (m % 4) + 2), ACT.Copy).then_inc(S("alone_A"), 1)

            def preparation(p):
                def piece(x):
                    if x[0] == "q":
                        q_out(p + 1, 6)
                    elif x[0] == "k":
                        k_out(p + 1, x[1], 6)
                    else:
                        m = x[1]
                        kind, h, t, k = PARTS[m]
                        if kind == "rest" or KIND[k] != "A":
                            return
                        i = h * NT + t
                        n = KIND[:k].count("A")
                        e.wait_ge(S("part_ps"), p * NX + (m + 1))
                        if n == 0:
                            if i >= 2:
                                e.wait_ge(S("tile_max"), p * 2 * NT + (i - 1))
                            dst = ME[:, i % 2, :]
                        else:
                            f = i * (NA - 1) + n - 1
                            if f >= 2:
                                e.wait_ge(S("merged"), p * 2 * NT * (NA - 1) + (f - 1))
                            dst = MF[:, f % 2, :]
                        e.activation(dst, bank(6, 8), ACT.Copy).then_inc(S("part_out"), 1)
                return piece

            if last >= 2:
                q_out(0, 0)
                for c in range(NKC):
                    k_out(0, c, 2 * ((c + 1) % 2))
                max_copies(0, 2)

                def pair(p, extra):
                    e.wait_ge(S("shift_ps"), p + 1)
                    e.wait_ge(S("shift_rows"), 1)
                    e.activation(QB[0][HD:HD + 1, :], bank(0, 2, slice(HD, HD + 1)), ACT.Copy)
                    e.activation(QB[1][0:1, :], bank(2, 4, slice(0, 1)), ACT.Copy).then_inc(S("shift"), 1)
                    for g in range(NVG):
                        e.wait_ge(S("v_ps"), p * NVG + g + 1)
                        full = [j for j in VG[g] if rows_of(j) == P]
                        ins = e.activation(V[:, full[0]:full[-1] + 1, :], PS[:, 4 + g % 4, 0:P * len(full)].rearrange(
                            "p (a b) -> p a b", b=P), ACT.Copy)
                        if len(full) < len(VG[g]):
                            ins = e.activation(V[0:TAIL, KT - 1, :],
                                               PS[0:TAIL, 4 + g % 4, P * len(full):P * len(full) + P], ACT.Copy)
                        ins.then_inc(S("v_ev"), 1)
                    exps(p * 2 * KT, 2, 2 * p, extra)

                with e.Fori(0, PAIRS - 1) as p:
                    pair(p, preparation(p))
                pair(PAIRS - 1, None)
                ln(2)
                to_fm(2, 0)
            if last >= 3:
                e.wait_ge(S("logits"), 1)
                e.activation(BIG[:, ROUT:ROUT + NT * E], bank(2), ACT.Sigmoid).then_inc(S("sig"), 1)
                e.wait_ge(S("rw_t"), 1)
                e.activation(RWF[0:E, :], bank(2, 4, slice(0, E)), ACT.Copy).then_inc(S("rw_fm"), 1)

                def silu(n, slot):
                    e.wait_ge(S("moe_gate"), n + 1)
                    if not isinstance(n, int) or n >= 2:
                        e.wait_ge(S("moe_h1"), n - 1)
                    e.activation(MS[slot], bank(0, 2), ACT.Silu).then_inc(S("moe_silu"), 1)

                silu(0, 0)
                silu(1, 1)
                with e.Fori(0, BLK // 4) as i:
                    for j in range(4):
                        silu(4 * i + (2 + j), j % 2)
                e.wait_ge(S("moe_down"), BLK + 2)
                e.activation(QS[:, :], bank(6, 8), ACT.Copy).then_inc(S("moe_fm"), 1)
                ln(3)
                to_fm(3, 0)
            if last >= 4:
                e.wait_ge(S("rot_n"), 1)
                e.activation(GD, GN, ACT.Sqrt).then_inc(S("rot_sd"), 1)
                e.wait_ge(S("hq"), 1)
                e.activation(HQ, bank(0, 2), ACT.Copy, scale=HS[:, 0:1])
                e.activation(HK, bank(2, 4), ACT.Copy)
                e.activation(HV.rearrange("p j d -> p (j d)"), bank(4, 6), ACT.Copy).then_inc(S("hqkv"), 1)
                for t in range(NT):
                    b = 2 * (t % 2)
                    e.wait_ge(S("h_max"), t + 1)
                    if t >= 2:
                        e.wait_ge(S("h_pt"), t - 1)
                    e.activation(HP[t % 2], bank(b, b + 2), ACT.Exp, bias=HNM[:, t:t + 1],
                                 accum_out=HL[:, t:t + 1]).then_inc(S("h_exp"), 1)
                    e.wait_ge(S("h_pt"), t + 1)
                    if t >= 2:
                        e.wait_ge(S("h_av"), t - 1)
                    e.activation(HPT[t % 2].rearrange("p j d -> p (j d)"), bank(4, 6),
                                 ACT.Copy).then_inc(S("h_ptc"), 1)
                for t in range(NT):
                    e.wait_ge(S("h_o"), 1)
                    ins = e.activation(HSQ[:, t, :], HO[:, t, :], ACT.Square, accum_out=HI[:, t:t + 1])
                ins.then_inc(S("h_inner"), 1)
                e.wait_ge(S("h_clip"), 1)
                e.activation(HID, HC, ACT.Sqrt).then_inc(S("h_sd"), 1)
                ln(4)
            if last >= 5:
                def scaled(out, a, w, q, bias, name, rows=slice(0, P), func=ACT.Identity):
                    e.activation(out, a, func, scale=WS[rows, q:q + 1], bias=bias).then_inc(S(name), 1)

                for lay, (q, bn) in enumerate((("0", "b_d2v"), ("1", "b_img"))):
                    e.wait_ge(S("ws"), lay + 1)
                    for m, (a, w) in enumerate(MCH):
                        e.wait_ge(S("bp"), lay * NM + m + 1)
                        b = 4 * (m % 2)
                        scaled(BIG[:, a:a + w], bank(b, b + 4)[:, 0:w], w, lay, sm(bn), "bev")
                e.wait_ge(S("f_int"), 1)
                e.wait_ge(S("ws"), 4)
                scaled(XT[:, :], bank(0, 2), T, 3, sm("b_txt"), "fused")
                for r in range(2):
                    e.wait_ge(S("kv_free"), r + 1)
                    for m, (a, w) in enumerate(MCH):
                        e.wait_ge(S("bp"), (2 + r) * NM + m + 1)
                        b = 4 * (m % 2)
                        scaled(KVF[:, a:a + w], bank(b, b + 4)[:, 0:w], w, 2 if r == 0 else 6,
                               sm(f"b_att{r}"), "bev")
                    e.wait_ge(S("vt_ps"), r + 1)
                    e.activation(V2[:, 0:KT - 1, :], bank(0, 7)[:, 0:(KT - 1) * HD].rearrange(
                        "p (a b) -> p a b", b=HD), ACT.Copy, scale=WS[:, (2 if r == 0 else 6):(3 if r == 0 else 7)])
                    e.activation(V2[0:TAIL, KT - 1, :], bank(0, 7, slice(0, TAIL))[:, (KT - 1) * HD:KT * HD],
                                 ACT.Copy, scale=WS[0:TAIL, (2 if r == 0 else 6):(3 if r == 0 else 7)]
                                 ).then_inc(S("vt_ev"), 1)
                    e.wait_ge(S("f2_ps"), r + 1)
                    e.activation(QS[:, :], bank(0, 2), ACT.Copy, scale=D ** -0.5).then_inc(S("f2"), 1)
                    max_copies(2 + r, 1)
                    e.wait_ge(S("shift_ps"), PAIRS + r + 1)
                    e.activation(QB[0][HD:HD + 1, :], bank(0, 2, slice(HD, HD + 1)),
                                 ACT.Copy).then_inc(S("shift"), 1)
                    exps(PAIRS * 2 * KT + r * KT, 1, 2 * PAIRS + r)
                for b in range(4):
                    e.wait_ge(S("h1_ps"), b + 1)
                    e.wait_ge(S("ws"), 5)
                    scaled(HB[b], bank(2 * b, 2 * b + 2), T, 4, SM[:, SMALL["b_f1"][0] + b:SMALL["b_f1"][0] + b + 1],
                           "hb", func=ACT.Relu)
                e.wait_ge(S("f2o_ps"), 1)
                e.activation(QS[:, :], bank(0, 2), ACT.Copy, scale=WS[:, 5:6]).then_inc(S("f2o"), 1)
                ln(5)
                to_fm(4, 0)
            if last >= 6:
                e.wait_ge(S("g_max"), 1)
                e.activation(GE_, GL0, ACT.Exp, bias=GNM).then_inc(S("g_exp"), 1)
                for b in range(4):
                    e.wait_ge(S("mid_ps"), b + 1)
                    e.wait_ge(S("g_col"), 1)
                    e.activation(MID[b], bank(2 * (b % 2), 2 * (b % 2) + 2), ACT.Copy,
                                 scale=GC[:, b:b + 1]).then_inc(S("mid"), 1)
                ln(6)

        @block.vector
        def _(e):
            n = [0]

            def link(ins):
                n[0] += 1
                ins.then_inc(S("dve_step"), 1)
                e.wait_ge(S("dve_step"), n[0])

            def ln(k):
                for t in range(NT):
                    ins = e.bn_stats(LNS[:, t, :], R[:, t, :])
                link(ins)
                for t in range(NT):
                    ins = e.bn_aggr(LNM[:, t, :], LNS[:, t, :])
                link(ins)
                e.tensor_scalar(LNV[:, :], LNM[:, :, 1], LN_EPS, None, ALU.add).then_inc(S("ln_var"), 1)
                e.wait_ge(S("ln_sd"), k)
                link(e.reciprocal(LNR[:, :], LND[:, :]))
                for t in range(NT):
                    ins = e.tensor_scalar(X_[:, t, :], R[:, t, :], LNM[:, t, 0:1], LNR[:, t:t + 1],
                                          ALU.subtract, ALU.mult)
                ins.then_inc(S("ln_x"), 1)
                e.wait_ge(S("ln_x"), k)

            def over_tiles(row, tiles=NT):
                return row.unsqueeze(1).to_broadcast([P, tiles, row.shape[-1]])

            x2 = X_[:, :, :].rearrange("p t d -> p (t d)")
            r2 = R[:, :, :].rearrange("p t d -> p (t d)")

            e.wait_ge(S("ld_small"), 16)
            e.wait_ge(S("ld_x"), 32)
            link(e.tensor_tensor(XB.rearrange("p (t d) -> p t d", t=NT), X_[:, :, :], over_tiles(sm("b_out")),
                                 ALU.add))
            e.wait_ge(S("v0"), NT)
            e.tensor_scalar(RMS.rearrange("p (t a) -> p t a", a=2), SS, 1.0 / D, RMS_EPS, ALU.mult,
                            ALU.add).then_inc(S("rms"), 1)
            e.wait_ge(S("rms_sd"), 1)
            link(e.reciprocal(RMR, RMD))
            w = sm("qk_w")
            for t in range(NT):
                for a in range(2):
                    ins = e.scalar_tensor_tensor(QK0[:, t, a, :], PS[:, t, a * D:(a + 1) * D],
                                                 RMR[:, 2 * t + a:2 * t + a + 1], w[:, a * D:(a + 1) * D],
                                                 ALU.mult, ALU.mult)
            link(ins)
            qk_all = QK0.rearrange("p t a d -> p (t a d)")
            e.tensor_scalar(qk_all, qk_all, 0.0, None, ALU.max).then_inc(S("qk0"), 1)
            e.wait_ge(S("kv0"), 1)
            e.wait_ge(S("consts"), 1)
            link(e.tensor_copy(KVS, bank(0)[:, 0:D + 1]))
            link(e.tensor_tensor(KVB[:, 0:D], KVS[:, 0:D], MASK, ALU.mult))
            e.tensor_scalar(KVB[:, D:2 * D], MASK, KVS[:, D:D + 1], None, ALU.mult).then_inc(S("kvb"), 1)
            e.wait_ge(S("o0"), 1)
            link(e.tensor_scalar(DEN, bank(5, 7), DEN_EPS, None, ALU.add))
            link(e.reciprocal(QS2, DEN))
            e.tensor_tensor(ON[:, :], bank(3, 5), QS2, ALU.mult).then_inc(S("on0"), 1)
            e.wait_ge(S("wo0"), 1)
            link(e.tensor_tensor(r2, bank(1, 3), XB, ALU.add))
            ln(1)

            def split_lo(out, full, hi):
                return e.tensor_tensor(out, full, hi, ALU.subtract)

            def maxima(first, heads):
                nv = ALONE.count("V")
                for h in range(heads):
                    for x, (kind, _, t, k) in enumerate(PARTS1):
                        m = (first + h) * len(PARTS1) + x
                        row, i = h * NT + t, (first + h) * NT + t
                        if kind == "rest":
                            e.wait_ge(S("alone_ps"), m + 1)
                            e.tensor_reduce(MXP[:, row:row + 2, nv + 1], PS[:, 2 * (m % 4):2 * (m % 4) + 2, 0:NC - FULLS * KW],
                                            X, ALU.max).then_inc(S("alone_V"), 1)
                        elif ALONE[k] == "V":
                            e.wait_ge(S("alone_ps"), m + 1)
                            c = 1 + ALONE[:k].count("V")
                            e.tensor_reduce(MXP[:, row, c:c + 1], bank(2 * (m % 4), 2 * (m % 4) + 2), X,
                                            ALU.max).then_inc(S("alone_V"), 1)
                        elif k:
                            f = i * (NAA - 1) + ALONE[:k].count("A") - 1
                            e.wait_ge(S("alone_A"), parts_on("A", m + 1))
                            if ALONE[:k].count("A") > 1:
                                e.wait_ge(S("alone_merged"), f)
                            e.tensor_tensor(ME[:, i % 2, :], ME[:, i % 2, :], MF[:, f % 2, :],
                                            ALU.max).then_inc(S("alone_merged"), 1)
                        if kind == "full" and k == ALONE.rindex("A"):
                            e.wait_ge(S("alone_merged"), (i + 1) * (NAA - 1))
                            e.tensor_reduce(MXP[:, row, 0:1], ME[:, i % 2, :], X, ALU.max).then_inc(S("alone_tile"), 1)
                e.wait_ge(S("alone_V"), parts_on("V", (first + heads) * len(PARTS1)))
                e.wait_ge(S("alone_tile"), (first + heads) * NT)
                e.tensor_reduce(NEGM[:, 0:heads * NT], MXP[:, 0:heads * NT, 0:nv + 2], X, ALU.max,
                                negate=True).then_inc(S("negm"), 1)

            def normalize(obase, u):
                e.wait_ge(S("den_ps"), obase + u + 1)
                e.reciprocal(DEN2, bank(5)).then_inc(S("den_r"), 1)
                e.wait_ge(S("den_r"), obase + u + 1)
                e.wait_ge(S("o_ev"), obase + u + 1)
                part = ON[:, u * HALF:(u + 1) * HALF]
                e.tensor_tensor(part, part, DEN2, ALU.mult).then_inc(S("on"), 1)

            def sums(base, units, obase, extra=None):
                for g in range(units * KT):
                    u, j = divmod(g, KT)
                    r = rows_of(j)
                    e.wait_ge(S("exp"), base + g + 1)
                    if j == 0:
                        ins = e.tensor_copy(ACC[:, u, :], PR[:, g % 3, :])
                    else:
                        e.wait_ge(S("acc"), base + g)
                        ins = e.tensor_tensor(ACC[0:r, u, :], ACC[0:r, u, :], PR[0:r, g % 3, :], ALU.add)
                    ins.then_inc(S("acc"), 1)
                    if g == KT + 4:
                        normalize(obase, 0)
                    for x in extras_of(g) if extra else ():
                        extra(x)
                normalize(obase, units - 1)

            def q_parts(p):
                e.wait_ge(S("q_ev"), p + 1)
                e.tensor_copy(QN[0][0:HD, :], QS[0:HD, :])
                e.tensor_copy(QN[0][HD:P, :], QS[0:HD, :])
                e.tensor_copy(QN[1][0:HD, :], QS[HD:P, :])
                e.tensor_copy(QN[1][HD:P, :], QS[HD:P, :]).then_inc(S("q_hi"), 1)

            def k_parts(p, c, b):
                a, w = KCH[c]
                e.wait_ge(S("k_hi"), p * NKC + c + 1)
                split_lo(KN[0][HD:P, a:a + w], bank(b, b + 2, slice(0, HD))[:, 0:w], KN[0][0:HD, a:a + w])
                split_lo(KN[1][0:HD, a:a + w], bank(b, b + 2, slice(HD, P))[:, 0:w],
                         KN[1][HD:P, a:a + w]).then_inc(S("k_lo"), 1)

            def preparation(p):
                def piece(x):
                    if x[0] == "q":
                        return q_parts(p + 1)
                    if x[0] == "k":
                        return k_parts(p + 1, x[1], 6)
                    m = x[1]
                    kind, h, t, k = PARTS[m]
                    i = h * NT + t
                    if kind == "rest":
                        e.wait_ge(S("part_ps"), p * NX + (m + 1))
                        a = FULLS * KW
                        e.tensor_reduce(MXP[:, i:i + 2, NM - 1], PS[:, 6:8, 0:NC - a], X,
                                        ALU.max).then_inc(S("part_out"), 1)
                    elif KIND[k] == "V":
                        e.wait_ge(S("part_ps"), p * NX + (m + 1))
                        c = 1 + KIND[:k].count("V")
                        e.tensor_reduce(MXP[:, i, c:c + 1], bank(6, 8), X, ALU.max).then_inc(S("part_out"), 1)
                    elif k:
                        f = i * (NA - 1) + KIND[:k].count("A") - 1
                        e.wait_ge(S("part_out"), p * NX + (m + 1))
                        if KIND[:k].count("A") > 1:
                            e.wait_ge(S("merged"), p * 2 * NT * (NA - 1) + f)
                        e.tensor_tensor(ME[:, i % 2, :], ME[:, i % 2, :], MF[:, f % 2, :],
                                        ALU.max).then_inc(S("merged"), 1)
                    if kind == "full" and k == KIND.rindex("A"):
                        e.wait_ge(S("merged"), p * 2 * NT * (NA - 1) + (i + 1) * (NA - 1))
                        e.tensor_reduce(MXP[:, i, 0:1], ME[:, i % 2, :], X, ALU.max).then_inc(S("tile_max"), 1)
                    if m == NX - 1:
                        e.wait_ge(S("part_out"), p * NX + NX)
                        e.wait_ge(S("tile_max"), p * 2 * NT + 2 * NT)
                        e.tensor_reduce(NEGM[:, :], MXP[:, :, :], X, ALU.max, negate=True).then_inc(S("negm"), 1)
                return piece

            if last >= 2:
                link(e.tensor_tensor(R[:, :, :], X_[:, :, :], over_tiles(sm("bo")), ALU.add))
                e.wait_ge(S("shift_rows"), 1)
                q_parts(0)
                for c in range(NKC):
                    k_parts(0, c, 2 * ((c + 1) % 2))
                maxima(0, 2)

                def pair(p, extra):
                    e.wait_ge(S("q_hi"), p + 1)
                    e.tensor_copy(QA[0][:, :], QN[0][:, :])
                    e.tensor_copy(QA[1][:, :], QN[1][:, :])
                    split_lo(QB[0][0:HD, :], QS[0:HD, :], QN[0][0:HD, :])
                    split_lo(QB[1][HD:P, :], QS[HD:P, :], QN[1][HD:P, :]).then_inc(S("q_split"), 1)
                    sums(p * 2 * KT, 2, 2 * p, extra)
                    e.wait_ge(S("wo_ps"), p + 1)
                    e.tensor_tensor(r2, r2, bank(0, 2), ALU.add).then_inc(S("r_add"), 1)
                    e.wait_ge(S("r_add"), p + 1)

                with e.Fori(0, PAIRS - 1) as p:
                    pair(p, preparation(p))
                pair(PAIRS - 1, None)
                ln(2)
            if last >= 3:
                at = [ROUT]

                def scratch(width):
                    a = at[0]
                    at[0] += width
                    return BIG[:, a:a + width]

                sig = scratch(NT * E)
                sfc = scratch(NT * E)
                e.wait_ge(S("sig"), 1)
                gb = sm("gate_b").unsqueeze(1).to_broadcast([P, NT, E])
                link(e.tensor_tensor(sfc.rearrange("p (t e) -> p t e", e=E), sig.rearrange("p (t e) -> p t e", e=E),
                                     gb, ALU.add))
                hi, lo = scratch(NT * E // 2), scratch(NT * E // 2)
                v = sfc.rearrange("p (n b) -> p n b", b=2)
                link(e.tensor_tensor(hi, v[:, :, 0], v[:, :, 1], ALU.max))
                link(e.tensor_tensor(lo, v[:, :, 0], v[:, :, 1], ALU.min))
                wdt = NT * E // 2
                while wdt > NT * NG:
                    wdt //= 2
                    nh, nl, t1 = scratch(wdt), scratch(wdt), scratch(wdt)
                    h2, l2 = (z.rearrange("p (n b) -> p n b", b=2) for z in (hi, lo))
                    link(e.tensor_tensor(nh, h2[:, :, 0], h2[:, :, 1], ALU.max))
                    link(e.tensor_tensor(t1, h2[:, :, 0], h2[:, :, 1], ALU.min))
                    link(e.tensor_tensor(nl, l2[:, :, 0], l2[:, :, 1], ALU.max))
                    link(e.tensor_tensor(nl, nl, t1, ALU.max))
                    hi, lo = nh, nl
                gs = scratch(NT * NG)
                link(e.tensor_tensor(gs, hi, lo, ALU.add))
                rank = scratch(NT * NG)
                cmp = scratch(NT * NG)
                g3 = gs.rearrange("p (t g) -> p t g", g=NG)
                k3 = rank.rearrange("p (t g) -> p t g", g=NG)
                c3 = cmp.rearrange("p (t g) -> p t g", g=NG)
                link(e.memset(rank, 0.0))
                for o in range(NG):
                    other = g3[:, :, o:o + 1].to_broadcast([P, NT, NG])
                    if o < NG - 1:
                        link(e.tensor_tensor(c3[:, :, o + 1:NG], other[:, :, o + 1:NG], g3[:, :, o + 1:NG], ALU.is_ge))
                    if o > 0:
                        link(e.tensor_tensor(c3[:, :, 0:o], other[:, :, 0:o], g3[:, :, 0:o], ALU.is_gt))
                    link(e.memset(c3[:, :, o:o + 1], 0.0))
                    link(e.tensor_tensor(rank, rank, cmp, ALU.add))
                link(e.tensor_scalar(cmp, rank, float(NG // 2), None, ALU.is_lt))
                msk = scratch(NT * E)
                link(e.tensor_tensor(msk.rearrange("p (n e) -> p n e", e=GE), sfc.rearrange("p (n e) -> p n e", e=GE),
                                     cmp.unsqueeze(2).to_broadcast([P, NT * NG, GE]), ALU.mult))
                top = scratch(NT * 8)
                rep = scratch(NT * E)
                for t in range(NT):
                    ins = e.max(top[:, 8 * t:8 * t + 8], msk[:, t * E:(t + 1) * E])
                link(ins)
                for t in range(NT):
                    ins = e.match_replace(rep[:, t * E:(t + 1) * E], top[:, 8 * t:8 * t + 8],
                                          msk[:, t * E:(t + 1) * E], NEG)
                link(ins)
                tw = scratch(NT * E)
                link(e.scalar_tensor_tensor(tw, rep, NEG, sig, ALU.is_equal, ALU.mult))
                ts, tr = scratch(NT), scratch(NT)
                link(e.tensor_reduce(ts, tw.rearrange("p (t e) -> p t e", e=E), X, ALU.add))
                link(e.tensor_scalar(ts, ts, 1e-20, None, ALU.add))
                link(e.reciprocal(tr, ts))
                link(e.tensor_scalar(tr, tr, ROUTED_SCALE, None, ALU.mult))
                e.tensor_tensor(rep.rearrange("p (t e) -> p t e", e=E), tw.rearrange("p (t e) -> p t e", e=E),
                                tr.unsqueeze(2).to_broadcast([P, NT, E]), ALU.mult).then_inc(S("rw"), 1)
                RW_TM[0] = rep
                e.wait_ge(S("rw_fm"), 1)
                link(e.tensor_copy(RWT[0:E, :], RWF[0:E, :]))
                split_lo(RWT[E:P, :], RWF[0:E, :], RWT[0:E, :]).then_inc(S("rw_split"), 1)

                def hidden(n, slot, routed):
                    e.wait_ge(S("moe_silu"), n + 1)
                    e.wait_ge(S("moe_up"), n + 1)
                    if not isinstance(n, int) or n >= 1:
                        e.wait_ge(S("moe_h"), n)
                    e.tensor_tensor(MU, bank(2, 4), MS[slot], ALU.mult).then_inc(S("moe_h1"), 1)
                    e.wait_ge(S("moe_h1"), n + 1)
                    if not isinstance(n, int) or n >= 2:
                        e.wait_ge(S("moe_down"), n - 1)
                    if routed:
                        e.wait_ge(S("moe_rw"), n - 1)
                        ins = e.tensor_tensor(MH[slot], bank(4, 6), MU, ALU.mult)
                    else:
                        ins = e.tensor_copy(MH[slot], MU)
                    ins.then_inc(S("moe_h"), 1)

                hidden(0, 0, False)
                hidden(1, 1, False)
                with e.Fori(0, BLK // 4) as i:
                    for j in range(4):
                        hidden(4 * i + (2 + j), j % 2, True)
                e.wait_ge(S("moe_tm"), 1)
                link(e.tensor_tensor(r2, bank(0, 2), x2, ALU.add))
                ln(3)
            if last >= 4:
                e.wait_ge(S("swap"), 1)
                g = sm("rot").rearrange("p (a b) -> p a b", b=2)
                link(e.tensor_tensor(GQ, g, g, ALU.mult))
                e.tensor_reduce(GN, GQ, X, ALU.add).then_inc(S("rot_n"), 1)
                e.wait_ge(S("rot_sd"), 1)
                link(e.reciprocal(GR, GD))
                link(e.tensor_tensor(G3, g, GR.unsqueeze(2).to_broadcast([P, 3, 2]), ALU.mult))
                for a in range(3):
                    link(e.tensor_scalar(ROT[:, a, :], ident[:, :], G3[:, a, 0:1], None, ALU.mult))
                    link(e.scalar_tensor_tensor(ROT[:, a, :], SWAP, G3[:, a, 1:2], ROT[:, a, :], ALU.mult, ALU.add))
                sbv = sm("sb")
                link(e.reciprocal(HS[:, 1:2], sbv[:, 0:1]))
                link(e.tensor_scalar(HS[:, 0:1], HS[:, 1:2], 2.0, None, ALU.mult))
                e.tensor_tensor(HS[:, 2:3], HS[:, 0:1], sbv[:, 1:2], ALU.add).then_inc(S("rot"), 1)
                e.wait_ge(S("rot"), 1)
                for t in range(NT):
                    b = 2 * (t % 2)
                    e.wait_ge(S("h_s"), t + 1)
                    link(e.tensor_reduce(HM[:, t:t + 1], bank(b, b + 2), X, ALU.max))
                    link(e.tensor_scalar(HM[:, t:t + 1], HM[:, t:t + 1], HS[:, 2:3], -1.0, ALU.add, ALU.mult))
                    e.tensor_scalar(HNM[:, t:t + 1], HM[:, t:t + 1], HS[:, 2:3], None,
                                    ALU.add).then_inc(S("h_max"), 1)
                e.wait_ge(S("h_av"), NT)
                e.wait_ge(S("h_exp"), NT)
                link(e.reciprocal(HLR, HL))
                e.tensor_tensor(HO, bank(6, 8).rearrange("p (t d) -> p t d", d=D),
                                HLR.unsqueeze(2).to_broadcast([P, NT, D]), ALU.mult).then_inc(S("h_o"), 1)
                e.wait_ge(S("h_inner"), 1)
                e.tensor_scalar(HC, HI, 1e-8, None, ALU.max).then_inc(S("h_clip"), 1)
                e.wait_ge(S("h_sd"), 1)
                link(e.reciprocal(HIR, HID))
                link(e.tensor_tensor(HO, HO, HIR.unsqueeze(2).to_broadcast([P, NT, D]), ALU.mult))
                link(e.tensor_tensor(R[:, :, :], HO, X_[:, :, :], ALU.add))
                ln(4)
            if last >= 5:
                e.wait_ge(S("ld_bit"), 32)
                for i, nme in enumerate(BIT_N):
                    c, w_, _, _ = BIT[nme]
                    ins = e.tensor_reduce(BR[:, i:i + 1], BW[:, c:c + w_], X, ALU.add, apply_absolute_value=True)
                ins.then_inc(S("bit_rows"), 1)
                e.wait_ge(S("bit_zero"), 1)
                e.tensor_reduce(AX[0:DC, 0:1], CTX[:, :], X, ALU.max, apply_absolute_value=True
                                ).then_inc(S("ax"), 1)
                e.wait_ge(S("bit_sum"), 1)
                for i, nme in enumerate(BIT_N):
                    ins = e.tensor_scalar(BS[:, i:i + 1], BT[:, i:i + 1], 1.0 / BIT[nme][3], 1e-5, ALU.mult, ALU.max)
                link(ins)
                link(e.tensor_scalar(BH[:, 0:7], BS[:, 0:7], 0.5, None, ALU.mult))
                link(e.tensor_scalar(BN[:, 0:7], BS[:, 0:7], -0.5, None, ALU.mult))
                for i, nme in enumerate(BIT_N):
                    c, w_, _, _ = BIT[nme]
                    link(e.tensor_scalar(BQ[:, c:c + w_], BW[:, c:c + w_], BN[:, i:i + 1], None, ALU.is_lt))
                    link(e.scalar_tensor_tensor(BQ[:, c:c + w_], BW[:, c:c + w_], BH[:, i:i + 1], BQ[:, c:c + w_],
                                                ALU.is_gt, ALU.subtract))
                for r in range(2):
                    for a in range(2):
                        ins = e.tensor_copy(BQD[:, r, a * HD:(a + 1) * HD], BQ[:, 384 + 64 * r:448 + 64 * r])
                ins.then_inc(S("bit_q"), 1)

                def scale_of(i, weights):
                    e.wait_ge(S("am"), i + 1)
                    link(e.tensor_scalar(AS[:, i:i + 1], AM[:, i:i + 1], 1e-8, 1.0 / 127.0, ALU.max, ALU.mult))
                    link(e.reciprocal(AI[:, i:i + 1], AS[:, i:i + 1]))
                    for col, nme in weights:
                        k = BIT_N.index(nme)
                        ins = e.tensor_tensor(WS[:, col:col + 1], AS[:, i:i + 1], BS[:, k:k + 1], ALU.mult)
                    ins.then_inc(S("ws"), 1)

                def quantize(dst, src, tmp, i, rows=slice(0, P)):
                    link(e.tensor_scalar(tmp, src, AI[rows, i:i + 1], 127.0, ALU.mult, ALU.min))
                    link(e.tensor_scalar(tmp, tmp, -128.0, MAGIC, ALU.max, ALU.add))
                    return e.tensor_scalar(dst, tmp, MAGIC, None, ALU.subtract)

                scale_of(0, [(0, "d2v")])
                quantize(CQ, CTX[:, :], CTX[:, :], 0, slice(0, DC)).then_inc(S("quant"), 1)
                e.wait_ge(S("bev"), NM)
                e.tensor_reduce(AX[:, 1:2], BIG[:, 0:NC], X, ALU.max, apply_absolute_value=True
                                ).then_inc(S("ax"), 1)
                scale_of(1, [(1, "img")])
                e.wait_ge(S("bp"), NM)
                quantize(VQ, BIG[:, 0:NC], BIG[:, 0:NC], 1).then_inc(S("quant"), 1)
                e.wait_ge(S("bev"), 2 * NM)
                e.tensor_reduce(AX[:, 2:3], BIG[:, 0:NC], X, ALU.max, apply_absolute_value=True
                                ).then_inc(S("ax"), 1)
                link(e.tensor_reduce(AVG[:, 0:1], BIG[:, 0:NC], X, ALU.add))
                link(e.tensor_scalar(AVG[:, 1:2], AVG[:, 0:1], 1.0 / NC, None, ALU.mult))
                scale_of(2, [(2, "att0"), (6, "att1")])
                quantize(IQ, BIG[:, 0:NC], BIG[:, 0:NC], 2).then_inc(S("quant"), 1)
                e.wait_ge(S("quant"), 3)
                e.tensor_reduce(AX[:, 3:4], x2, X, ALU.max, apply_absolute_value=True).then_inc(S("ax"), 1)
                scale_of(3, [(3, "txt")])
                e.wait_ge(S("x4_t"), 1)
                quantize(XQ, bank(0, 2), XF, 3).then_inc(S("quant"), 1)

                for r in range(2):
                    wcol = 2 if r == 0 else 6
                    if r == 0:
                        e.sem_inc(S("kv_free"), 1)
                    e.wait_ge(S("bev"), (3 + r) * NM)
                    link(e.tensor_copy(KA[0][:, :], BIG[:, 0:NC]))
                    link(e.tensor_copy(KB[0][0:HD, :], KA[0][0:HD, :]))
                    link(split_lo(KA[0][HD:P, :], BIG[HD:P, 0:NC], KA[0][HD:P, :]))
                    e.sem_inc(S("kv_split"), 1)
                    e.wait_ge(S("vt_ev"), r + 1)
                    brow = sm(f"b_att{r}_row")
                    link(e.tensor_tensor(V2[:, 0:KT - 1, :], V2[:, 0:KT - 1, :],
                                         brow.unsqueeze(1).to_broadcast([P, KT - 1, HD]), ALU.add))
                    e.tensor_tensor(V2[0:TAIL, KT - 1, :], V2[0:TAIL, KT - 1, :], brow[0:TAIL, :],
                                    ALU.add).then_inc(S("v2"), 1)
                    e.wait_ge(S("f2"), r + 1)
                    link(e.tensor_copy(QA[0][:, :], QS[:, :]))
                    split_lo(QB[0][0:HD, :], QS[0:HD, :], QA[0][0:HD, :]).then_inc(S("q_split"), 1)
                    maxima(2 + r, 1)
                    sums(PAIRS * 2 * KT + r * KT, 1, 2 * PAIRS + r)
                    e.wait_ge(S("on"), 2 * PAIRS + r + 1)
                    for qh in range(2):
                        for fh in range(2):
                            ins = e.tensor_copy(OO[fh * HD:(fh + 1) * HD, qh * HALF:(qh + 1) * HALF],
                                                ON[qh * HD:(qh + 1) * HD, 0:HALF])
                    link(ins)
                    ins = e.scalar_tensor_tensor(XT[:, :], OO, 0.1, XT[:, :], ALU.mult, ALU.add)
                    if r == 0:
                        ins.then_inc(S("kv_free"), 1)
                        e.wait_ge(S("kv_free"), 2)
                    else:
                        link(ins)
                    e.sem_inc(S("fused_upd"), 1)
                link(e.tensor_reduce(AVG[:, 2:3], XT[:, :], X, ALU.max, apply_absolute_value=True))
                link(e.tensor_reduce(AVG[:, 3:4], AVG[:, 1:2], X, ALU.max, apply_absolute_value=True))
                e.tensor_tensor(AX[:, 4:5], AVG[:, 2:3], AVG[:, 3:4], ALU.max).then_inc(S("ax"), 1)
                scale_of(4, [(4, "f1")])
                link(quantize(FQ, XT[:, :], XF, 4))
                link(quantize(AVG[:, 2:3], AVG[:, 1:2], AVG[:, 0:1], 4))
                e.tensor_copy(AQ, AVG[:, 2:3].to_broadcast([P, HALF])).then_inc(S("quant"), 1)
                e.wait_ge(S("hb"), 4)
                e.tensor_reduce(AX[:, 5:6], BIG[:, 0:4 * T], X, ALU.max).then_inc(S("ax"), 1)
                scale_of(5, [(5, "f2")])
                quantize(KA[1][:, 0:4 * T].bitcast(BF16), BIG[:, 0:4 * T], BIG[:, 0:4 * T], 5).then_inc(S("quant"), 1)
                e.wait_ge(S("f2o"), 1)
                link(e.tensor_tensor(R[:, :, :], QS[:, :].rearrange("p (t d) -> p t d", d=D),
                                     over_tiles(sm("b_f2")), ALU.add))
                link(e.tensor_tensor(r2, r2, x2, ALU.add))
                ln(5)
            if last >= 6:
                e.wait_ge(S("gl_ps"), 1)
                link(e.tensor_copy(GL0, PS[0:1, 2, 0:RE]))
                rank, cmp = GT[:, 0:RE], GT[:, RE:2 * RE]
                link(e.memset(rank, 0.0))
                for o in range(RE):
                    other = GL0[:, o:o + 1]
                    if o < RE - 1:
                        link(e.tensor_scalar(cmp[:, o + 1:RE], GL0[:, o + 1:RE], other, None, ALU.is_le))
                    if o > 0:
                        link(e.tensor_scalar(cmp[:, 0:o], GL0[:, 0:o], other, None, ALU.is_lt))
                    link(e.memset(cmp[:, o:o + 1], 0.0))
                    link(e.tensor_tensor(rank, rank, cmp, ALU.add))
                link(e.tensor_scalar(cmp, rank, 2.0, None, ALU.is_lt))
                e.tensor_reduce(GNM, GL0, X, ALU.max, negate=True).then_inc(S("g_max"), 1)
                e.wait_ge(S("g_exp"), 1)
                gm, gsum, grec, gate = GT[:, 16:24], GT[:, 24:25], GT[:, 25:26], GT[:, 32:40]
                link(e.tensor_tensor(gm, GE_, cmp, ALU.mult))
                link(e.tensor_reduce(gsum, gm, X, ALU.add))
                link(e.reciprocal(grec, gsum))
                link(e.tensor_scalar(gate, gm, grec, None, ALU.mult))
                e.tensor_copy(GX.rearrange("p (e r) -> p e r", r=RR),
                              gate.unsqueeze(2).to_broadcast([1, RE, RR])).then_inc(S("g_row"), 1)
                e.wait_ge(S("gc_ps"), 1)
                e.tensor_copy(GC[:, :], PS[:, 7, 0:4]).then_inc(S("g_col"), 1)
                e.wait_ge(S("lr_ps"), 1)
                link(e.scalar_tensor_tensor(r2, x2, 2.0, bank(5, 7), ALU.mult, ALU.add))
                ln(6)

        @block.tensor
        def _(e):
            def transposes(src, a, k, gate=None):
                for t in range(NT):
                    ins = e.transpose(PS[:, a + t // 4, (t % 4) * P:(t % 4 + 1) * P], src[:, t, :], ident[:, :])
                return ins

            def to_fm(k, a, lns):
                e.wait_ge(S("ln_x"), lns)
                transposes(X_, a, k).then_inc(S("xt_ps"), 1)

            e.wait_ge(S("ld_small"), 16)
            e.wait_ge(S("ld_x"), 32)
            for t in range(NT):
                e.matmul(PS[:, t, 0:3 * D], XT[:, t * P:(t + 1) * P], sm("w_qkv"), start=True,
                         stop=True).then_inc(S("qkv"), 1)
            e.wait_ge(S("qk0"), 1)
            e.wait_ge(S("v0"), NT)
            e.wait_ge(S("consts"), 1)
            for t in range(NT):
                ins = e.matmul(PS[:, 0, 0:D + 1], QK0[:, t, 1, :], VA[:, t, :], start=(t == 0), stop=(t == NT - 1))
            ins.then_inc(S("kv0"), 1)
            for t in range(NT):
                ins = e.transpose(PS[:, 1 + t // 4, (t % 4) * P:(t % 4 + 1) * P], QK0[:, t, 0, :], ident[:, :])
            ins.then_inc(S("q0_t"), 1)
            e.wait_ge(S("kvb"), 1)
            e.wait_ge(S("q0_fm"), 1)
            for a in range(2):
                for h in range(2):
                    ins = e.matmul(bank(3 + 2 * a + h), KVB[:, a * D:(a + 1) * D], QS[:, h * HALF:(h + 1) * HALF],
                                   start=True, stop=True)
            ins.then_inc(S("o0"), 1)
            e.wait_ge(S("on0"), 1)
            for t in range(NT):
                ins = e.matmul(PS[:, 1 + t // 4, (t % 4) * P:(t % 4 + 1) * P], ON[:, t * P:(t + 1) * P], sm("w_out"),
                               start=True, stop=True)
            ins.then_inc(S("wo0"), 1)
            to_fm(1, 0, 1)

            def part_scores(part, q, kn, b):
                kind, _, t, k = part
                for i in range(2):
                    if kind == "full":
                        tile, a, w = t, k * KW + i * HALF, HALF
                    else:
                        tile, a, w = t + i, FULLS * KW, NC - FULLS * KW
                    ins = e.matmul(PS[:, b + i, 0:w], q[:, tile * P:(tile + 1) * P], kn[:, a:a + w],
                                   start=True, stop=True)
                return ins

            def max_scores(first, heads, qn, kn):
                for h in range(heads):
                    for i, part in enumerate(PARTS1):
                        m = (first + h) * len(PARTS1) + i
                        if m >= 4:
                            engine = ENGINE1[(m - 4) % len(PARTS1)]
                            e.wait_ge(S("alone_" + engine), parts_on(engine, m - 3))
                        part_scores(part, qn[h], kn[h], 2 * (m % 4)).then_inc(S("alone_ps"), 1)

            def shift_row(h, r, b):
                for t in range(NT):
                    ins = e.matmul(PS[r:r + 1, b + t // 4, (t % 4) * P:(t % 4 + 1) * P],
                                   NEGM[:, h * NT + t:h * NT + t + 1], ident[:, :], start=True, stop=True)
                return ins

            def attend(base, units, operands, obase, extra=None):
                def scores(g):
                    u, j = divmod(g, KT)
                    r = rows_of(j)
                    if g >= 2:
                        e.wait_ge(S("exp"), base + g - 1)
                    for side in range(2):
                        ka, kb, qa, qb, _ = operands(u, side)
                        o = PS[0:r, 2 * (g % 2) + side, :]
                        e.matmul(o, ka[:, j * P:j * P + r], qa, start=True, stop=False)
                        ins = e.matmul(o, kb[:, j * P:j * P + r], qb, start=False, stop=True)
                    ins.then_inc(S("scores"), 1)

                def values(g):
                    u, j = divmod(g, KT)
                    r = rows_of(j)
                    e.wait_ge(S("exp"), base + g + 1)
                    if u and j == 0:
                        e.wait_ge(S("o_ev"), obase + u)
                    for side in range(2):
                        v = operands(u, side)[4]
                        ins = e.matmul(PS[side * HD:(side + 1) * HD, 4, :], v(r, j),
                                       PR[0:r, g % 3, side * HALF:(side + 1) * HALF], start=(j == 0),
                                       stop=(j == KT - 1), skip_group_check=True)
                    ins.then_inc(S("pv"), 1)

                def denominators(u):
                    e.wait_ge(S("acc"), base + KT * (u + 1))
                    if u:
                        e.wait_ge(S("on"), obase + u)
                    for side in range(2):
                        ins = e.matmul(PS[side * HD:(side + 1) * HD, 5, :], ones[:, 0:HD],
                                       ACC[:, u, side * HALF:(side + 1) * HALF], start=True, stop=True)
                    ins.then_inc(S("den_ps"), 1)

                for g in range(units * KT):
                    scores(g)
                    if g:
                        values(g - 1)
                    if g == KT + 2:
                        denominators(0)
                    for x in extras_of(g) if extra else ():
                        extra(x)
                values(units * KT - 1)
                denominators(units - 1)

            def project_q(p, b):
                e.wait_ge(S("ld_pwq"), p * 16 + 16)
                for h in range(2):
                    ins = e.matmul(bank(b + h), PWQ[:, 0, :], XT[:, h * HALF:(h + 1) * HALF], start=True, stop=True)
                ins.then_inc(S("q_ps"), 1)

            def project_k(p, c, b):
                a, w = KCH[c]
                for i in range(-(-w // HALF)):
                    cw = min(HALF, w - i * HALF)
                    ins = e.matmul(PS[:, b + i, 0:cw], PWQ[0:DC, 1, :], CTX[:, a + i * HALF:a + i * HALF + cw],
                                   start=True, stop=True)
                ins.then_inc(S("k_ps"), 1)

            def preparation(p):
                def piece(x):
                    if x[0] == "q":
                        return project_q(p + 1, 6)
                    if x[0] == "k":
                        c = x[1]
                        if c:
                            e.wait_ge(S("k_lo"), p * NKC + (NKC + c))
                        else:
                            e.wait_ge(S("q_ev"), p + 2)
                        return project_k(p + 1, c, 6)
                    m = x[1]
                    kind, h, t, k = PARTS[m]
                    if m:
                        e.wait_ge(S("part_out"), p * NX + m)
                    else:
                        e.wait_ge(S("k_lo"), p * NKC + 2 * NKC)
                        e.wait_ge(S("q_hi"), p + 2)
                    part_scores(PARTS[m], QN[h], KN[h], 6).then_inc(S("part_ps"), 1)
                return piece

            if last >= 2:
                e.wait_ge(S("x_fm"), 1)
                e.wait_ge(S("ld_ctx"), 16)
                project_q(0, 0)
                for c in range(NKC):
                    if c == 1:
                        e.wait_ge(S("q_ev"), 1)
                    if c >= 2:
                        e.wait_ge(S("k_lo"), c - 1)
                    project_k(0, c, 2 * ((c + 1) % 2))
                e.wait_ge(S("k_lo"), NKC)
                e.wait_ge(S("q_hi"), 1)
                max_scores(0, 2, QN, KN)

                def pair(p, extra):
                    e.wait_ge(S("negm"), p + 1)
                    shift_row(0, HD, 0)
                    shift_row(1, 0, 2).then_inc(S("shift_ps"), 1)
                    e.wait_ge(S("ld_pwv"), p * 16 + 16)
                    for g in range(NVG):
                        if g >= 4:
                            e.wait_ge(S("v_ev"), p * NVG + g - 3)
                        for i, j in enumerate(VG[g]):
                            r = rows_of(j)
                            ins = e.matmul(PS[0:r, 4 + g % 4, i * P:(i + 1) * P], CTX[:, j * P:j * P + r],
                                           PWV[0:DC, :], start=True, stop=True)
                        ins.then_inc(S("v_ps"), 1)
                    e.wait_ge(S("v_ev"), p * NVG + NVG)
                    e.wait_ge(S("q_split"), p + 1)
                    e.wait_ge(S("shift"), p + 1)
                    e.wait_ge(S("keys"), p * 64 + 64)
                    e.wait_ge(S("shift_rows"), 1)

                    def operands(u, side):
                        q = slice(u * HALF, (u + 1) * HALF)
                        return (KA[side], KB[side], QA[side][:, q], QB[side][:, q],
                                lambda r, j: V[0:r, j, side * HD:(side + 1) * HD])
                    attend(p * 2 * KT, 2, operands, 2 * p, extra)
                    e.wait_ge(S("on"), 2 * p + 2)
                    e.wait_ge(S("ld_pwo"), p * 16 + 16)
                    for t in range(NT):
                        ins = e.matmul(PS[:, t // 4, (t % 4) * P:(t % 4 + 1) * P], ON[:, t * P:(t + 1) * P],
                                       PWO[:, :], start=True, stop=True)
                    ins.then_inc(S("wo_ps"), 1)
                    e.wait_ge(S("r_add"), p + 1)

                with e.Fori(0, PAIRS - 1) as p:
                    pair(p, preparation(p))
                pair(PAIRS - 1, None)
                to_fm(2, 0, 2)
            if last >= 3:
                e.wait_ge(S("x_fm"), 2)
                for t in range(NT):
                    ins = e.matmul(PS[:, 2, t * E:(t + 1) * E], XT[:, t * P:(t + 1) * P], sm("gate_w"),
                                   start=True, stop=True)
                ins.then_inc(S("logits"), 1)
                e.wait_ge(S("rw"), 1)
                for t in range(NT):
                    ins = e.transpose(PS[0:E, 2 + t // 4, (t % 4) * P:(t % 4 + 1) * P],
                                      RW_TM[0][:, t * E:(t + 1) * E], ident[:, :])
                ins.then_inc(S("rw_t"), 1)
                e.wait_ge(S("rw_split"), 1)
                e.wait_ge(S("moe_zero"), 1)

                def product(b, w_, n, name, ready):
                    for h in range(2):
                        ins = e.matmul(bank(b + h), w_, XT[:, h * HALF:(h + 1) * HALF], start=True, stop=True)
                    ins.then_inc(S(name), 1)

                def expert(n, slot, ld, block_at):
                    e.wait_ge(S(f"ld_w{slot}"), ld)
                    if not isinstance(n, int) or n >= 1:
                        e.wait_ge(S("moe_silu"), n)
                    product(0, MW_(slot)[:, 0, :], n, "moe_gate", None)
                    if not isinstance(n, int) or n >= 1:
                        e.wait_ge(S("moe_h1"), n)
                    product(2, MW_(slot)[:, 1, :], n, "moe_up", None)
                    if block_at is not None:
                        e.wait_ge(S("moe_h"), n)
                        for h in range(2):
                            ins = e.matmul(bank(4 + h), SEL[:, bass.ds(block_at, P)],
                                           RWT[:, h * HALF:(h + 1) * HALF], start=True, stop=True)
                        ins.then_inc(S("moe_rw"), 1)

                def down(n, slot, hslot, first=False, stop=False):
                    e.wait_ge(S("moe_h"), n + 1)
                    for h in range(2):
                        ins = e.matmul(bank(6 + h), MW_(slot)[:, 2, :], MH[hslot][:, h * HALF:(h + 1) * HALF],
                                       start=first, stop=stop, skip_group_check=True)
                    ins.then_inc(S("moe_down"), 1)

                expert(0, 2, 32, None)
                expert(1, 3, 32, None)
                down(0, 2, 0, first=True)
                with e.Fori(0, BLK // 4) as i:
                    for j in range(4):
                        expert(4 * i + (2 + j), j, 16 * i + (48 if j >= 2 else 16), 4 * P * i + j * P)
                        down(4 * i + (1 + j), (j - 1) % 4, (j + 1) % 2)
                down(BLK + 1, 3, 1, stop=True)
                e.wait_ge(S("moe_fm"), 1)
                for t in range(NT):
                    ins = e.transpose(PS[:, t // 4, (t % 4) * P:(t % 4 + 1) * P], QS[:, t * P:(t + 1) * P], ident[:, :])
                ins.then_inc(S("moe_tm"), 1)
                to_fm(3, 0, 3)
            if last >= 4:
                e.wait_ge(S("x_fm"), 3)
                e.wait_ge(S("rot"), 1)
                for a in range(2):
                    for h in range(2):
                        e.matmul(bank(2 * a + h), ROT[:, a, :], XT[:, h * HALF:(h + 1) * HALF], start=True, stop=True)
                for t in range(NT):
                    ins = e.matmul(PS[:, 4 + t // 4, (t % 4) * P:(t % 4 + 1) * P], XT[:, t * P:(t + 1) * P],
                                   ROT[:, 2, :], start=True, stop=True)
                ins.then_inc(S("hq"), 1)
                e.wait_ge(S("hqkv"), 1)

                def h_scores(t):
                    b = 2 * (t % 2)
                    if t >= 2:
                        e.wait_ge(S("h_exp"), t - 1)
                    for h in range(2):
                        ins = e.matmul(bank(b + h), HQ[:, t * P:(t + 1) * P], HK[:, h * HALF:(h + 1) * HALF],
                                       start=True, stop=True)
                    ins.then_inc(S("h_s"), 1)

                h_scores(0)
                for t in range(NT):
                    if t + 1 < NT:
                        h_scores(t + 1)
                    e.wait_ge(S("h_exp"), t + 1)
                    if t:
                        e.wait_ge(S("h_ptc"), t)
                    for j in range(NT):
                        ins = e.transpose(PS[:, 4 + j // 4, (j % 4) * P:(j % 4 + 1) * P], HP[t % 2][:, j * P:(j + 1) * P],
                                          ident[:, :])
                    ins.then_inc(S("h_pt"), 1)
                    e.wait_ge(S("h_ptc"), t + 1)
                    for j in range(NT):
                        ins = e.matmul(PS[:, 6 + t // 4, (t % 4) * P:(t % 4 + 1) * P], HPT[t % 2][:, j, :], HV[:, j, :],
                                       start=(j == 0), stop=(j == NT - 1))
                    ins.then_inc(S("h_av"), 1)
            if last >= 5:
                def ctx_layer(k, rhs, w_, rows, waits):
                    for s_, v_ in waits:
                        e.wait_ge(S(s_), v_)
                    for m, (a, w) in enumerate(MCH):
                        if m >= 2:
                            e.wait_ge(S("bev"), k * NM + m - 1)
                        for i in range(-(-w // HALF)):
                            c = min(HALF, w - i * HALF)
                            ins = e.matmul(PS[:, 4 * (m % 2) + i, 0:c], w_,
                                           rhs[:, a + i * HALF:a + i * HALF + c], start=True, stop=True)
                        ins.then_inc(S("bp"), 1)

                e.wait_ge(S("ln_x"), 4)
                ctx_layer(0, CQ, BQ[0:DC, 0:128], DC, [("bit_q", 1), ("quant", 1)])
                ctx_layer(1, VQ, BQ[:, 128:256], P, [("quant", 2), ("bev", NM)])
                e.wait_ge(S("bev"), 2 * NM)
                transposes(X_, 0, 0).then_inc(S("x4_t"), 1)
                e.wait_ge(S("quant"), 4)
                for h in range(2):
                    ins = e.matmul(bank(h), BQ[:, 256:384], XQ[:, h * HALF:(h + 1) * HALF], start=True, stop=True)
                ins.then_inc(S("f_int"), 1)
                e.wait_ge(S("fused"), 1)
                for r in range(2):
                    ctx_layer(2 + r, IQ, BQD[:, r, :], P, [("kv_free", r + 1)])
                    e.wait_ge(S("bev"), (3 + r) * NM)
                    for j in range(KT):
                        rr = rows_of(j)
                        ins = e.matmul(PS[0:rr, j // 8, (j % 8) * HD:(j % 8 + 1) * HD], IQ[:, j * P:j * P + rr],
                                       BQ[:, 384 + 64 * r:448 + 64 * r], start=True, stop=True)
                    ins.then_inc(S("vt_ps"), 1)
                    e.wait_ge(S("vt_ev"), r + 1)
                    if r:
                        e.wait_ge(S("fused_upd"), 1)
                    for h in range(2):
                        ins = e.matmul(bank(h), DUP, XT[:, h * HALF:(h + 1) * HALF], start=True, stop=True)
                    ins.then_inc(S("f2_ps"), 1)
                    e.wait_ge(S("kv_split"), r + 1)
                    e.wait_ge(S("q_split"), PAIRS + r + 1)
                    max_scores(2 + r, 1, QA, KA)
                    e.wait_ge(S("negm"), PAIRS + r + 1)
                    shift_row(0, HD, 0).then_inc(S("shift_ps"), 1)
                    e.wait_ge(S("shift"), PAIRS + r + 1)
                    e.wait_ge(S("v2"), r + 1)

                    def operands(u, side):
                        q = slice(side * HALF, (side + 1) * HALF)
                        return KA[0], KB[0], QA[0][:, q], QB[0][:, q], lambda r_, j: V2[0:r_, j, :]
                    attend(PAIRS * 2 * KT + r * KT, 1, operands, 2 * PAIRS + r)
                e.wait_ge(S("quant"), 5)
                e.wait_ge(S("on"), 2 * PAIRS + 2)
                for b in range(4):
                    for h in range(2):
                        e.matmul(bank(2 * b + h), BQ[:, 512 + b * P:512 + (b + 1) * P],
                                 FQ[:, h * HALF:(h + 1) * HALF], start=True, stop=False)
                        ins = e.matmul(bank(2 * b + h), BQ[:, 512 + FFN + b * P:512 + FFN + (b + 1) * P], AQ,
                                       start=False, stop=True)
                    ins.then_inc(S("h1_ps"), 1)
                e.wait_ge(S("quant"), 6)
                for t in range(NT):
                    for b in range(4):
                        ins = e.matmul(PS[:, t // 4, (t % 4) * P:(t % 4 + 1) * P], HBQ[b][:, t * P:(t + 1) * P],
                                       BQ[:, 1536 + b * P:1536 + (b + 1) * P], start=(b == 0), stop=(b == 3))
                ins.then_inc(S("f2o_ps"), 1)
                to_fm(4, 0, 5)
            if last >= 6:
                e.wait_ge(S("x_fm"), 4)
                e.wait_ge(S("ld_lr"), 32)
                e.matmul(PS[0:1, 2, 0:RE], XT[:, 0:1], sm("w_r"), start=True, stop=True).then_inc(S("gl_ps"), 1)
                e.wait_ge(S("g_row"), 1)
                for b in range(4):
                    ins = e.matmul(PS[:, 7, b:b + 1], GX[:, b * P:(b + 1) * P], ones[0:1, 0:1], start=True, stop=True)
                ins.then_inc(S("gc_ps"), 1)
                for b in range(4):
                    if b >= 2:
                        e.wait_ge(S("mid"), b - 1)
                    for h in range(2):
                        ins = e.matmul(bank(2 * (b % 2) + h), LA[:, b * P:(b + 1) * P], XT[:, h * HALF:(h + 1) * HALF],
                                       start=True, stop=True)
                    ins.then_inc(S("mid_ps"), 1)
                e.wait_ge(S("mid"), 4)
                for t in range(NT):
                    for b in range(4):
                        ins = e.matmul(PS[:, 5 + t // 4, (t % 4) * P:(t % 4 + 1) * P], MID[b][:, t * P:(t + 1) * P],
                                       LB[:, b, :], start=(b == 0), stop=(b == 3))
                ins.then_inc(S("lr_ps"), 1)


def kernel(**inputs):
    import numpy as np
    import concourse.bacc as bacc
    from concourse.bass_utils import run_bass_kernel_spmd

    v = {k: np.asarray(a) for k, a in inputs.items()}

    def rows(a):
        a = a.reshape(1, -1)
        return np.broadcast_to(a, (P, a.shape[1]))

    def col(a):
        return a.reshape(-1, P).T

    x = v["x"][0]
    ctx = v["ctx_768"][0]
    parts = {
        "qk_w": rows(np.concatenate([v["L0_attn_qn_w"], v["L0_attn_kn_w"]])),
        "b_out": rows(v["L0_attn_b_out"]), "bo": rows(v["L0_xattn_bo"]),
        "gate_w": v["L0_ffn_gate_w"].T, "gate_b": rows(v["L0_ffn_gate_bias"]),
        "rot": np.repeat(v["L1_attn_rot_w"].reshape(3, D // 2, 2).transpose(1, 0, 2).reshape(D // 2, 6), 2, axis=0),
        "sb": rows(np.concatenate([v["L1_attn_scale"].reshape(1), v["L1_attn_bias"].reshape(1)])),
        "b_d2v": col(v["L1_xattn_b_d2v"]), "b_img": col(v["L1_xattn_b_img"]), "b_txt": col(v["L1_xattn_b_txt"]),
        "b_att0": col(np.tile(v["L1_xattn_b_att0"], 2)), "b_att1": col(np.tile(v["L1_xattn_b_att1"], 2)),
        "b_f1": col(v["L1_xattn_b_f1"]), "b_f2": rows(v["L1_xattn_b_f2"]),
        "b_att0_row": rows(v["L1_xattn_b_att0"]), "b_att1_row": rows(v["L1_xattn_b_att1"]),
        "w_r": v["L1_ffn_Wr"].T, "w_out": v["L0_attn_W_out"], "w_qkv": v["L0_attn_W_qkv"],
    }
    small = np.concatenate([parts[n] for n in SMALL], axis=1)
    pair_w = np.zeros((PAIRS, P, 4, P), np.float32)
    for i, n in enumerate(("Wq", "Wk", "Wv")):
        w = v["L0_xattn_" + n]
        pair_w[:, :w.shape[0], i, :] = w.reshape(w.shape[0], PAIRS, P).transpose(1, 0, 2)
    pair_w[:, :, 3, :] = v["L0_xattn_Wo"].reshape(PAIRS, P, D)
    moe_w = np.stack([v["L0_ffn_Wg"].reshape(BLK, P, D).transpose(0, 2, 1),
                      v["L0_ffn_Wu"].reshape(BLK, P, D).transpose(0, 2, 1),
                      v["L0_ffn_Wd"].transpose(0, 2, 1).reshape(BLK, P, D)], axis=2)
    sh_gu = np.stack([v["L0_ffn_Sg"].reshape(2, EI, D).transpose(0, 2, 1),
                      v["L0_ffn_Su"].reshape(2, EI, D).transpose(0, 2, 1)], axis=2)
    sh_d = v["L0_ffn_Sd"].T.reshape(2, EI, D)
    bit_w = np.zeros((P, NBIT), np.float32)
    for n in ("d2v", "img", "txt", "att0", "att1"):
        w = v["L1_xattn_W_" + n].T
        bit_w[:w.shape[0], BIT[n][0]:BIT[n][0] + w.shape[1]] = w
    for n in ("f1", "f2"):
        w = v["L1_xattn_W_" + n].T
        bit_w[:, BIT[n][0]:BIT[n][0] + BIT[n][1]] = w.reshape(-1, P, w.shape[1]).transpose(1, 0, 2).reshape(P, -1)
    named = {
        "x_tm": x, "x_fm": x.T, "ctx_fm": ctx.T, "small": small, "pair_w": pair_w, "moe_w": moe_w, "sh_gu": sh_gu,
        "sh_d": sh_d, "bit_w": bit_w, "lr_a": v["L1_ffn_A"].reshape(RE * RR, D).T,
        "lr_b": v["L1_ffn_Bw"].transpose(0, 2, 1).reshape(RE * RR, D),
    }
    nc = bacc.Bacc("TRN2", target_bir_lowering=False, num_devices=1)
    arrays, args = {}, {}
    for n, a in named.items():
        a = np.ascontiguousarray(a)
        arrays[f"in_{n}_dram"] = a
        args[n] = nc.dram_tensor(f"in_{n}_dram", a.shape, mybir.dt.from_np(a.dtype), kind="ExternalInput").ap()
    args["out"] = nc.dram_tensor("out_0_dram", (1, T, D), F32, kind="ExternalOutput").ap()
    build_decoder(nc, **args)
    r = run_bass_kernel_spmd(nc, [arrays], core_ids=[0])
    return r.results[0]["out_0_dram"]
```

```python
from contextlib import ExitStack

import concourse.bass as bass
from concourse import mybir

P = 128
T = 1024
NT = T // P
D = 128
HALF = 512
NC = 6404
DC = 96
KT = -(-NC // P)
TAIL = NC - (KT - 1) * P
HD = 64
HEADS0 = 8
PAIRS = HEADS0 // 2
L0H = 16
L0D = D // L0H
E = 64
EI = 88
NG = 8
GE = E // NG
BLK = E * EI // P
RE = 8
RR = 64
FFN = 512
LN_EPS = 1e-5
RMS_EPS = 1e-6
DEN_EPS = 1e-6
ROUTED_SCALE = 2.5
MAGIC = 12582912.0
NEG = -3.0e38
KW = 1024
KCH = [(c, min(KW, NC - c)) for c in range(0, NC, KW)]
NKC = len(KCH)
KP = [(c, min(HALF, NC - c)) for c in range(0, NC, HALF)]
NKP = len(KP)
TQ = [KT * i // 4 for i in range(5)]
VG = [list(range(g, min(g + 4, KT))) for g in range(0, KT, 4)]
NVG = len(VG)
PW = 3 * HALF
NPW = NC // PW
RESTW = NC - NPW * PW
PARTS = []
for _h in range(2):
    for _t in range(NT):
        PARTS += [("full", _h, _t, _k) for _k in range(NPW)]
        if _t % 3 == 2 or _t == NT - 1:
            PARTS.append(("rest", _h, _t - _t % 3, _t % 3 + 1))
NX = len(PARTS)
ALONE = "AAAVAA"
FULLS = NC // KW
NAA = ALONE.count("A")
PARTS1 = []
for _t in range(NT):
    PARTS1 += [("full", _t, _k) for _k in range(FULLS)] + [("rest", _t - 1, 0)] * (_t % 2)
ENGINE1 = [ALONE[k] if kind == "full" else "V" for kind, _, k in PARTS1]


def parts_on(engine, m):
    full, some = divmod(m, len(PARTS1))
    return full * ENGINE1.count(engine) + ENGINE1[:some].count(engine)


EXTRAS = ([("wk",), ("q",)] + [("k", c) for c in range(NKP)] + [("part", m) for m in range(NX // 2)] + [("wv",)]
          + [("part", m) for m in range(NX // 2, NX)])
PAUSE = (KT + 2) * (len(EXTRAS) + 4) // (2 * KT)
EXTRAS[PAUSE:PAUSE] = [("none",)] * 4
DEN_PARTS = sum(x[0] == "part" for x in EXTRAS[:(KT + 2) * len(EXTRAS) // (2 * KT)])

CHAIN = [("none",)] * 6 + [("ctx_max", c) for c in range(NKC)]
for _l in range(3):
    CHAIN += [("bit_sums",)] * (_l == 0) + [("max", _l)] + [("bit_weights",)] * (_l == 0) + [("none",)] * 2
    CHAIN += [("scale", _l)] + [("round", _l, c) for c in range(NKC + 1)]
    if _l < 2:
        CHAIN += [("project", _l, c) for c in range(NKC + 1)]
NVT = -(-KT // 16)
NEXT_KV = [("keys", c) for c in range(NKC)] + [("values", i) for i in range(NVT)]


def beside(extra, g, steps):
    if extra is not None:
        items, do = extra
        n = len(items)
        for x in items[g * n // steps:(g + 1) * n // steps]:
            do(x)


F32 = mybir.dt.float32
F16 = mybir.dt.float16
BF16 = mybir.dt.bfloat16
ALU = mybir.AluOpType
ACT = mybir.ActivationFunctionType
X = mybir.AxisListType.X
RED = bass.bass_isa.ReduceOp

SMALL = {}
_at = 0
for _n, _w in [("qk_w", 2 * D), ("b_out", D), ("bo", D), ("gate_w", E), ("gate_b", E), ("rot", 6), ("sb", 2),
               ("b_d2v", 1), ("b_img", 1), ("b_txt", 1), ("b_att0", 1), ("b_att1", 1), ("b_f1", FFN // P),
               ("b_f2", D), ("b_att0_row", HD), ("b_att1_row", HD), ("w_r", RE), ("w_out", D), ("w_qkv", 3 * D)]:
    SMALL[_n] = (_at, _at + _w)
    _at += _w
NSMALL = _at
BIT = {"d2v": (0, 128, DC, DC * 128), "img": (128, 128, 128, 128 * 128), "txt": (256, 128, 128, 128 * 128),
       "att0": (384, 64, 128, 64 * 128), "att1": (448, 64, 128, 64 * 128),
       "f1": (512, 2 * FFN, 128, 2 * D * FFN), "f2": (1536, 4 * D, 128, D * FFN)}
BIT_N = list(BIT)
NBIT = 2048


def rows_of(j):
    return P if j < KT - 1 else TAIL


def build_decoder(nc, x_tm, x_fm, ctx_fm, small, pair_w, moe_w, sh_gu, sh_d, bit_w, lr_a, lr_b, out):
    with ExitStack() as ctx:
        def sb(name, shape, dt=F32):
            return ctx.enter_context(nc.sbuf_tensor(name, shape, dt))

        def sem(name):
            return ctx.enter_context(nc.semaphore(name))

        PS = ctx.enter_context(nc.psum_tensor("PS", [P, 8, HALF], F32))

        CTX = sb("CTX", [P, NC])
        C_HI, C_LO = CTX[:, :].bitcast(F16)[:, 0:NC], CTX[:, :].bitcast(F16)[:, NC:2 * NC]
        KA = [sb(f"KA{h}", [P, NC], F16) for h in range(2)]
        KB = [sb(f"KB{h}", [P, NC], F16) for h in range(2)]
        KNB = sb("KNB", [P, 2 * NC], F16)
        KN = [KNB[:, h * NC:(h + 1) * NC] for h in range(2)]
        V = sb("V", [P, KT, P])
        PR = sb("PR", [P, 3, T])
        ACC = sb("ACC", [P, 2, T])
        X_ = sb("X", [P, NT, D])
        R = sb("R", [P, NT, D])
        XT = sb("XT", [P, T])
        QS = sb("QS", [P, T])
        ON = sb("ON", [P, T])
        QA = [sb(f"QA{h}", [P, T], F16) for h in range(2)]
        QB = [sb(f"QB{h}", [P, T], F16) for h in range(2)]
        QN = [sb(f"QN{h}", [P, T], F16) for h in range(2)]
        MAXB = sb("MAXB", [P, 4 * PW], F16)
        ME3, MF3 = ([MAXB[:, i * PW:(i + 1) * PW] for i in z] for z in ((0, 1), (2, 3)))
        ME = MAXB[:, 0:2 * KW].rearrange("p (a b) -> p a b", a=2)
        MF = MAXB[:, 2 * KW:4 * KW].rearrange("p (a b) -> p a b", a=2)
        BQ = MAXB[:, 4 * KW:].bitcast(BF16)
        SM = sb("SM", [P, NSMALL])
        ident = sb("ident", [P, P])
        ones = sb("ones", [P, P])
        PWQ = sb("PWQ", [P, 2, P])
        PWV = sb("PWV", [P, P])
        PWO = sb("PWO", [P, D])
        LNS = sb("LNS", [P, NT, 6])
        LNM = sb("LNM", [P, NT, 2])
        LNV = sb("LNV", [P, NT])
        LND = sb("LND", [P, NT])
        LNR = sb("LNR", [P, NT])
        MXP = sb("MXP", [P, 2 * NT, 4])
        NEGM = sb("NEGM", [P, 2 * NT], F16)
        ident16 = sb("ident16", [P, P], F16)
        WK2 = sb("WK2", [P, 2, P], F16)
        WV2 = sb("WV2", [P, 2, P], F16)
        CTX32 = KNB[:, :].bitcast(F32)[0:DC, :]

        def sm(name):
            a, b = SMALL[name]
            return SM[:, a:b]

        BIG = V[:, :, :].rearrange("p a b -> p (a b)")
        KF = [KA[h][:, :].bitcast(F32) for h in range(2)]
        KG = [KB[h][:, :].bitcast(F32) for h in range(2)]

        sems = {}

        def S(name):
            if name not in sems:
                sems[name] = sem(name)
            return sems[name]

        def bank(a, b=None, part=slice(0, P)):
            b = a + 1 if b is None else b
            return PS[part, a:b, :].rearrange("p a b -> p (a b)")

        def MW_(s):
            return BIG[:, s * 384:(s + 1) * 384].rearrange("p (a b) -> p a b", a=3)

        def W_HI(s):
            return KN[1][:, s * 768:s * 768 + 384].rearrange("p (a b) -> p a b", a=3)

        def W_LO(s):
            return KN[1][:, s * 768 + 384:s * 768 + 768].rearrange("p (a b) -> p a b", a=3)

        HS_ = [z.bitcast(F16) for z in (PR[:, 1, :], PR[:, 2, :], ACC[:, 0, :], ACC[:, 1, :])]
        H_HI = [z[:, 0:T] for z in HS_]
        H_LO = [z[:, T:2 * T] for z in HS_]
        X_HI = PR[:, 0, :].bitcast(F16)[:, 0:T]
        X_LO = PR[:, 0, :].bitcast(F16)[:, T:2 * T]
        ROUT = 1536
        SEL = KA[0][:, 0:E * EI]
        MH = [KG[0][:, 0:T], KG[0][:, T:2 * T]]
        MS = [KG[1][:, 0:T], KG[1][:, T:2 * T]]
        MU = KA[1][:, 0:2 * T].bitcast(F32)
        RWT = KA[1][:, 2 * T:3 * T]
        RWF = KA[1][:, 3 * T:5 * T].bitcast(F32)
        VA = BIG[:, 0:NT * (D + 1)].rearrange("p (t d) -> p t d", t=NT)
        QK0 = KF[0][:, 0:NT * 2 * D].rearrange("p (t a d) -> p t a d", t=NT, a=2)
        SCR = KF[1][:, 0:2 * NT * D].rearrange("p (n d) -> p n d", d=D)
        SS = LNS[:, :, 0:2]
        MASK = KG[0][:, 0:D]
        KVB = KG[0][:, D:3 * D]
        KVS = KG[0][:, 3 * D:4 * D + 1]
        DEN = KG[1][:, 0:T]
        RMS = KG[1][:, T:T + 2 * NT]
        RMD = KG[1][:, T + 32:T + 32 + 2 * NT]
        RMR = KG[1][:, T + 64:T + 64 + 2 * NT]
        QS2 = KG[1][:, T + 128:2 * T + 128]
        XB = PR[:, 0, :]
        DEN2 = sb("DEN2", [P, HALF])[:, :]
        RW_TM = [None]
        HB_ = BIG[:, KT * HD:2 * KT * HD]
        HN = KN[1].bitcast(F32)
        SWAP = HB_[:, 0:D]
        ROT = HB_[:, D:4 * D].rearrange("p (a d) -> p a d", a=3)
        G3 = HB_[:, 512:518].rearrange("p (a b) -> p a b", b=2)
        GQ = HB_[:, 520:526].rearrange("p (a b) -> p a b", b=2)
        GN = HB_[:, 528:531]
        GD = HB_[:, 532:535]
        GR = HB_[:, 536:539]
        HS = HB_[:, 540:544]
        HM = HB_[:, 544:544 + NT]
        HL = HB_[:, 552:552 + NT]
        HLR = HB_[:, 560:560 + NT]
        HI = HB_[:, 568:568 + NT]
        HID = HB_[:, 576:576 + NT]
        HIR = HB_[:, 584:584 + NT]
        HC = HB_[:, 592:592 + NT]
        HNM = HB_[:, 600:600 + NT]
        HQ = HN[:, 0:T]
        HK = HN[:, T:2 * T]
        HV = HN[:, 2 * T:3 * T].rearrange("p (j d) -> p j d", j=NT)
        HP = [PR[:, 0, :], PR[:, 1, :]]
        HPT = [ACC[:, i, :].rearrange("p (j d) -> p j d", j=NT) for i in range(2)]
        HO = KF[1][:, 0:T].rearrange("p (j d) -> p j d", j=NT)
        HSQ = KF[1][:, T:2 * T].rearrange("p (j d) -> p j d", j=NT)
        BW = KN[1].bitcast(F32)[:, 0:NBIT]
        BQD = sb("BQD", [P, 2, P], BF16)
        BR = sb("BR", [P, 8])
        BT = sb("BT", [P, 8])
        BS = sb("BS", [P, 8])
        BH = sb("BH", [P, 8])
        BN = sb("BN", [P, 8])
        NQ = 8
        AX = sb("AX", [P, NQ])
        AM = sb("AM", [P, NQ])
        AS = sb("AS", [P, NQ])
        AI = sb("AI", [P, NQ])
        WS = sb("WS", [P, NQ + 2])
        AVG = sb("AVG", [P, 4])
        AXP = sb("AXP", [P, NKC])
        AVP = sb("AVP", [P, NKC])
        NMAG = sb("NMAG", [P, 1])
        DUP = sb("DUP", [P, P])[:, :]
        LA = PR[:, 0, 0:4 * P]
        LB = PR[:, 0, 4 * P:8 * P].rearrange("p (a d) -> p a d", a=4)


        EMB = [KN[0].bitcast(BF16), KN[1].bitcast(BF16), KN[0].bitcast(BF16)]
        IQ = EMB[2]
        V2 = [BIG[:, r * KT * HD:(r + 1) * KT * HD].rearrange("p (a b) -> p a b", b=HD) for r in range(2)]
        HB = [BIG[:, b * T:(b + 1) * T] for b in range(4)]
        HBQ = [KA[1][:, b * T:(b + 1) * T].bitcast(BF16) for b in range(4)]
        FQ = KB[1][:, 0:T].bitcast(BF16)
        AQ = KB[1][:, T:T + HALF].bitcast(BF16)
        XQ = KA[1][:, 0:T].bitcast(BF16)
        XF = PR[:, 0, :]
        OO = PR[:, 1, :]
        GC = sb("GC", [P, 4])
        GNM = sb("GNM", [1, 1])[:, :]
        GE_ = sb("GE", [1, RE])[:, :]
        GL0 = sb("GL", [1, RE])[:, :]
        GX = PR[0:1, 2, 0:4 * P]
        GT = sb("GT", [1, 64])
        MID = [BIG[:, b * T:(b + 1) * T] for b in range(4)]

        block = ctx.enter_context(nc.Block())

        @block.sync
        def _(q):
            q.dma_start(SM[:, :], small).then_inc(S("ld_small"), 16)
            q.dma_start(XT[:, :], x_fm).then_inc(S("ld_x"), 16)
            q.dma_start(X_[:, :, :], x_tm.rearrange("(t p) d -> p t d", p=P)).then_inc(S("ld_x"), 16)
            q.dma_start(CTX32, ctx_fm).then_inc(S("ld_ctx"), 16)
            def load_qk(p, w):
                q.dma_start(PWQ[:, :, :], w[:, 0:2, :]).then_inc(S("ld_pwq"), 16)

            def copy_keys(p, behind):
                q.wait_ge(S("k_lo"), p * NKP + NKP)
                for i in range(4):
                    a, b = TQ[i] * P, min(TQ[i + 1] * P, NC)
                    if behind:
                        q.wait_ge(S("scores"), (p - 1) * 2 * KT + (KT + TQ[i + 1]))
                    for h in range(2):
                        hi = slice(0, HD) if h == 0 else slice(HD, P)
                        q.dma_start(KA[h][:, a:b], KN[h][:, a:b]).then_inc(S("keys"), 16)
                        q.dma_start(KB[h][hi, a:b], KN[h][hi, a:b]).then_inc(S("keys"), 16)

            load_qk(0, pair_w[0])
            q.dma_start(PWV[:, :], pair_w[0, :, 2, :]).then_inc(S("ld_pwv"), 16)
            q.dma_start(PWO[:, :], pair_w[0, :, 3, :]).then_inc(S("ld_pwo"), 16)
            copy_keys(0, False)
            with q.Fori(0, PAIRS - 1) as p:
                w = pair_w[bass.ds(p + 1, 1)].rearrange("o p a b -> (o p) a b")
                q.wait_ge(S("k_ps"), p * NKP + NKP)
                load_qk(p + 1, w)
                q.wait_ge(S("v_ps"), p * NVG + NVG)
                q.dma_start(PWV[:, :], w[:, 2, :]).then_inc(S("ld_pwv"), 16)
                copy_keys(p + 1, True)
                q.wait_ge(S("wo_ps"), p + 1)
                q.dma_start(PWO[:, :], w[:, 3, :]).then_inc(S("ld_pwo"), 16)
            q.wait_ge(S("v_ps"), PAIRS * NVG)
            q.dma_start(CTX[0:DC, :], ctx_fm).then_inc(S("ld_ctx"), 16)
            q.wait_ge(S("bit_zero"), 1)
            q.dma_start(BW[:, 128:NBIT], bit_w[:, 128:NBIT]).then_inc(S("ld_bit"), 16)
            q.dma_start(BW[0:DC, 0:128], bit_w[0:DC, 0:128]).then_inc(S("ld_bit"), 16)
            q.wait_ge(S("x_fm"), 2)
            q.wait_ge(S("moe_zero"), 1)
            for h in range(2):
                q.dma_start(MW_(2 + h)[:, 0:2, 0:EI], sh_gu[h]).then_inc(S(f"ld_w{2 + h}"), 16)
                q.dma_start(MW_(2 + h)[0:EI, 2, :], sh_d[h]).then_inc(S(f"ld_w{2 + h}"), 16)
            for j in range(4):
                if j >= 2:
                    q.wait_ge(S("w_lo"), j - 1)
                q.dma_start(MW_(j)[:, :, :], moe_w[j]).then_inc(S(f"ld_w{j}"), 16)
            with q.Fori(1, BLK // 4) as i:
                for j in range(4):
                    q.wait_ge(S("w_lo"), 4 * i + (j - 1))
                    q.dma_start(MW_(j)[:, :, :],
                                moe_w[bass.ds(4 * i + j, 1)].rearrange("o p a b -> (o p) a b")
                                ).then_inc(S(f"ld_w{j}"), 16)
            q.wait_ge(S("ln_x"), 5)
            q.dma_start(LA, lr_a).then_inc(S("ld_lr"), 16)
            q.dma_start(LB, lr_b.rearrange("(a p) d -> p a d", p=P)).then_inc(S("ld_lr"), 16)
            q.wait_ge(S("ln_x"), 6)
            q.dma_start(out.rearrange("o (t p) d -> p (o t) d", p=P), X_[:, :, :]).then_inc(S("stored"), 16)
            q.wait_ge(S("stored"), 16)

        @block.gpsimd
        def _(e):
            n = [0]

            def link(ins):
                n[0] += 1
                ins.then_inc(S("pool_step"), 1)
                e.wait_ge(S("pool_step"), n[0])

            def diag(ap, base, fill=1.0, pattern=None, mult=1):
                link(e.affine_select(out=ap, in_=ap, compare_op=ALU.not_equal, fill=fill, base=base,
                                     pattern=pattern or [[-1, P]], channel_multiplier=mult))

            link(e.memset(ident[:, :], 0.0))
            diag(ident[:, :], 0)
            link(e.memset(ident16[:, :], 0.0))
            diag(ident16[:, :], 0)
            link(e.memset(ones[:, :], 1.0))
            link(e.memset(MASK, 1.0))
            m3 = MASK.rearrange("p (a b) -> p a b", b=L0D)
            link(e.affine_select(out=m3, in_=m3, compare_op=ALU.is_ge, fill=0.0, base=0,
                                 pattern=[[-L0D, L0H], [0, L0D]], channel_multiplier=1))
            link(e.affine_select(out=m3, in_=m3, compare_op=ALU.is_ge, fill=0.0, base=L0D - 1,
                                 pattern=[[L0D, L0H], [0, L0D]], channel_multiplier=-1))
            link(e.memset(VA[:, :, D:D + 1], 1.0))
            e.sem_inc(S("consts"), 1)
            e.wait_ge(S("c_hi"), 1)
            link(e.tensor_tensor(C_LO[0:DC, :], CTX32, C_HI[0:DC, :], ALU.subtract))
            e.sem_inc(S("c_lo"), 1)

            e.wait_ge(S("x_fm"), 1)
            for h in range(2):
                lo = slice(HD, P) if h == 0 else slice(0, HD)
                link(e.memset(KB[h][lo, :], 0.0))
                link(e.memset(KB[h][lo.start:lo.start + 1, :], 1.0))
                link(e.memset(QB[h][lo, :], 0.0))
            e.sem_inc(S("shift_rows"), 1)
            link(e.memset(AX[:, :], 0.0))
            link(e.memset(NMAG[:, :], -MAGIC))
            e.wait_ge(S("keys"), PAIRS * 256)
            link(e.memset(BW[:, 0:128], 0.0))
            e.sem_inc(S("bit_zero"), 1)
            e.wait_ge(S("bit_rows"), 1)
            e.partition_all_reduce(BT[:, 0:7], BR[:, 0:7], P, RED.add).then_inc(S("bit_sum"), 1)
            for i in range(3):
                e.wait_ge(S("ax"), i + 1)
                e.partition_all_reduce(AM[:, i:i + 1], AX[:, i:i + 1], P, RED.max).then_inc(S("am"), 1)
            e.wait_ge(S("ln_x"), 2)
            link(e.memset(BIG[:, 2 * 384:4 * 384], 0.0))
            e.sem_inc(S("moe_zero"), 1)
            sv = SEL.rearrange("p (e i) -> p e i", i=EI)
            link(e.memset(SEL, 0.0))
            for base in (0, -E):
                diag(sv, base, pattern=[[-1, E], [0, EI]])
            e.sem_inc(S("selector"), 1)

            def hidden_lo(n, hslot):
                e.wait_ge(S("h_hi"), n + 1)
                e.tensor_tensor(H_LO[hslot], MH[hslot % 2], H_HI[hslot], ALU.subtract).then_inc(S("h_lo"), 1)

            hidden_lo(0, 0)
            hidden_lo(1, 1)
            with e.Fori(0, BLK // 4) as i:
                for j in range(4):
                    hidden_lo(4 * i + (2 + j), (2 + j) % 4)
            e.wait_ge(S("ln_x"), 3)
            link(e.memset(SWAP, 0.0))
            w3 = SWAP.rearrange("p (a b) -> p a b", b=2)
            diag(w3[:, :, 1], 0, 1.0, [[-2, D // 2]])
            diag(w3[:, :, 0], -1, -1.0, [[-2, D // 2]])
            e.sem_inc(S("swap"), 1)
            for r in range(2):
                link(e.memset(KB[r][HD:P, :], 0.0))
                link(e.memset(KB[r][HD:HD + 1, :], 1.0))
            link(e.memset(QB[0][HD:P, :], 0.0))
            link(e.memset(DUP, 0.0))
            for base in (0, HD, -HD):
                diag(DUP, base)
            e.sem_inc(S("bit_rows1"), 1)
            for i in range(3, 6):
                e.wait_ge(S("ax"), i + 1)
                e.partition_all_reduce(AM[:, i:i + 1], AX[:, i:i + 1], P, RED.max).then_inc(S("am"), 1)

        @block.scalar
        def _(e):
            def ln(k):
                e.wait_ge(S("ln_var"), k)
                e.activation(LND[:, :], LNV[:, :], ACT.Sqrt).then_inc(S("ln_sd"), 1)

            def to_fm(k, a):
                e.wait_ge(S("xt_ps"), k)
                e.activation(XT[:, :], bank(a, a + 2), ACT.Copy).then_inc(S("x_fm"), 1)

            def weight_hi(p, name, out, full):
                e.wait_ge(S("ld_" + name), p * 16 + 16)
                e.activation(out[0:DC, 0, :], full, ACT.Copy).then_inc(S(name + "_hi"), 1)

            for t in range(NT):
                e.wait_ge(S("qkv"), t + 1)
                for a in range(2):
                    e.activation(SCR[:, 2 * t + a, :], PS[:, t, a * D:(a + 1) * D], ACT.Square,
                                 accum_out=SS[:, t, a:a + 1])
                e.wait_ge(S("consts"), 1)
                e.activation(VA[:, t, 0:D], PS[:, t, 2 * D:3 * D], ACT.Copy).then_inc(S("v0"), 1)
            e.wait_ge(S("rms"), 1)
            e.activation(RMD, RMS, ACT.Sqrt).then_inc(S("rms_sd"), 1)
            e.wait_ge(S("ld_ctx"), 16)
            e.activation(C_HI[0:DC, :], CTX32, ACT.Copy).then_inc(S("c_hi"), 1)
            weight_hi(0, "pwq", WK2, PWQ[0:DC, 1, :])
            weight_hi(0, "pwv", WV2, PWV[0:DC, :])
            e.wait_ge(S("q0_t"), 1)
            e.activation(QS[:, :], bank(1, 3), ACT.Copy).then_inc(S("q0_fm"), 1)
            ln(1)
            to_fm(1, 0)

            def copy_out(base, obase, u):
                e.wait_ge(S("pv"), base + KT * (u + 1))
                e.activation(ON[:, u * HALF:(u + 1) * HALF], bank(4), ACT.Copy).then_inc(S("o_ev"), 1)

            def exps(base, units, obase, extra=None):
                for g in range(units * KT):
                    r = rows_of(g % KT)
                    e.wait_ge(S("scores"), base + g + 1)
                    if g >= 3:
                        e.wait_ge(S("pv"), base + g - 2)
                        e.wait_ge(S("acc"), base + g - 2)
                    e.activation(PR[0:r, g % 3, :], bank(2 * (g % 2), 2 * (g % 2) + 2, slice(0, r)),
                                 ACT.Exp).then_inc(S("exp"), 1)
                    if g == KT:
                        copy_out(base, obase, 0)
                    beside(extra, g, units * KT)
                copy_out(base, obase, units - 1)

            def q_out(p, b):
                e.wait_ge(S("q_ps"), p + 1)
                e.activation(QS[:, :], bank(b, b + 2), ACT.Copy, scale=HD ** -0.5).then_inc(S("q_ev"), 1)

            def k_out(p, c, b):
                a, w = KP[c]
                e.wait_ge(S("k_ps"), p * NKP + c + 1)
                e.activation(KN[0][0:HD, a:a + w], PS[0:HD, b, 0:w], ACT.Copy)
                e.activation(KN[1][HD:P, a:a + w], PS[HD:P, b, 0:w], ACT.Copy).then_inc(S("k_hi"), 1)

            def max_copies(first, heads):
                for h in range(heads):
                    for x, (kind, t, k) in enumerate(PARTS1):
                        if kind == "rest" or ALONE[k] != "A":
                            continue
                        m, i = (first + h) * len(PARTS1) + x, (first + h) * NT + t
                        n = ALONE[:k].count("A")
                        e.wait_ge(S("alone_ps"), m + 1)
                        if n == 0:
                            if i >= 2:
                                e.wait_ge(S("alone_tile"), i - 1)
                            dst = ME[:, i % 2, :]
                        else:
                            f = i * (NAA - 1) + n - 1
                            if f >= 2:
                                e.wait_ge(S("alone_merged"), f - 1)
                            dst = MF[:, f % 2, :]
                        e.activation(dst, bank(2 * (m % 4), 2 * (m % 4) + 2), ACT.Copy).then_inc(S("alone_A"), 1)

            def preparation(p):
                def piece(x):
                    if x[0] == "none":
                        return
                    if x[0] == "wk":
                        weight_hi(p + 1, "pwq", WK2, PWQ[0:DC, 1, :])
                    elif x[0] == "wv":
                        weight_hi(p + 1, "pwv", WV2, PWV[0:DC, :])
                    elif x[0] == "q":
                        q_out(p + 1, 6)
                    elif x[0] == "k":
                        k_out(p + 1, x[1], 6 + x[1] % 2)
                    else:
                        m = x[1]
                        kind, h, t, k = PARTS[m]
                        if kind == "rest":
                            return
                        i = h * NT + t
                        e.wait_ge(S("part_ps"), p * NX + (m + 1))
                        if k == 0:
                            if i >= 2:
                                e.wait_ge(S("tile_max"), p * 2 * NT + (i - 1))
                            dst = ME3[i % 2]
                        else:
                            f = i * (NPW - 1) + k - 1
                            if f >= 2:
                                e.wait_ge(S("merged"), p * 2 * NT * (NPW - 1) + (f - 1))
                            dst = MF3[f % 2]
                        e.activation(dst, bank(5, 8), ACT.Copy).then_inc(S("part_out"), 1)
                return EXTRAS, piece

            q_out(0, 0)
            for c in range(NKP):
                k_out(0, c, 2 + c % 6)
            max_copies(0, 2)

            def head(p):
                e.wait_ge(S("shift_ps"), p + 1)
                e.wait_ge(S("shift_rows"), 1)
                e.activation(QB[0][HD:HD + 1, :], bank(6, 8, slice(HD, HD + 1)), ACT.Copy)
                e.activation(QB[1][0:1, :], bank(6, 8, slice(0, 1)), ACT.Copy).then_inc(S("shift"), 1)
                for g in range(NVG):
                    e.wait_ge(S("v_ps"), p * NVG + g + 1)
                    full = [j for j in VG[g] if rows_of(j) == P]
                    ins = e.activation(V[:, full[0]:full[-1] + 1, :], PS[:, g % 4, 0:P * len(full)].rearrange(
                        "p (a b) -> p a b", b=P), ACT.Copy)
                    if len(full) < len(VG[g]):
                        ins = e.activation(V[0:TAIL, KT - 1, :],
                                           PS[0:TAIL, g % 4, P * len(full):P * len(full) + P], ACT.Copy)
                    ins.then_inc(S("v_ev"), 1)

            head(0)
            with e.Fori(0, PAIRS - 1) as p:
                exps(p * 2 * KT, 2, 2 * p, preparation(p))
                head(p + 1)

            def chain(x):
                if x[0] == "round" and x[2]:
                    a, w = KCH[x[2] - 1]
                    rows = slice(0, DC) if x[1] == 0 else slice(0, P)
                    e.wait_ge(S("magic"), x[1] * NKC + x[2])
                    e.activation(EMB[x[1]][rows, a:a + w], CTX[rows, a:a + w], ACT.Identity,
                                 bias=NMAG[rows, :]).then_inc(S("emb"), 1)
                elif x[0] == "project" and x[2] < NKC:
                    a, w = KCH[x[2]]
                    e.wait_ge(S("bp"), x[1] * NKC + x[2] + 1)
                    more = {"accum_out": AVP[:, x[2]:x[2] + 1]} if x[1] else {}
                    e.activation(CTX[:, a:a + w], bank(6, 8)[:, 0:w], ACT.Identity, scale=WS[:, x[1]:x[1] + 1],
                                 bias=sm("b_img" if x[1] else "b_d2v"), **more).then_inc(S("bev"), 1)

            exps((PAIRS - 1) * 2 * KT, 2, 2 * (PAIRS - 1), (CHAIN, chain))
            ln(2)
            to_fm(2, 0)
            e.wait_ge(S("x_fm"), 2)
            e.activation(X_HI, XT[:, :], ACT.Copy).then_inc(S("x_hi"), 1)

            def silu(n, slot):
                e.wait_ge(S("moe_gate"), n + 1)
                if not isinstance(n, int) or n >= 2:
                    e.wait_ge(S("moe_h1"), n - 1)
                e.activation(MS[slot], bank(0, 2), ACT.Silu).then_inc(S("moe_silu"), 1)

            def weights_hi(n, slot, ld):
                e.wait_ge(S(f"ld_w{slot}"), ld)
                if not isinstance(n, int) or n >= 4:
                    e.wait_ge(S("moe_down"), n - 3)
                e.activation(W_HI(slot), MW_(slot), ACT.Copy).then_inc(S("w_hi"), 1)

            def hidden_hi(n, hslot):
                e.wait_ge(S("moe_h"), n + 1)
                if not isinstance(n, int) or n >= 4:
                    e.wait_ge(S("moe_down"), n - 3)
                e.activation(H_HI[hslot], MH[hslot % 2], ACT.Copy).then_inc(S("h_hi"), 1)

            def four(i):
                for j in range(4):
                    weights_hi(4 * i + (2 + j), j, 16 * i + (48 if j >= 2 else 16))
                    hidden_hi(4 * i + j, j)
                    silu(4 * i + (1 + j), (1 + j) % 2)

            weights_hi(0, 2, 32)
            weights_hi(1, 3, 32)
            e.wait_ge(S("logits"), 1)
            e.activation(BIG[:, ROUT:ROUT + NT * E], bank(4), ACT.Sigmoid).then_inc(S("sig"), 1)
            silu(0, 0)
            e.wait_ge(S("rw_t"), 1)
            e.activation(RWF[0:E, :], bank(4, 6, slice(0, E)), ACT.Copy).then_inc(S("rw_fm"), 1)
            four(0)
            with e.Fori(1, BLK // 4) as i:
                four(i)
            hidden_hi(BLK, 0)
            silu(BLK + 1, 1)
            hidden_hi(BLK + 1, 1)
            e.wait_ge(S("moe_down"), BLK + 2)
            e.activation(QS[:, :], bank(6, 8), ACT.Copy).then_inc(S("moe_fm"), 1)
            ln(3)
            to_fm(3, 0)
            def kv(r, b):
                wcol = 2 if r == 0 else 6

                def piece(x):
                    if x[0] == "keys":
                        c = x[1]
                        a, w = KCH[c]
                        e.wait_ge(S("kv_ps"), r * NKC + c + 1)
                        if r:
                            e.wait_ge(S("kv_lo"), c + 1)
                        e.activation(CTX[:, a:a + w], bank(b, b + 2)[:, 0:w], ACT.Identity,
                                     scale=WS[:, wcol:wcol + 1], bias=sm(f"b_att{r}")).then_inc(S("kv_ev"), 1)
                        e.wait_ge(S("kv_ev"), r * NKC + c + 1)
                        e.activation(KA[r][:, a:a + w], CTX[:, a:a + w], ACT.Copy).then_inc(S("kv_hi"), 1)
                    else:
                        i = x[1]
                        full = min(16, KT - 1 - 16 * i)
                        e.wait_ge(S("vt_ps"), r * NVT + i + 1)
                        ins = e.activation(V2[r][:, 16 * i:16 * i + full, :], bank(b, b + 2)[:, 0:full * HD].rearrange(
                            "p (a b) -> p a b", b=HD), ACT.Copy, scale=WS[:, wcol:wcol + 1])
                        if full < 16:
                            ins = e.activation(V2[r][0:TAIL, KT - 1, :],
                                               bank(b, b + 2, slice(0, TAIL))[:, full * HD:(full + 1) * HD],
                                               ACT.Copy, scale=WS[0:TAIL, wcol:wcol + 1])
                        ins.then_inc(S("vt_ev"), 1)
                return piece

            e.wait_ge(S("rot_n"), 1)
            e.activation(GD, GN, ACT.Sqrt).then_inc(S("rot_sd"), 1)
            e.wait_ge(S("hq"), 1)
            e.activation(HQ, bank(0, 2), ACT.Copy, scale=HS[:, 0:1])
            e.activation(HK, bank(2, 4), ACT.Copy)
            e.activation(HV.rearrange("p j d -> p (j d)"), bank(4, 6), ACT.Copy).then_inc(S("hqkv"), 1)
            def h_exp(t):
                b = 2 * (t % 2)
                e.wait_ge(S("h_max"), t + 1)
                if t >= 2:
                    e.wait_ge(S("h_pt"), t - 1)
                e.activation(HP[t % 2], bank(b, b + 2), ACT.Exp, bias=HNM[:, t:t + 1],
                             accum_out=HL[:, t:t + 1]).then_inc(S("h_exp"), 1)

            h_exp(0)
            for t in range(NT):
                e.wait_ge(S("h_pt"), t + 1)
                if t >= 2:
                    e.wait_ge(S("h_av"), t - 1)
                e.activation(HPT[t % 2].rearrange("p j d -> p (j d)"), bank(4, 6),
                             ACT.Copy).then_inc(S("h_ptc"), 1)
                if t + 1 < NT:
                    h_exp(t + 1)
                beside((NEXT_KV, kv(0, 4)), t, NT)
            for t in range(NT):
                e.wait_ge(S("h_o"), 1)
                ins = e.activation(HSQ[:, t, :], HO[:, t, :], ACT.Square, accum_out=HI[:, t:t + 1])
            ins.then_inc(S("h_inner"), 1)
            e.wait_ge(S("h_clip"), 1)
            e.activation(HID, HC, ACT.Sqrt).then_inc(S("h_sd"), 1)
            ln(4)
            def scaled(out, a, w, q, bias, name, rows=slice(0, P), func=ACT.Identity):
                e.activation(out, a, func, scale=WS[rows, q:q + 1], bias=bias).then_inc(S(name), 1)

            e.wait_ge(S("f_int"), 1)
            e.wait_ge(S("ws"), 4)
            scaled(XT[:, :], bank(0, 2), T, 3, sm("b_txt"), "fused")
            for r in range(2):
                e.wait_ge(S("f2_ps"), r + 1)
                e.activation(QS[:, :], bank(0, 2), ACT.Copy, scale=D ** -0.5).then_inc(S("f2"), 1)
                max_copies(2 + r, 1)
                e.wait_ge(S("shift_ps"), PAIRS + r + 1)
                e.activation(QB[0][HD:HD + 1, :], bank(0, 2, slice(HD, HD + 1)),
                             ACT.Copy).then_inc(S("shift"), 1)
                exps(PAIRS * 2 * KT + r * KT, 1, 2 * PAIRS + r, None if r else (NEXT_KV, kv(1, 6)))
            for b in range(4):
                e.wait_ge(S("h1_ps"), b + 1)
                e.wait_ge(S("ws"), 5)
                scaled(HB[b], bank(2 * b, 2 * b + 2), T, 4, SM[:, SMALL["b_f1"][0] + b:SMALL["b_f1"][0] + b + 1],
                       "hb", func=ACT.Relu)
            for b in range(4):
                e.wait_ge(S("h_magic"), b + 1)
                e.activation(HBQ[b], HB[b], ACT.Identity, bias=NMAG[:, :]).then_inc(S("h_int"), 1)
            e.wait_ge(S("f2o_ps"), 1)
            e.activation(QS[:, :], bank(0, 2), ACT.Copy, scale=WS[:, 5:6]).then_inc(S("f2o"), 1)
            ln(5)
            to_fm(4, 0)
            e.wait_ge(S("g_max"), 1)
            e.activation(GE_, GL0, ACT.Exp, bias=GNM).then_inc(S("g_exp"), 1)
            for b in range(4):
                e.wait_ge(S("mid_ps"), b + 1)
                e.wait_ge(S("g_col"), 1)
                e.activation(MID[b], bank(2 * (b % 3), 2 * (b % 3) + 2), ACT.Copy,
                             scale=GC[:, b:b + 1]).then_inc(S("mid"), 1)
            ln(6)

        @block.vector
        def _(e):
            n = [0]

            def link(ins):
                n[0] += 1
                ins.then_inc(S("dve_step"), 1)
                e.wait_ge(S("dve_step"), n[0])

            def ln(k):
                for t in range(NT):
                    ins = e.bn_stats(LNS[:, t, :], R[:, t, :])
                link(ins)
                for t in range(NT):
                    ins = e.bn_aggr(LNM[:, t, :], LNS[:, t, :])
                link(ins)
                e.tensor_scalar(LNV[:, :], LNM[:, :, 1], LN_EPS, None, ALU.add).then_inc(S("ln_var"), 1)
                e.wait_ge(S("ln_sd"), k)
                link(e.reciprocal(LNR[:, :], LND[:, :]))
                for t in range(NT):
                    ins = e.tensor_scalar(X_[:, t, :], R[:, t, :], LNM[:, t, 0:1], LNR[:, t:t + 1],
                                          ALU.subtract, ALU.mult)
                ins.then_inc(S("ln_x"), 1)
                e.wait_ge(S("ln_x"), k)

            def over_tiles(row, tiles=NT):
                return row.unsqueeze(1).to_broadcast([P, tiles, row.shape[-1]])

            x2 = X_[:, :, :].rearrange("p t d -> p (t d)")
            r2 = R[:, :, :].rearrange("p t d -> p (t d)")

            def split_lo(out, full, hi):
                return e.tensor_tensor(out, full, hi, ALU.subtract)

            e.wait_ge(S("ld_small"), 16)
            e.wait_ge(S("ld_x"), 32)
            link(e.tensor_tensor(XB.rearrange("p (t d) -> p t d", t=NT), X_[:, :, :], over_tiles(sm("b_out")),
                                 ALU.add))
            e.wait_ge(S("v0"), NT)
            e.tensor_scalar(RMS.rearrange("p (t a) -> p t a", a=2), SS, 1.0 / D, RMS_EPS, ALU.mult,
                            ALU.add).then_inc(S("rms"), 1)
            e.wait_ge(S("rms_sd"), 1)
            link(e.reciprocal(RMR, RMD))
            w = sm("qk_w")
            for t in range(NT):
                for a in range(2):
                    ins = e.scalar_tensor_tensor(QK0[:, t, a, :], PS[:, t, a * D:(a + 1) * D],
                                                 RMR[:, 2 * t + a:2 * t + a + 1], w[:, a * D:(a + 1) * D],
                                                 ALU.mult, ALU.mult)
            link(ins)
            qk_all = QK0.rearrange("p t a d -> p (t a d)")
            e.tensor_scalar(qk_all, qk_all, 0.0, None, ALU.max).then_inc(S("qk0"), 1)
            e.wait_ge(S("kv0"), 1)
            e.wait_ge(S("consts"), 1)
            link(e.tensor_copy(KVS, bank(0)[:, 0:D + 1]))
            link(e.tensor_tensor(KVB[:, 0:D], KVS[:, 0:D], MASK, ALU.mult))
            e.tensor_scalar(KVB[:, D:2 * D], MASK, KVS[:, D:D + 1], None, ALU.mult).then_inc(S("kvb"), 1)
            e.wait_ge(S("o0"), 1)
            link(e.tensor_scalar(DEN, bank(5, 7), DEN_EPS, None, ALU.add))
            link(e.reciprocal(QS2, DEN))
            e.tensor_tensor(ON[:, :], bank(3, 5), QS2, ALU.mult).then_inc(S("on0"), 1)
            e.wait_ge(S("wo0"), 1)
            link(e.tensor_tensor(r2, bank(1, 3), XB, ALU.add))
            ln(1)

            def maxima(first, heads):
                nv = ALONE.count("V")
                for h in range(heads):
                    for x, (kind, t, k) in enumerate(PARTS1):
                        m = (first + h) * len(PARTS1) + x
                        row, i = h * NT + t, (first + h) * NT + t
                        if kind == "rest":
                            e.wait_ge(S("alone_ps"), m + 1)
                            e.tensor_reduce(MXP[:, row:row + 2, nv + 1], PS[:, 2 * (m % 4):2 * (m % 4) + 2, 0:NC - FULLS * KW],
                                            X, ALU.max).then_inc(S("alone_V"), 1)
                        elif ALONE[k] == "V":
                            e.wait_ge(S("alone_ps"), m + 1)
                            c = 1 + ALONE[:k].count("V")
                            e.tensor_reduce(MXP[:, row, c:c + 1], bank(2 * (m % 4), 2 * (m % 4) + 2), X,
                                            ALU.max).then_inc(S("alone_V"), 1)
                        elif k:
                            f = i * (NAA - 1) + ALONE[:k].count("A") - 1
                            e.wait_ge(S("alone_A"), parts_on("A", m + 1))
                            if ALONE[:k].count("A") > 1:
                                e.wait_ge(S("alone_merged"), f)
                            e.tensor_tensor(ME[:, i % 2, :], ME[:, i % 2, :], MF[:, f % 2, :],
                                            ALU.max).then_inc(S("alone_merged"), 1)
                        if kind == "full" and k == ALONE.rindex("A"):
                            e.wait_ge(S("alone_merged"), (i + 1) * (NAA - 1))
                            best = ME[:, i % 2, :]
                            e.tensor_tensor(best[:, 0:KW // 2], best[:, 0:KW // 2], best[:, KW // 2:], ALU.max
                                            ).then_inc(S("alone_folded"), 1)
                            e.wait_ge(S("alone_folded"), i + 1)
                            e.tensor_reduce(MXP[:, row, 0:1], best[:, 0:KW // 2], X, ALU.max).then_inc(S("alone_tile"), 1)
                e.wait_ge(S("alone_V"), parts_on("V", (first + heads) * len(PARTS1)))
                e.wait_ge(S("alone_tile"), (first + heads) * NT)
                e.tensor_reduce(NEGM[:, 0:heads * NT], MXP[:, 0:heads * NT, 0:nv + 2], X, ALU.max,
                                negate=True).then_inc(S("negm"), 1)

            def normalize(obase, u):
                e.wait_ge(S("den_ps"), obase + u + 1)
                e.reciprocal(DEN2, bank(5)).then_inc(S("den_r"), 1)
                e.wait_ge(S("den_r"), obase + u + 1)
                e.wait_ge(S("o_ev"), obase + u + 1)
                part = ON[:, u * HALF:(u + 1) * HALF]
                e.tensor_tensor(part, part, DEN2, ALU.mult).then_inc(S("on"), 1)

            def sums(base, units, obase, extra=None):
                for g in range(units * KT):
                    u, j = divmod(g, KT)
                    r = rows_of(j)
                    e.wait_ge(S("exp"), base + g + 1)
                    if j == 0:
                        ins = e.tensor_copy(ACC[:, u, :], PR[:, g % 3, :])
                    else:
                        e.wait_ge(S("acc"), base + g)
                        ins = e.tensor_tensor(ACC[0:r, u, :], ACC[0:r, u, :], PR[0:r, g % 3, :], ALU.add)
                    ins.then_inc(S("acc"), 1)
                    if g == KT + 4:
                        normalize(obase, 0)
                    beside(extra, g, units * KT)
                normalize(obase, units - 1)

            def q_parts(p):
                e.wait_ge(S("q_ev"), p + 1)
                e.tensor_copy(QN[0][0:HD, :], QS[0:HD, :])
                e.tensor_copy(QN[0][HD:P, :], QS[0:HD, :])
                e.tensor_copy(QN[1][0:HD, :], QS[HD:P, :])
                e.tensor_copy(QN[1][HD:P, :], QS[HD:P, :]).then_inc(S("q_hi"), 1)

            def weight_lo(p, name, out, full):
                e.wait_ge(S(name + "_hi"), p + 1)
                split_lo(out[0:DC, 1, :], full, out[0:DC, 0, :]).then_inc(S(name + "_lo"), 1)

            def k_parts(p, c, b):
                a, w = KP[c]
                e.wait_ge(S("k_hi"), p * NKP + c + 1)
                split_lo(KN[0][HD:P, a:a + w], PS[0:HD, b, 0:w], KN[0][0:HD, a:a + w])
                split_lo(KN[1][0:HD, a:a + w], PS[HD:P, b, 0:w], KN[1][HD:P, a:a + w]).then_inc(S("k_lo"), 1)

            def preparation(p):
                def piece(x):
                    if x[0] == "none":
                        return
                    if x[0] == "wk":
                        return weight_lo(p + 1, "pwq", WK2, PWQ[0:DC, 1, :])
                    if x[0] == "wv":
                        return weight_lo(p + 1, "pwv", WV2, PWV[0:DC, :])
                    if x[0] == "q":
                        return q_parts(p + 1)
                    if x[0] == "k":
                        return k_parts(p + 1, x[1], 6 + x[1] % 2)
                    m = x[1]
                    kind, h, t, k = PARTS[m]
                    i = h * NT + t
                    if kind == "rest":
                        e.wait_ge(S("part_ps"), p * NX + (m + 1))
                        e.tensor_reduce(MXP[:, i:i + k, 1], PS[:, 5:5 + k, 0:RESTW], X,
                                        ALU.max).then_inc(S("part_out"), 1)
                    elif k:
                        f = i * (NPW - 1) + k - 1
                        m3 = ME3[i % 2]
                        e.wait_ge(S("part_out"), p * NX + (m + 1))
                        if k > 1:
                            e.wait_ge(S("merged"), p * 2 * NT * (NPW - 1) + f)
                        e.tensor_tensor(m3, m3, MF3[f % 2], ALU.max).then_inc(S("merged"), 1)
                        if k == NPW - 1:
                            e.wait_ge(S("merged"), p * 2 * NT * (NPW - 1) + (i + 1) * (NPW - 1))
                            e.tensor_tensor(m3[:, 0:PW // 2], m3[:, 0:PW // 2], m3[:, PW // 2:], ALU.max
                                            ).then_inc(S("folded"), 1)
                            e.wait_ge(S("folded"), p * 2 * NT + (i + 1))
                            e.tensor_reduce(MXP[:, i, 0:1], m3[:, 0:PW // 2], X, ALU.max).then_inc(S("tile_max"), 1)
                    if m == NX - 1:
                        e.wait_ge(S("part_out"), p * NX + NX)
                        e.wait_ge(S("tile_max"), p * 2 * NT + 2 * NT)
                        e.tensor_reduce(NEGM[:, :], MXP[:, :, 0:2], X, ALU.max, negate=True).then_inc(S("negm"), 1)
                return EXTRAS, piece

            def bit_sums():
                e.wait_ge(S("ld_bit"), 32)
                for i, nme in enumerate(BIT_N):
                    c, w_, _, _ = BIT[nme]
                    ins = e.tensor_reduce(BR[:, i:i + 1], BW[:, c:c + w_], X, ALU.add, apply_absolute_value=True)
                ins.then_inc(S("bit_rows"), 1)

            def bit_weights():
                e.wait_ge(S("bit_sum"), 1)
                for i, nme in enumerate(BIT_N):
                    ins = e.tensor_scalar(BS[:, i:i + 1], BT[:, i:i + 1], 1.0 / BIT[nme][3], 1e-5, ALU.mult, ALU.max)
                link(ins)
                link(e.tensor_scalar(BH[:, 0:7], BS[:, 0:7], 0.5, None, ALU.mult))
                link(e.tensor_scalar(BN[:, 0:7], BS[:, 0:7], -0.5, None, ALU.mult))
                for i, nme in enumerate(BIT_N):
                    c, w_, _, _ = BIT[nme]
                    ins = e.tensor_scalar(BQ[:, c:c + w_], BW[:, c:c + w_], BN[:, i:i + 1], None, ALU.is_lt)
                link(ins)
                for i, nme in enumerate(BIT_N):
                    c, w_, _, _ = BIT[nme]
                    ins = e.scalar_tensor_tensor(BQ[:, c:c + w_], BW[:, c:c + w_], BH[:, i:i + 1], BQ[:, c:c + w_],
                                                 ALU.is_gt, ALU.subtract)
                link(ins)
                for r in range(2):
                    for a in range(2):
                        ins = e.tensor_copy(BQD[:, r, a * HD:(a + 1) * HD], BQ[:, 384 + 64 * r:448 + 64 * r])
                ins.then_inc(S("bit_q"), 1)

            def scale_of(i, weights):
                e.wait_ge(S("am"), i + 1)
                link(e.tensor_scalar(AS[:, i:i + 1], AM[:, i:i + 1], 1e-8, 1.0 / 127.0, ALU.max, ALU.mult))
                link(e.reciprocal(AI[:, i:i + 1], AS[:, i:i + 1]))
                for col, nme in weights:
                    k = BIT_N.index(nme)
                    ins = e.tensor_tensor(WS[:, col:col + 1], AS[:, i:i + 1], BS[:, k:k + 1], ALU.mult)
                ins.then_inc(S("ws"), 1)

            def quantize(dst, src, tmp, i, rows=slice(0, P)):
                link(e.tensor_scalar(tmp, src, AI[rows, i:i + 1], 127.0, ALU.mult, ALU.min))
                link(e.tensor_scalar(tmp, tmp, -128.0, MAGIC, ALU.max, ALU.add))
                return e.tensor_scalar(dst, tmp, MAGIC, None, ALU.subtract)

            link(e.tensor_tensor(R[:, :, :], X_[:, :, :], over_tiles(sm("bo")), ALU.add))
            weight_lo(0, "pwq", WK2, PWQ[0:DC, 1, :])
            weight_lo(0, "pwv", WV2, PWV[0:DC, :])
            q_parts(0)
            for c in range(NKP):
                k_parts(0, c, 2 + c % 6)
            maxima(0, 2)
            e.wait_ge(S("shift_rows"), 1)

            def head(p):
                e.wait_ge(S("q_hi"), p + 1)
                e.tensor_copy(QA[0][:, :], QN[0][:, :])
                e.tensor_copy(QA[1][:, :], QN[1][:, :])
                split_lo(QB[0][0:HD, :], QS[0:HD, :], QN[0][0:HD, :])
                split_lo(QB[1][HD:P, :], QS[HD:P, :], QN[1][HD:P, :]).then_inc(S("q_split"), 1)

            def tail(p):
                e.wait_ge(S("wo_ps"), p + 1)
                e.tensor_tensor(r2, r2, bank(4, 6), ALU.add).then_inc(S("r_add"), 1)
                e.wait_ge(S("r_add"), p + 1)

            head(0)
            with e.Fori(0, PAIRS - 1) as p:
                sums(p * 2 * KT, 2, 2 * p, preparation(p))
                head(p + 1)
                tail(p)

            def chain(x):
                kind = x[0]
                rows = slice(0, DC) if kind == "ctx_max" or len(x) > 1 and x[1] == 0 and kind != "project" else slice(0, P)
                if kind == "ctx_max":
                    e.wait_ge(S("ld_ctx"), 32)
                if kind == "ctx_max" or kind == "project" and x[2]:
                    if kind == "project":
                        e.wait_ge(S("bev"), x[1] * NKC + x[2])
                    c = x[1] if kind == "ctx_max" else x[2] - 1
                    a, w = KCH[c]
                    e.tensor_reduce(AXP[rows, c:c + 1], CTX[rows, a:a + w], X, ALU.max,
                                    apply_absolute_value=True).then_inc(S("axp"), 1)
                elif kind == "max":
                    e.wait_ge(S("axp"), (x[1] + 1) * NKC)
                    e.tensor_reduce(AX[rows, x[1]:x[1] + 1], AXP[rows, :], X, ALU.max).then_inc(S("ax"), 1)
                    if x[1] == 2:
                        link(e.tensor_reduce(AVG[:, 0:1], AVP[:, :], X, ALU.add))
                        link(e.tensor_scalar(AVG[:, 1:2], AVG[:, 0:1], 1.0 / NC, None, ALU.mult))
                elif kind == "bit_sums":
                    bit_sums()
                elif kind == "bit_weights":
                    bit_weights()
                elif kind == "scale":
                    scale_of(x[1], ([(0, "d2v")], [(1, "img")], [(2, "att0"), (6, "att1")])[x[1]])
                elif kind == "round" and x[2] < NKC:
                    a, w = KCH[x[2]]
                    part = CTX[rows, a:a + w]
                    link(e.tensor_scalar(part, part, AI[rows, x[1]:x[1] + 1], 127.0, ALU.mult, ALU.min))
                    e.tensor_scalar(part, part, -128.0, MAGIC, ALU.max, ALU.add).then_inc(S("magic"), 1)

            sums((PAIRS - 1) * 2 * KT, 2, 2 * (PAIRS - 1), (CHAIN, chain))
            tail(PAIRS - 1)
            ln(2)
            def hidden(n, slot, routed):
                e.wait_ge(S("moe_silu"), n + 1)
                e.wait_ge(S("moe_up"), n + 1)
                if not isinstance(n, int) or n >= 1:
                    e.wait_ge(S("moe_h"), n)
                e.tensor_tensor(MU, bank(2, 4), MS[slot], ALU.mult).then_inc(S("moe_h1"), 1)
                e.wait_ge(S("moe_h1"), n + 1)
                if not isinstance(n, int) or n >= 2:
                    e.wait_ge(S("h_lo"), n - 1)
                if routed:
                    e.wait_ge(S("moe_rw"), n - 1)
                    ins = e.tensor_tensor(MH[slot], bank(4, 6), MU, ALU.mult)
                else:
                    ins = e.tensor_copy(MH[slot], MU)
                ins.then_inc(S("moe_h"), 1)

            def weights_lo(n, slot):
                e.wait_ge(S("w_hi"), n + 1)
                split_lo(W_LO(slot), MW_(slot), W_HI(slot)).then_inc(S("w_lo"), 1)

            def four(i):
                for j in range(4):
                    weights_lo(4 * i + (2 + j), j)
                    hidden(4 * i + (1 + j), (1 + j) % 2, not isinstance(i, int) or j > 0)

            at = [ROUT]

            def scratch(width):
                a = at[0]
                at[0] += width
                return BIG[:, a:a + width]

            sig = scratch(NT * E)
            sfc = scratch(NT * E)
            e.wait_ge(S("x_hi"), 1)
            split_lo(X_LO, XT[:, :], X_HI).then_inc(S("x_split"), 1)
            weights_lo(0, 2)
            weights_lo(1, 3)
            e.wait_ge(S("sig"), 1)
            gb = sm("gate_b").unsqueeze(1).to_broadcast([P, NT, E])
            link(e.tensor_tensor(sfc.rearrange("p (t e) -> p t e", e=E), sig.rearrange("p (t e) -> p t e", e=E),
                                 gb, ALU.add))
            hi, lo = scratch(NT * E // 2), scratch(NT * E // 2)
            v = sfc.rearrange("p (n b) -> p n b", b=2)
            link(e.tensor_tensor(hi, v[:, :, 0], v[:, :, 1], ALU.max))
            link(e.tensor_tensor(lo, v[:, :, 0], v[:, :, 1], ALU.min))
            wdt = NT * E // 2
            while wdt > NT * NG:
                wdt //= 2
                nh, nl, t1 = scratch(wdt), scratch(wdt), scratch(wdt)
                h2, l2 = (z.rearrange("p (n b) -> p n b", b=2) for z in (hi, lo))
                link(e.tensor_tensor(nh, h2[:, :, 0], h2[:, :, 1], ALU.max))
                link(e.tensor_tensor(t1, h2[:, :, 0], h2[:, :, 1], ALU.min))
                link(e.tensor_tensor(nl, l2[:, :, 0], l2[:, :, 1], ALU.max))
                link(e.tensor_tensor(nl, nl, t1, ALU.max))
                hi, lo = nh, nl
            gs = scratch(NT * NG)
            link(e.tensor_tensor(gs, hi, lo, ALU.add))
            rank = scratch(NT * NG)
            cmp = scratch(NT * NG)
            g3 = gs.rearrange("p (t g) -> p t g", g=NG)
            c3 = cmp.rearrange("p (t g) -> p t g", g=NG)
            link(e.memset(rank, 0.0))
            for o in range(NG):
                other = g3[:, :, o:o + 1].to_broadcast([P, NT, NG])
                if o < NG - 1:
                    link(e.tensor_tensor(c3[:, :, o + 1:NG], other[:, :, o + 1:NG], g3[:, :, o + 1:NG], ALU.is_ge))
                if o > 0:
                    link(e.tensor_tensor(c3[:, :, 0:o], other[:, :, 0:o], g3[:, :, 0:o], ALU.is_gt))
                link(e.memset(c3[:, :, o:o + 1], 0.0))
                link(e.tensor_tensor(rank, rank, cmp, ALU.add))
            link(e.tensor_scalar(cmp, rank, float(NG // 2), None, ALU.is_lt))
            hidden(0, 0, False)
            msk = scratch(NT * E)
            link(e.tensor_tensor(msk.rearrange("p (n e) -> p n e", e=GE), sfc.rearrange("p (n e) -> p n e", e=GE),
                                 cmp.unsqueeze(2).to_broadcast([P, NT * NG, GE]), ALU.mult))
            top = scratch(NT * 8)
            rep = scratch(NT * E)
            for t in range(NT):
                ins = e.max(top[:, 8 * t:8 * t + 8], msk[:, t * E:(t + 1) * E])
            link(ins)
            for t in range(NT):
                ins = e.match_replace(rep[:, t * E:(t + 1) * E], top[:, 8 * t:8 * t + 8],
                                      msk[:, t * E:(t + 1) * E], NEG)
            link(ins)
            tw = scratch(NT * E)
            link(e.scalar_tensor_tensor(tw, rep, NEG, sig, ALU.is_equal, ALU.mult))
            ts, tr = scratch(NT), scratch(NT)
            link(e.tensor_reduce(ts, tw.rearrange("p (t e) -> p t e", e=E), X, ALU.add))
            link(e.tensor_scalar(ts, ts, 1e-20, None, ALU.add))
            link(e.reciprocal(tr, ts))
            link(e.tensor_scalar(tr, tr, ROUTED_SCALE, None, ALU.mult))
            e.tensor_tensor(rep.rearrange("p (t e) -> p t e", e=E), tw.rearrange("p (t e) -> p t e", e=E),
                            tr.unsqueeze(2).to_broadcast([P, NT, E]), ALU.mult).then_inc(S("rw"), 1)
            RW_TM[0] = rep
            e.wait_ge(S("rw_fm"), 1)
            link(e.tensor_copy(RWT[0:E, :], RWF[0:E, :]))
            split_lo(RWT[E:P, :], RWF[0:E, :], RWT[0:E, :]).then_inc(S("rw_split"), 1)

            four(0)
            with e.Fori(1, BLK // 4) as i:
                four(i)
            hidden(BLK + 1, 1, True)
            e.wait_ge(S("moe_tm"), 1)
            link(e.tensor_tensor(r2, bank(0, 2), x2, ALU.add))
            ln(3)
            def kv(r):
                def piece(x):
                    if x[0] == "keys":
                        a, w = KCH[x[1]]
                        e.wait_ge(S("kv_hi"), r * NKC + x[1] + 1)
                        e.tensor_copy(KB[r][0:HD, a:a + w], KA[r][0:HD, a:a + w])
                        split_lo(KA[r][HD:P, a:a + w], CTX[HD:P, a:a + w],
                                 KA[r][HD:P, a:a + w]).then_inc(S("kv_lo"), 1)
                    else:
                        i = x[1]
                        full = min(16, KT - 1 - 16 * i)
                        brow = sm(f"b_att{r}_row")
                        e.wait_ge(S("vt_ev"), r * NVT + i + 1)
                        part = V2[r][:, 16 * i:16 * i + full, :]
                        ins = e.tensor_tensor(part, part, brow.unsqueeze(1).to_broadcast([P, full, HD]), ALU.add)
                        if full < 16:
                            part = V2[r][0:TAIL, KT - 1, :]
                            ins = e.tensor_tensor(part, part, brow[0:TAIL, :], ALU.add)
                        ins.then_inc(S("v2"), 1)
                return piece

            e.wait_ge(S("swap"), 1)
            g = sm("rot").rearrange("p (a b) -> p a b", b=2)
            link(e.tensor_tensor(GQ, g, g, ALU.mult))
            e.tensor_reduce(GN, GQ, X, ALU.add).then_inc(S("rot_n"), 1)
            e.wait_ge(S("rot_sd"), 1)
            link(e.reciprocal(GR, GD))
            link(e.tensor_tensor(G3, g, GR.unsqueeze(2).to_broadcast([P, 3, 2]), ALU.mult))
            for a in range(3):
                link(e.tensor_scalar(ROT[:, a, :], ident[:, :], G3[:, a, 0:1], None, ALU.mult))
                link(e.scalar_tensor_tensor(ROT[:, a, :], SWAP, G3[:, a, 1:2], ROT[:, a, :], ALU.mult, ALU.add))
            sbv = sm("sb")
            link(e.reciprocal(HS[:, 1:2], sbv[:, 0:1]))
            link(e.tensor_scalar(HS[:, 0:1], HS[:, 1:2], 2.0, None, ALU.mult))
            e.tensor_tensor(HS[:, 2:3], HS[:, 0:1], sbv[:, 1:2], ALU.add).then_inc(S("rot"), 1)
            e.wait_ge(S("rot"), 1)
            for t in range(NT):
                b = 2 * (t % 2)
                e.wait_ge(S("h_s"), t + 1)
                link(e.tensor_reduce(HM[:, t:t + 1], bank(b, b + 2), X, ALU.max))
                link(e.tensor_scalar(HM[:, t:t + 1], HM[:, t:t + 1], HS[:, 2:3], -1.0, ALU.add, ALU.mult))
                e.tensor_scalar(HNM[:, t:t + 1], HM[:, t:t + 1], HS[:, 2:3], None,
                                ALU.add).then_inc(S("h_max"), 1)
                if t:
                    beside((NEXT_KV, kv(0)), t - 1, NT)
            beside((NEXT_KV, kv(0)), NT - 1, NT)
            e.wait_ge(S("h_av"), NT)
            e.wait_ge(S("h_exp"), NT)
            link(e.reciprocal(HLR, HL))
            e.tensor_tensor(HO, bank(6, 8).rearrange("p (t d) -> p t d", d=D),
                            HLR.unsqueeze(2).to_broadcast([P, NT, D]), ALU.mult).then_inc(S("h_o"), 1)
            e.wait_ge(S("h_inner"), 1)
            e.tensor_scalar(HC, HI, 1e-8, None, ALU.max).then_inc(S("h_clip"), 1)
            e.wait_ge(S("h_sd"), 1)
            link(e.reciprocal(HIR, HID))
            link(e.tensor_tensor(HO, HO, HIR.unsqueeze(2).to_broadcast([P, NT, D]), ALU.mult))
            link(e.tensor_tensor(R[:, :, :], HO, X_[:, :, :], ALU.add))
            ln(4)
            e.wait_ge(S("bit_rows1"), 1)
            e.tensor_reduce(AX[:, 3:4], x2, X, ALU.max, apply_absolute_value=True).then_inc(S("ax"), 1)
            scale_of(3, [(3, "txt")])
            e.wait_ge(S("x4_t"), 1)
            quantize(XQ, bank(0, 2), XF, 3).then_inc(S("quant"), 1)

            for r in range(2):
                e.wait_ge(S("f2"), r + 1)
                link(e.tensor_copy(QA[0][:, :], QS[:, :]))
                split_lo(QB[0][0:HD, :], QS[0:HD, :], QA[0][0:HD, :]).then_inc(S("q_split"), 1)
                maxima(2 + r, 1)
                sums(PAIRS * 2 * KT + r * KT, 1, 2 * PAIRS + r, None if r else (NEXT_KV, kv(1)))
                e.wait_ge(S("on"), 2 * PAIRS + r + 1)
                for qh in range(2):
                    for fh in range(2):
                        ins = e.tensor_copy(OO[fh * HD:(fh + 1) * HD, qh * HALF:(qh + 1) * HALF],
                                            ON[qh * HD:(qh + 1) * HD, 0:HALF])
                link(ins)
                link(e.scalar_tensor_tensor(XT[:, :], OO, 0.1, XT[:, :], ALU.mult, ALU.add))
                e.sem_inc(S("fused_upd"), 1)
            link(e.tensor_reduce(AVG[:, 2:3], XT[:, :], X, ALU.max, apply_absolute_value=True))
            link(e.tensor_reduce(AVG[:, 3:4], AVG[:, 1:2], X, ALU.max, apply_absolute_value=True))
            e.tensor_tensor(AX[:, 4:5], AVG[:, 2:3], AVG[:, 3:4], ALU.max).then_inc(S("ax"), 1)
            scale_of(4, [(4, "f1")])
            link(quantize(FQ, XT[:, :], XF, 4))
            link(quantize(AVG[:, 2:3], AVG[:, 1:2], AVG[:, 0:1], 4))
            e.tensor_copy(AQ, AVG[:, 2:3].to_broadcast([P, HALF])).then_inc(S("quant"), 1)
            for b in range(4):
                e.wait_ge(S("hb"), b + 1)
                ins = e.tensor_reduce(AXP[:, b:b + 1], HB[b], X, ALU.max)
            link(ins)
            e.tensor_reduce(AX[:, 5:6], AXP[:, 0:4], X, ALU.max).then_inc(S("ax"), 1)
            scale_of(5, [(5, "f2")])
            for b in range(4):
                link(e.tensor_scalar(HB[b], HB[b], AI[:, 5:6], 127.0, ALU.mult, ALU.min))
                e.tensor_scalar(HB[b], HB[b], -128.0, MAGIC, ALU.max, ALU.add).then_inc(S("h_magic"), 1)
            e.wait_ge(S("f2o"), 1)
            link(e.tensor_tensor(R[:, :, :], QS[:, :].rearrange("p (t d) -> p t d", d=D),
                                 over_tiles(sm("b_f2")), ALU.add))
            link(e.tensor_tensor(r2, r2, x2, ALU.add))
            ln(5)
            e.wait_ge(S("gl_ps"), 1)
            link(e.tensor_copy(GL0, PS[0:1, 7, RE:2 * RE]))
            rank, cmp = GT[:, 0:RE], GT[:, RE:2 * RE]
            link(e.memset(rank, 0.0))
            for o in range(RE):
                other = GL0[:, o:o + 1]
                if o < RE - 1:
                    link(e.tensor_scalar(cmp[:, o + 1:RE], GL0[:, o + 1:RE], other, None, ALU.is_le))
                if o > 0:
                    link(e.tensor_scalar(cmp[:, 0:o], GL0[:, 0:o], other, None, ALU.is_lt))
                link(e.memset(cmp[:, o:o + 1], 0.0))
                link(e.tensor_tensor(rank, rank, cmp, ALU.add))
            link(e.tensor_scalar(cmp, rank, 2.0, None, ALU.is_lt))
            e.tensor_reduce(GNM, GL0, X, ALU.max, negate=True).then_inc(S("g_max"), 1)
            e.wait_ge(S("g_exp"), 1)
            gm, gsum, grec, gate = GT[:, 16:24], GT[:, 24:25], GT[:, 25:26], GT[:, 32:40]
            link(e.tensor_tensor(gm, GE_, cmp, ALU.mult))
            link(e.tensor_reduce(gsum, gm, X, ALU.add))
            link(e.reciprocal(grec, gsum))
            link(e.tensor_scalar(gate, gm, grec, None, ALU.mult))
            e.tensor_copy(GX.rearrange("p (e r) -> p e r", r=RR),
                          gate.unsqueeze(2).to_broadcast([1, RE, RR])).then_inc(S("g_row"), 1)
            e.wait_ge(S("gc_ps"), 1)
            e.tensor_copy(GC[:, :], PS[:, 7, 0:4]).then_inc(S("g_col"), 1)
            e.wait_ge(S("lr_ps"), 1)
            link(e.scalar_tensor_tensor(r2, x2, 2.0, bank(6, 8), ALU.mult, ALU.add))
            ln(6)

        @block.tensor
        def _(e):
            def transposes(src, a):
                for t in range(NT):
                    ins = e.transpose(PS[:, a + t // 4, (t % 4) * P:(t % 4 + 1) * P], src[:, t, :], ident[:, :])
                return ins

            def to_fm(k, a, lns):
                e.wait_ge(S("ln_x"), lns)
                transposes(X_, a).then_inc(S("xt_ps"), 1)

            e.wait_ge(S("ld_small"), 16)
            e.wait_ge(S("ld_x"), 32)
            for t in range(NT):
                e.matmul(PS[:, t, 0:3 * D], XT[:, t * P:(t + 1) * P], sm("w_qkv"), start=True,
                         stop=True).then_inc(S("qkv"), 1)
            e.wait_ge(S("qk0"), 1)
            e.wait_ge(S("v0"), NT)
            e.wait_ge(S("consts"), 1)
            for t in range(NT):
                ins = e.matmul(PS[:, 0, 0:D + 1], QK0[:, t, 1, :], VA[:, t, :], start=(t == 0), stop=(t == NT - 1))
            ins.then_inc(S("kv0"), 1)
            for t in range(NT):
                ins = e.transpose(PS[:, 1 + t // 4, (t % 4) * P:(t % 4 + 1) * P], QK0[:, t, 0, :], ident[:, :])
            ins.then_inc(S("q0_t"), 1)
            e.wait_ge(S("kvb"), 1)
            e.wait_ge(S("q0_fm"), 1)
            for a in range(2):
                for h in range(2):
                    ins = e.matmul(bank(3 + 2 * a + h), KVB[:, a * D:(a + 1) * D], QS[:, h * HALF:(h + 1) * HALF],
                                   start=True, stop=True)
            ins.then_inc(S("o0"), 1)
            e.wait_ge(S("on0"), 1)
            for t in range(NT):
                ins = e.matmul(PS[:, 1 + t // 4, (t % 4) * P:(t % 4 + 1) * P], ON[:, t * P:(t + 1) * P], sm("w_out"),
                               start=True, stop=True)
            ins.then_inc(S("wo0"), 1)
            to_fm(1, 0, 1)

            def part_scores(part, q, kn, b):
                kind, t, k = part
                for i in range(2):
                    if kind == "full":
                        tile, a, w = t, k * KW + i * HALF, HALF
                    else:
                        tile, a, w = t + i, FULLS * KW, NC - FULLS * KW
                    ins = e.matmul(PS[:, b + i, 0:w], q[:, tile * P:(tile + 1) * P], kn[:, a:a + w],
                                   start=True, stop=True)
                return ins

            def max_scores(first, heads, qn, kn):
                for h in range(heads):
                    for i, part in enumerate(PARTS1):
                        m = (first + h) * len(PARTS1) + i
                        if m >= 4:
                            engine = ENGINE1[(m - 4) % len(PARTS1)]
                            e.wait_ge(S("alone_" + engine), parts_on(engine, m - 3))
                        part_scores(part, qn[h], kn[h], 2 * (m % 4)).then_inc(S("alone_ps"), 1)

            def shift_row(h, r, b):
                for t in range(NT):
                    ins = e.matmul(PS[r:r + 1, b + t // 4, (t % 4) * P:(t % 4 + 1) * P],
                                   NEGM[:, h * NT + t:h * NT + t + 1], ident16[:, :], start=True, stop=True)
                return ins

            def attend(base, units, operands, obase, extra=None, bank5_free=None):
                def scores(g):
                    u, j = divmod(g, KT)
                    r = rows_of(j)
                    if g >= 2:
                        e.wait_ge(S("exp"), base + g - 1)
                    for side in range(2):
                        ka, kb, qa, qb, _ = operands(u, side)
                        o = PS[0:r, 2 * (g % 2) + side, :]
                        e.matmul(o, ka[:, j * P:j * P + r], qa, start=True, stop=False)
                        ins = e.matmul(o, kb[:, j * P:j * P + r], qb, start=False, stop=True)
                    ins.then_inc(S("scores"), 1)

                def values(g):
                    u, j = divmod(g, KT)
                    r = rows_of(j)
                    e.wait_ge(S("exp"), base + g + 1)
                    if u and j == 0:
                        e.wait_ge(S("o_ev"), obase + u)
                    for side in range(2):
                        v = operands(u, side)[4]
                        ins = e.matmul(PS[side * HD:(side + 1) * HD, 4, :], v(r, j),
                                       PR[0:r, g % 3, side * HALF:(side + 1) * HALF], start=(j == 0),
                                       stop=(j == KT - 1), skip_group_check=True)
                    ins.then_inc(S("pv"), 1)

                def denominators(u):
                    if bank5_free is not None:
                        bank5_free(u)
                    e.wait_ge(S("acc"), base + KT * (u + 1))
                    if u:
                        e.wait_ge(S("on"), obase + u)
                    for side in range(2):
                        ins = e.matmul(PS[side * HD:(side + 1) * HD, 5, :], ones[:, 0:HD],
                                       ACC[:, u, side * HALF:(side + 1) * HALF], start=True, stop=True)
                    ins.then_inc(S("den_ps"), 1)

                for g in range(units * KT):
                    scores(g)
                    if g:
                        values(g - 1)
                    if g == KT + 2:
                        denominators(0)
                    beside(extra, g, units * KT)
                values(units * KT - 1)
                denominators(units - 1)

            def project_q(p, b):
                e.wait_ge(S("ld_pwq"), p * 16 + 16)
                for h in range(2):
                    ins = e.matmul(bank(b + h), PWQ[:, 0, :], XT[:, h * HALF:(h + 1) * HALF], start=True, stop=True)
                ins.then_inc(S("q_ps"), 1)

            def project_k(p, c, b):
                a, w = KP[c]
                for i, (w_, c_) in enumerate(((1, C_HI), (0, C_LO), (0, C_HI))):
                    ins = e.matmul(PS[:, b, 0:w], WK2[0:DC, w_, :], c_[0:DC, a:a + w], start=(i == 0), stop=(i == 2))
                ins.then_inc(S("k_ps"), 1)

            def preparation(p):
                def piece(x):
                    if x[0] in ("none", "wk", "wv"):
                        return
                    if x[0] == "q":
                        return project_q(p + 1, 6)
                    if x[0] == "k":
                        c = x[1]
                        if c >= 2:
                            e.wait_ge(S("k_lo"), p * NKP + (NKP + c - 1))
                        else:
                            e.wait_ge(S("q_ev"), p + 2)
                            e.wait_ge(S("pwq_lo"), p + 2)
                        return project_k(p + 1, c, 6 + c % 2)
                    m = x[1]
                    kind, h, t, k = PARTS[m]
                    if m:
                        e.wait_ge(S("part_out"), p * NX + m)
                    else:
                        e.wait_ge(S("k_lo"), p * NKP + 2 * NKP)
                        e.wait_ge(S("q_hi"), p + 2)
                    if m == DEN_PARTS:
                        e.wait_ge(S("on"), 2 * p + 1)
                    for i in range(3 if kind == "full" else k):
                        tile, a, w = (t, k * PW + i * HALF, HALF) if kind == "full" else (t + i, NPW * PW, RESTW)
                        ins = e.matmul(PS[:, 5 + i, 0:w], QN[h][:, tile * P:(tile + 1) * P], KN[h][:, a:a + w],
                                       start=True, stop=True)
                    ins.then_inc(S("part_ps"), 1)
                return EXTRAS, piece

            e.wait_ge(S("x_fm"), 1)
            e.wait_ge(S("c_lo"), 1)
            e.wait_ge(S("pwq_lo"), 1)
            project_q(0, 0)
            for c in range(NKP):
                if c >= 6:
                    e.wait_ge(S("k_lo"), c - 5)
                project_k(0, c, 2 + c % 6)
            e.wait_ge(S("k_lo"), NKP)
            e.wait_ge(S("q_ev"), 1)
            e.wait_ge(S("q_hi"), 1)
            max_scores(0, 2, QN, KN)

            def head(p):
                e.wait_ge(S("negm"), p + 1)
                shift_row(0, HD, 6)
                shift_row(1, 0, 6).then_inc(S("shift_ps"), 1)
                e.wait_ge(S("pwv_lo"), p + 1)
                for g in range(NVG):
                    if g >= 4:
                        e.wait_ge(S("v_ev"), p * NVG + (g - 3))
                    for i, j in enumerate(VG[g]):
                        r = rows_of(j)
                        for k, (c_, w_) in enumerate(((C_LO, 0), (C_HI, 1), (C_HI, 0))):
                            ins = e.matmul(PS[0:r, g % 4, i * P:(i + 1) * P], c_[0:DC, j * P:j * P + r],
                                           WV2[0:DC, w_, :], start=(k == 0), stop=(k == 2))
                    ins.then_inc(S("v_ps"), 1)

            def main(p, extra, before=None):
                e.wait_ge(S("v_ev"), p * NVG + NVG)
                e.wait_ge(S("q_split"), p + 1)
                e.wait_ge(S("shift"), p + 1)
                e.wait_ge(S("keys"), p * 256 + 256)
                e.wait_ge(S("shift_rows"), 1)

                def operands(u, side):
                    q = slice(u * HALF, (u + 1) * HALF)
                    return (KA[side], KB[side], QA[side][:, q], QB[side][:, q],
                            lambda r, j: V[0:r, j, side * HD:(side + 1) * HD])

                def bank5_free(u):
                    e.wait_ge(S("part_out"), p * NX + (NX if u else DEN_PARTS))

                attend(p * 2 * KT, 2, operands, 2 * p, extra, None if isinstance(p, int) else bank5_free)

            def tail(p):
                e.wait_ge(S("on"), 2 * p + 2)
                e.wait_ge(S("ld_pwo"), p * 16 + 16)
                for t in range(NT):
                    ins = e.matmul(PS[:, 4 + t // 4, (t % 4) * P:(t % 4 + 1) * P], ON[:, t * P:(t + 1) * P],
                                   PWO[:, :], start=True, stop=True)
                ins.then_inc(S("wo_ps"), 1)
                e.wait_ge(S("r_add"), p + 1)

            head(0)
            with e.Fori(0, PAIRS - 1) as p:
                main(p, preparation(p))
                head(p + 1)
                tail(p)

            def chain(x):
                if x[0] != "project" or x[2] == NKC:
                    return
                lay, c = x[1], x[2]
                a, w = KCH[c]
                if c == 0:
                    e.wait_ge(S("bit_q"), 1)
                    e.wait_ge(S("emb"), (lay + 1) * NKC)
                if lay or c:
                    e.wait_ge(S("bev"), lay * NKC + c)
                rows = slice(0, P) if lay else slice(0, DC)
                for i in range(-(-w // HALF)):
                    cw = min(HALF, w - i * HALF)
                    ins = e.matmul(PS[:, 6 + i, 0:cw], BQ[rows, lay * P:(lay + 1) * P],
                                   EMB[lay][rows, a + i * HALF:a + i * HALF + cw], start=True, stop=True)
                ins.then_inc(S("bp"), 1)

            main(PAIRS - 1, (CHAIN, chain))
            tail(PAIRS - 1)
            to_fm(2, 0, 2)
            e.wait_ge(S("x_fm"), 2)
            for t in range(NT):
                ins = e.matmul(PS[:, 4, t * E:(t + 1) * E], XT[:, t * P:(t + 1) * P], sm("gate_w"),
                               start=True, stop=True)
            ins.then_inc(S("logits"), 1)
            e.wait_ge(S("x_split"), 1)

            def split_product(b, slot, part, hi, lo, start=True, stop=True):
                passes = ((W_LO(slot), hi), (W_HI(slot), lo), (W_HI(slot), hi))
                for h in range(2):
                    for i, (w_, rows) in enumerate(passes):
                        ins = e.matmul(bank(b + h), w_[:, part, :], rows[:, h * HALF:(h + 1) * HALF],
                                       start=start and i == 0, stop=stop and i == 2, skip_group_check=True)
                return ins

            def expert(n, slot, block_at):
                e.wait_ge(S("w_lo"), n + 1)
                if not isinstance(n, int) or n >= 1:
                    e.wait_ge(S("moe_silu"), n)
                split_product(0, slot, 0, X_HI, X_LO).then_inc(S("moe_gate"), 1)
                if not isinstance(n, int) or n >= 1:
                    e.wait_ge(S("moe_h1"), n)
                split_product(2, slot, 1, X_HI, X_LO).then_inc(S("moe_up"), 1)
                if block_at is not None:
                    e.wait_ge(S("moe_h"), n)
                    for h in range(2):
                        ins = e.matmul(bank(4 + h), SEL[:, bass.ds(block_at, P)],
                                       RWT[:, h * HALF:(h + 1) * HALF], start=True, stop=True)
                    ins.then_inc(S("moe_rw"), 1)

            def down(n, slot, hslot, first=False, stop=False):
                e.wait_ge(S("h_lo"), n + 1)
                split_product(6, slot, 2, H_HI[hslot], H_LO[hslot], first, stop).then_inc(S("moe_down"), 1)

            def four(i):
                for j in range(4):
                    expert(4 * i + (2 + j), j, 4 * P * i + j * P)
                    down(4 * i + j, (j + 2) % 4, j, first=isinstance(i, int) and j == 0)

            expert(0, 2, None)
            expert(1, 3, None)
            e.wait_ge(S("rw"), 1)
            for t in range(NT):
                ins = e.transpose(PS[0:E, 4 + t // 4, (t % 4) * P:(t % 4 + 1) * P],
                                  RW_TM[0][:, t * E:(t + 1) * E], ident[:, :])
            ins.then_inc(S("rw_t"), 1)
            e.wait_ge(S("rw_split"), 1)
            e.wait_ge(S("selector"), 1)
            four(0)
            with e.Fori(1, BLK // 4) as i:
                four(i)
            down(BLK, 2, 0)
            down(BLK + 1, 3, 1, stop=True)
            e.wait_ge(S("moe_fm"), 1)
            for t in range(NT):
                ins = e.transpose(PS[:, t // 4, (t % 4) * P:(t % 4 + 1) * P], QS[:, t * P:(t + 1) * P], ident[:, :])
            ins.then_inc(S("moe_tm"), 1)
            to_fm(3, 0, 3)
            def kv(r, b):
                def piece(x):
                    i = x[1] + (NKC if x[0] == "values" else 0)
                    back = i - 1
                    if back >= NKC:
                        e.wait_ge(S("vt_ev"), r * NVT + back - NKC + 1)
                    elif back >= 0:
                        e.wait_ge(S("kv_ev"), r * NKC + back + 1)
                    if x[0] == "keys":
                        a, w = KCH[x[1]]
                        for h in range(-(-w // HALF)):
                            c = min(HALF, w - h * HALF)
                            ins = e.matmul(PS[:, b + h, 0:c], BQD[:, r, :], IQ[:, a + h * HALF:a + h * HALF + c],
                                           start=True, stop=True)
                        ins.then_inc(S("kv_ps"), 1)
                    else:
                        for j in range(16 * x[1], min(16 * x[1] + 16, KT)):
                            rr = rows_of(j)
                            ins = e.matmul(PS[0:rr, b + j % 16 // 8, (j % 8) * HD:(j % 8 + 1) * HD],
                                           IQ[:, j * P:j * P + rr], BQ[:, 384 + 64 * r:448 + 64 * r],
                                           start=True, stop=True)
                        ins.then_inc(S("vt_ps"), 1)
                return piece

            e.wait_ge(S("x_fm"), 3)
            e.wait_ge(S("rot"), 1)
            for a in range(2):
                for h in range(2):
                    e.matmul(bank(2 * a + h), ROT[:, a, :], XT[:, h * HALF:(h + 1) * HALF], start=True, stop=True)
            for t in range(NT):
                ins = e.matmul(PS[:, 4 + t // 4, (t % 4) * P:(t % 4 + 1) * P], XT[:, t * P:(t + 1) * P],
                               ROT[:, 2, :], start=True, stop=True)
            ins.then_inc(S("hq"), 1)
            e.wait_ge(S("hqkv"), 1)

            def h_scores(t):
                b = 2 * (t % 2)
                if t >= 2:
                    e.wait_ge(S("h_exp"), t - 1)
                for h in range(2):
                    ins = e.matmul(bank(b + h), HQ[:, t * P:(t + 1) * P], HK[:, h * HALF:(h + 1) * HALF],
                                   start=True, stop=True)
                ins.then_inc(S("h_s"), 1)

            e.wait_ge(S("emb"), 3 * NKC)
            h_scores(0)
            for t in range(NT):
                if t + 1 < NT:
                    h_scores(t + 1)
                e.wait_ge(S("h_exp"), t + 1)
                if t:
                    e.wait_ge(S("h_ptc"), t)
                    done = NEXT_KV[:t * len(NEXT_KV) // NT]
                    e.wait_ge(*((S("kv_ev"), len(done)) if done[-1][0] == "keys" else (S("vt_ev"), done[-1][1] + 1)))
                for j in range(NT):
                    ins = e.transpose(PS[:, 4 + j // 4, (j % 4) * P:(j % 4 + 1) * P], HP[t % 2][:, j * P:(j + 1) * P],
                                      ident[:, :])
                ins.then_inc(S("h_pt"), 1)
                e.wait_ge(S("h_ptc"), t + 1)
                for j in range(NT):
                    ins = e.matmul(PS[:, 6 + t // 4, (t % 4) * P:(t % 4 + 1) * P], HPT[t % 2][:, j, :], HV[:, j, :],
                                   start=(j == 0), stop=(j == NT - 1))
                ins.then_inc(S("h_av"), 1)
                beside((NEXT_KV, kv(0, 4)), t, NT)
            e.wait_ge(S("ln_x"), 4)
            transposes(X_, 0).then_inc(S("x4_t"), 1)
            e.wait_ge(S("quant"), 1)
            for h in range(2):
                ins = e.matmul(bank(h), BQ[:, 256:384], XQ[:, h * HALF:(h + 1) * HALF], start=True, stop=True)
            ins.then_inc(S("f_int"), 1)
            e.wait_ge(S("fused"), 1)
            e.wait_ge(S("bit_rows1"), 1)
            for r in range(2):
                if r:
                    e.wait_ge(S("fused_upd"), 1)
                for h in range(2):
                    ins = e.matmul(bank(h), DUP, XT[:, h * HALF:(h + 1) * HALF], start=True, stop=True)
                ins.then_inc(S("f2_ps"), 1)
                e.wait_ge(S("kv_lo"), (r + 1) * NKC)
                e.wait_ge(S("v2"), (r + 1) * NVT)
                e.wait_ge(S("q_split"), PAIRS + r + 1)
                max_scores(2 + r, 1, QA, [KA[r]])
                e.wait_ge(S("negm"), PAIRS + r + 1)
                shift_row(0, HD, 0).then_inc(S("shift_ps"), 1)
                e.wait_ge(S("shift"), PAIRS + r + 1)

                def operands(u, side):
                    q = slice(side * HALF, (side + 1) * HALF)
                    return KA[r], KB[r], QA[0][:, q], QB[0][:, q], lambda r_, j: V2[r][0:r_, j, :]
                attend(PAIRS * 2 * KT + r * KT, 1, operands, 2 * PAIRS + r,
                       None if r else (NEXT_KV, kv(1, 6)))
            e.wait_ge(S("quant"), 2)
            e.wait_ge(S("on"), 2 * PAIRS + 2)
            for b in range(4):
                for h in range(2):
                    e.matmul(bank(2 * b + h), BQ[:, 512 + b * P:512 + (b + 1) * P],
                             FQ[:, h * HALF:(h + 1) * HALF], start=True, stop=False)
                    ins = e.matmul(bank(2 * b + h), BQ[:, 512 + FFN + b * P:512 + FFN + (b + 1) * P], AQ,
                                   start=False, stop=True)
                ins.then_inc(S("h1_ps"), 1)
            e.wait_ge(S("hb"), 1)
            for t in range(NT):
                for b in range(4):
                    if t == 0:
                        e.wait_ge(S("h_int"), b + 1)
                    ins = e.matmul(PS[:, t // 4, (t % 4) * P:(t % 4 + 1) * P], HBQ[b][:, t * P:(t + 1) * P],
                                   BQ[:, 1536 + b * P:1536 + (b + 1) * P], start=(b == 0), stop=(b == 3))
            ins.then_inc(S("f2o_ps"), 1)
            to_fm(4, 0, 5)
            e.wait_ge(S("x_fm"), 4)
            e.wait_ge(S("ld_lr"), 32)
            e.matmul(PS[0:1, 7, RE:2 * RE], XT[:, 0:1], sm("w_r"), start=True, stop=True).then_inc(S("gl_ps"), 1)

            def mid(b):
                a = 2 * (b % 3)
                for h in range(2):
                    ins = e.matmul(bank(a + h), LA[:, b * P:(b + 1) * P], XT[:, h * HALF:(h + 1) * HALF],
                                   start=True, stop=True)
                ins.then_inc(S("mid_ps"), 1)

            for b in range(3):
                mid(b)
            e.wait_ge(S("g_row"), 1)
            for b in range(4):
                ins = e.matmul(PS[:, 7, b:b + 1], GX[:, b * P:(b + 1) * P], ones[0:1, 0:1], start=True, stop=True)
            ins.then_inc(S("gc_ps"), 1)
            e.wait_ge(S("mid"), 1)
            mid(3)
            e.wait_ge(S("g_col"), 1)
            e.wait_ge(S("mid"), 4)
            for t in range(NT):
                for b in range(4):
                    ins = e.matmul(PS[:, 6 + t // 4, (t % 4) * P:(t % 4 + 1) * P], MID[b][:, t * P:(t + 1) * P],
                                   LB[:, b, :], start=(b == 0), stop=(b == 3))
            ins.then_inc(S("lr_ps"), 1)


def kernel(**inputs):
    import numpy as np
    import concourse.bacc as bacc
    from concourse.bass_utils import run_bass_kernel_spmd

    v = {k: np.asarray(a) for k, a in inputs.items()}

    def rows(a):
        a = a.reshape(1, -1)
        return np.broadcast_to(a, (P, a.shape[1]))

    def col(a):
        return a.reshape(-1, P).T

    x = v["x"][0]
    ctx = v["ctx_768"][0]
    parts = {
        "qk_w": rows(np.concatenate([v["L0_attn_qn_w"], v["L0_attn_kn_w"]])),
        "b_out": rows(v["L0_attn_b_out"]), "bo": rows(v["L0_xattn_bo"]),
        "gate_w": v["L0_ffn_gate_w"].T, "gate_b": rows(v["L0_ffn_gate_bias"]),
        "rot": np.repeat(v["L1_attn_rot_w"].reshape(3, D // 2, 2).transpose(1, 0, 2).reshape(D // 2, 6), 2, axis=0),
        "sb": rows(np.concatenate([v["L1_attn_scale"].reshape(1), v["L1_attn_bias"].reshape(1)])),
        "b_d2v": col(v["L1_xattn_b_d2v"]), "b_img": col(v["L1_xattn_b_img"]), "b_txt": col(v["L1_xattn_b_txt"]),
        "b_att0": col(np.tile(v["L1_xattn_b_att0"], 2)), "b_att1": col(np.tile(v["L1_xattn_b_att1"], 2)),
        "b_f1": col(v["L1_xattn_b_f1"]), "b_f2": rows(v["L1_xattn_b_f2"]),
        "b_att0_row": rows(v["L1_xattn_b_att0"]), "b_att1_row": rows(v["L1_xattn_b_att1"]),
        "w_r": v["L1_ffn_Wr"].T, "w_out": v["L0_attn_W_out"], "w_qkv": v["L0_attn_W_qkv"],
    }
    small = np.concatenate([parts[n] for n in SMALL], axis=1)
    pair_w = np.zeros((PAIRS, P, 4, P), np.float32)
    for i, n in enumerate(("Wq", "Wk", "Wv")):
        w = v["L0_xattn_" + n]
        pair_w[:, :w.shape[0], i, :] = w.reshape(w.shape[0], PAIRS, P).transpose(1, 0, 2)
    pair_w[:, :, 3, :] = v["L0_xattn_Wo"].reshape(PAIRS, P, D)
    moe_w = np.stack([v["L0_ffn_Wg"].reshape(BLK, P, D).transpose(0, 2, 1),
                      v["L0_ffn_Wu"].reshape(BLK, P, D).transpose(0, 2, 1),
                      v["L0_ffn_Wd"].transpose(0, 2, 1).reshape(BLK, P, D)], axis=2)
    sh_gu = np.stack([v["L0_ffn_Sg"].reshape(2, EI, D).transpose(0, 2, 1),
                      v["L0_ffn_Su"].reshape(2, EI, D).transpose(0, 2, 1)], axis=2)
    sh_d = v["L0_ffn_Sd"].T.reshape(2, EI, D)
    bit_w = np.zeros((P, NBIT), np.float32)
    for n in ("d2v", "img", "txt", "att0", "att1"):
        w = v["L1_xattn_W_" + n].T
        bit_w[:w.shape[0], BIT[n][0]:BIT[n][0] + w.shape[1]] = w
    for n in ("f1", "f2"):
        w = v["L1_xattn_W_" + n].T
        bit_w[:, BIT[n][0]:BIT[n][0] + BIT[n][1]] = w.reshape(-1, P, w.shape[1]).transpose(1, 0, 2).reshape(P, -1)
    named = {
        "x_tm": x, "x_fm": x.T, "ctx_fm": ctx.T, "small": small, "pair_w": pair_w, "moe_w": moe_w, "sh_gu": sh_gu,
        "sh_d": sh_d, "bit_w": bit_w, "lr_a": v["L1_ffn_A"].reshape(RE * RR, D).T,
        "lr_b": v["L1_ffn_Bw"].transpose(0, 2, 1).reshape(RE * RR, D),
    }
    nc = bacc.Bacc("TRN2", target_bir_lowering=False, num_devices=1)
    arrays, args = {}, {}
    for n, a in named.items():
        a = np.ascontiguousarray(a)
        arrays[f"in_{n}_dram"] = a
        args[n] = nc.dram_tensor(f"in_{n}_dram", a.shape, mybir.dt.from_np(a.dtype), kind="ExternalInput").ap()
    args["out"] = nc.dram_tensor("out_0_dram", (1, T, D), F32, kind="ExternalOutput").ap()
    build_decoder(nc, **args)
    r = run_bass_kernel_spmd(nc, [arrays], core_ids=[0])
    return r.results[0]["out_0_dram"]
```
